# Optimizing a Trainium2 kernel written in Bass

```python
import numpy as np
import jax
import jax.numpy as jnp

def _softmax(x, axis=-1):
    return jax.nn.softmax(x, axis=axis)

def _gelu(x):
    return jax.nn.gelu(x, approximate=True)

def _silu(x):
    return jax.nn.silu(x)

def _sigmoid(x):
    return jax.nn.sigmoid(x)

def _layernorm(x, axis=-1, eps=1e-05):
    m = jnp.mean(x, axis=axis, keepdims=True)
    v = jnp.var(x, axis=axis, keepdims=True)
    return (x - m) / jnp.sqrt(v + eps)

def _scatter_add(tgt, idx, src, axis=0):
    return tgt.at[idx].add(src)

def _segment_sum(src, seg, n):
    return jax.ops.segment_sum(src, seg, n)
kernel_name = 'mk_xattn_ffn_d2_seqx_r8_0024cc'

def setup_inputs(seed: int=0):
    np.random.seed(seed)
    _w = jnp.asarray

    def _rec_inputs():
        import jax
        import jax.numpy as jnp
        _rk = jax.random.key(seed)
        x = 7.22e-05 + 1 * jax.random.normal(jax.random.fold_in(_rk, 1), (2, 512, 128), jnp.float32)
        _lenS = 512 - jax.random.randint(jax.random.fold_in(_rk, 7), (2,), 0, max(1, 512 // 4) + 1, jnp.int32)
        _lenS2 = 154 - jax.random.randint(jax.random.fold_in(_rk, 8), (2,), 0, max(1, 154 // 4) + 1, jnp.int32)
        _ctx_768P = jax.random.normal(jax.random.fold_in(_rk, 11), (2, 16, 96), jnp.float32)
        _ctx_768c = jax.random.dirichlet(jax.random.fold_in(_rk, 511), 0.3 * jnp.ones((16,), jnp.float32), (2, 154))
        _ctx_768t = jnp.einsum('bsk,bkd->bsd', _ctx_768c, _ctx_768P)
        _ctx_768t = _ctx_768t * jax.lax.rsqrt(jnp.mean(jnp.square(_ctx_768t)) + 1e-12) * 0.953939
        ctx_768 = -0.000191848 + 0.999787 * (_ctx_768t + 0.3 * jax.random.normal(jax.random.fold_in(_rk, 611), (2, 154, 96), jnp.float32))
        return (x, ctx_768)
    x, ctx_768 = _rec_inputs()

    def _L0_xattn_setup():
        import jax, jax.numpy as jnp
        import numpy as np
        NUM_HEADS = 16
        CLAMP = 10000.0
        key = jax.random.key(seed)
        ks = jax.random.split(key, 8)
        B, Nq, Nkv, Cq, Ckv = (4, 256, 256, 128, 96)
        s_q = 1.0 / np.sqrt(Cq)
        s_kv = 1.0 / np.sqrt(Ckv)
        return {'query': jax.random.normal(ks[0], (B, Nq, Cq), jnp.float32), 'key_value': jax.random.normal(ks[1], (B, Nkv, Ckv), jnp.float32), 'Wq': jax.random.normal(ks[2], (Cq, Cq), jnp.float32) * s_q, 'bq': jnp.zeros((Cq,), jnp.float32), 'Wk': jax.random.normal(ks[3], (Ckv, Cq), jnp.float32) * s_kv, 'bk': jnp.zeros((Cq,), jnp.float32), 'Wv': jax.random.normal(ks[4], (Ckv, Cq), jnp.float32) * s_kv, 'bv': jnp.zeros((Cq,), jnp.float32), 'Wo': jax.random.normal(ks[5], (Cq, Cq), jnp.float32) * s_q, 'bo': jnp.zeros((Cq,), jnp.float32)}
    _L0_xattn_all = _L0_xattn_setup()
    _L0_xattn_in = {k: v for k, v in _L0_xattn_all.items() if k in ('Wq', 'bq', 'Wk', 'bk', 'Wv', 'bv', 'Wo', 'bo')}
    del _L0_xattn_all

    def _L0_ffn_setup():
        import jax, jax.numpy as jnp
        import numpy as np
        DIM = 128
        HIDDEN = 384
        SCALE = 1.0 / 127.0

        def _dequant(w_int, dtype):
            return w_int.astype(dtype) * jnp.asarray(SCALE, dtype)
        key = jax.random.key(seed)
        k_x, k_g, k_u, k_d = jax.random.split(key, 4)
        x = jax.random.normal(k_x, (4, 256, DIM), dtype=jnp.float32)
        w_gate = jax.random.randint(k_g, (HIDDEN, DIM), -127, 128, dtype=jnp.int32)
        w_up = jax.random.randint(k_u, (HIDDEN, DIM), -127, 128, dtype=jnp.int32)
        w_down = jax.random.randint(k_d, (DIM, HIDDEN), -127, 128, dtype=jnp.int32)
        return {'x': x, 'w_gate': w_gate, 'w_up': w_up, 'w_down': w_down}
    _L0_ffn_all = _L0_ffn_setup()
    _L0_ffn_in = {k: v for k, v in _L0_ffn_all.items() if k in ('w_gate', 'w_up', 'w_down')}
    del _L0_ffn_all

    def _L1_xattn_setup():
        import jax, jax.numpy as jnp
        import numpy as np
        import math
        E = 128
        EV = 128
        FFN = 512
        DINO = 96
        B, S, P = (64, 64, 32)

        def bitnet_linear(x, W, b):
            w_scale = jnp.maximum(jnp.mean(jnp.abs(W)), 1e-05)
            qW = jnp.sign(W) * (jnp.abs(W) > 0.5 * w_scale).astype(W.dtype)
            i_scale = jnp.maximum(jnp.max(jnp.abs(x)), 1e-08) / 127.0
            qx = jnp.clip(jnp.round(x / i_scale), -128.0, 127.0)
            out = jnp.einsum('...i,oi->...o', qx, qW) * (w_scale * i_scale)
            return out + b
        key = jax.random.key(seed)
        ks = iter(jax.random.split(key, 32))

        def lin_w(fin, fout):
            return jax.random.normal(next(ks), (fout, fin), jnp.float32) * math.sqrt(2.0 / fin)
        return {'text_embeddings': jax.random.normal(next(ks), (B, S, E), jnp.float32), 'dinov2_features': jax.random.normal(next(ks), (B, P, DINO), jnp.float32), 'W_d2v': lin_w(DINO, EV), 'b_d2v': jnp.zeros((EV,), jnp.float32), 'W_img': lin_w(EV, E), 'b_img': jnp.zeros((E,), jnp.float32), 'W_txt': lin_w(E, E), 'b_txt': jnp.zeros((E,), jnp.float32), 'W_att0': lin_w(E, E // 2), 'b_att0': jnp.zeros((E // 2,), jnp.float32), 'W_att1': lin_w(E, E // 2), 'b_att1': jnp.zeros((E // 2,), jnp.float32), 'W_f1': lin_w(2 * E, FFN), 'b_f1': jnp.zeros((FFN,), jnp.float32), 'W_f2': lin_w(FFN, E), 'b_f2': jnp.zeros((E,), jnp.float32)}
    _L1_xattn_all = _L1_xattn_setup()
    _L1_xattn_in = {k: v for k, v in _L1_xattn_all.items() if k in ('W_d2v', 'b_d2v', 'W_img', 'b_img', 'W_txt', 'b_txt', 'W_att0', 'b_att0', 'W_att1', 'b_att1', 'W_f1', 'b_f1', 'W_f2', 'b_f2')}
    del _L1_xattn_all

    def _L1_ffn_setup():
        import jax, jax.numpy as jnp
        import numpy as np
        import math
        HID, HD, E, MIN_E = (128, 128, 16, 2)
        B, T = (4, 256)
        IS_CAUSAL = True

        def _l2norm(x, axis):
            return x / jnp.sqrt(jnp.sum(x * x, axis=axis, keepdims=True) + 1e-12)

        def _gating(hidden_states, sim_matrix, gates):
            b, t, c = hidden_states.shape
            flat = hidden_states.reshape(b * t, c)
            logits = _l2norm(flat, -1) @ _l2norm(sim_matrix, 0) - jax.nn.sigmoid(gates)
            gated = jax.nn.relu(logits)
            mask = (gated > 0).astype(gated.dtype)
            inactive = jnp.sum(mask, axis=1) == 0
            _, top_idx = jax.lax.top_k(logits, MIN_E)
            fb = jnp.sum(jax.nn.one_hot(top_idx, E, dtype=mask.dtype), axis=1)
            mask = mask + inactive[:, None].astype(mask.dtype) * fb
            masked = jnp.where(mask > 0, gated, -jnp.inf)
            probs = jax.nn.softmax(masked, axis=-1)
            return probs
        key = jax.random.key(seed)
        ks = jax.random.split(key, 6)
        a_qkv = math.sqrt(6.0 / (HID + HD))
        a_o = math.sqrt(6.0 / (HD + HID))
        return {'hidden_states': jax.random.normal(ks[0], (B, T, HID), jnp.float32), 'sim_matrix': jax.random.normal(ks[1], (HID, E), jnp.float32), 'gates': jnp.zeros((E,), jnp.float32), 'q_proj': jax.random.uniform(ks[2], (E, HID, HD), jnp.float32, -a_qkv, a_qkv), 'k_proj': jax.random.uniform(ks[3], (E, HID, HD), jnp.float32, -a_qkv, a_qkv), 'v_proj': jax.random.uniform(ks[4], (E, HID, HD), jnp.float32, -a_qkv, a_qkv), 'o_proj': jax.random.uniform(ks[5], (E, HD, HID), jnp.float32, -a_o, a_o)}
    _L1_ffn_all = _L1_ffn_setup()
    _L1_ffn_in = {k: v for k, v in _L1_ffn_all.items() if k in ('sim_matrix', 'gates', 'q_proj', 'k_proj', 'v_proj', 'o_proj')}
    del _L1_ffn_all
    return {'x': x, 'ctx_768': ctx_768, 'L0_xattn_Wq': _L0_xattn_in['Wq'], 'L0_xattn_bq': _L0_xattn_in['bq'], 'L0_xattn_Wk': _L0_xattn_in['Wk'], 'L0_xattn_bk': _L0_xattn_in['bk'], 'L0_xattn_Wv': _L0_xattn_in['Wv'], 'L0_xattn_bv': _L0_xattn_in['bv'], 'L0_xattn_Wo': _L0_xattn_in['Wo'], 'L0_xattn_bo': _L0_xattn_in['bo'], 'L0_ffn_w_gate': _L0_ffn_in['w_gate'], 'L0_ffn_w_up': _L0_ffn_in['w_up'], 'L0_ffn_w_down': _L0_ffn_in['w_down'], 'L1_xattn_W_d2v': _L1_xattn_in['W_d2v'], 'L1_xattn_b_d2v': _L1_xattn_in['b_d2v'], 'L1_xattn_W_img': _L1_xattn_in['W_img'], 'L1_xattn_b_img': _L1_xattn_in['b_img'], 'L1_xattn_W_txt': _L1_xattn_in['W_txt'], 'L1_xattn_b_txt': _L1_xattn_in['b_txt'], 'L1_xattn_W_att0': _L1_xattn_in['W_att0'], 'L1_xattn_b_att0': _L1_xattn_in['b_att0'], 'L1_xattn_W_att1': _L1_xattn_in['W_att1'], 'L1_xattn_b_att1': _L1_xattn_in['b_att1'], 'L1_xattn_W_f1': _L1_xattn_in['W_f1'], 'L1_xattn_b_f1': _L1_xattn_in['b_f1'], 'L1_xattn_W_f2': _L1_xattn_in['W_f2'], 'L1_xattn_b_f2': _L1_xattn_in['b_f2'], 'L1_ffn_sim_matrix': _L1_ffn_in['sim_matrix'], 'L1_ffn_gates': _L1_ffn_in['gates'], 'L1_ffn_q_proj': _L1_ffn_in['q_proj'], 'L1_ffn_k_proj': _L1_ffn_in['k_proj'], 'L1_ffn_v_proj': _L1_ffn_in['v_proj'], 'L1_ffn_o_proj': _L1_ffn_in['o_proj']}

def reference(x, ctx_768, L0_xattn_Wq, L0_xattn_bq, L0_xattn_Wk, L0_xattn_bk, L0_xattn_Wv, L0_xattn_bv, L0_xattn_Wo, L0_xattn_bo, L0_ffn_w_gate, L0_ffn_w_up, L0_ffn_w_down, L1_xattn_W_d2v, L1_xattn_b_d2v, L1_xattn_W_img, L1_xattn_b_img, L1_xattn_W_txt, L1_xattn_b_txt, L1_xattn_W_att0, L1_xattn_b_att0, L1_xattn_W_att1, L1_xattn_b_att1, L1_xattn_W_f1, L1_xattn_b_f1, L1_xattn_W_f2, L1_xattn_b_f2, L1_ffn_sim_matrix, L1_ffn_gates, L1_ffn_q_proj, L1_ffn_k_proj, L1_ffn_v_proj, L1_ffn_o_proj):
    import jax
    import jax.numpy as jnp

    def _L0_xattn_ref(query, key_value, Wq, bq, Wk, bk, Wv, bv, Wo, bo):
        import jax, jax.numpy as jnp
        import numpy as np
        NUM_HEADS = 16
        CLAMP = 10000.0
        B, Nq, Cq = query.shape
        Nkv = key_value.shape[1]
        H = NUM_HEADS
        D = Cq // H
        scale = D ** (-0.5)
        q = (query @ Wq + bq).reshape(B, Nq, H, D).transpose(0, 2, 1, 3)
        k = (key_value @ Wk + bk).reshape(B, Nkv, H, D).transpose(0, 2, 1, 3)
        v = (key_value @ Wv + bv).reshape(B, Nkv, H, D).transpose(0, 2, 1, 3)
        attn = jnp.einsum('bhqd,bhkd->bhqk', q, k) * scale
        attn = jnp.clip(attn, -CLAMP, CLAMP)
        attn = jax.nn.softmax(attn, axis=-1)
        attn = jnp.where(jnp.any(jnp.isnan(attn)), jnp.asarray(1.0 / Nkv, attn.dtype), attn)
        x = jnp.einsum('bhqk,bhkd->bqhd', attn, v).reshape(B, Nq, Cq)
        return x @ Wo + bo

    def _L0_ffn_ref(x, w_gate, w_up, w_down):
        import jax, jax.numpy as jnp
        import numpy as np
        DIM = 128
        HIDDEN = 384
        SCALE = 1.0 / 127.0

        def _dequant(w_int, dtype):
            return w_int.astype(dtype) * jnp.asarray(SCALE, dtype)
        wg = _dequant(w_gate, x.dtype)
        wu = _dequant(w_up, x.dtype)
        wd = _dequant(w_down, x.dtype)
        gate = jnp.einsum('bsd,hd->bsh', x, wg)
        up = jnp.einsum('bsd,hd->bsh', x, wu)
        h = jax.nn.silu(gate) * up
        return jnp.einsum('bsh,dh->bsd', h, wd)

    def _L1_xattn_ref(text_embeddings, dinov2_features, W_d2v, b_d2v, W_img, b_img, W_txt, b_txt, W_att0, b_att0, W_att1, b_att1, W_f1, b_f1, W_f2, b_f2):
        import jax, jax.numpy as jnp
        import numpy as np
        import math
        E = 128
        EV = 128
        FFN = 512
        DINO = 96
        B, S, P = (64, 64, 32)

        def bitnet_linear(x, W, b):
            w_scale = jnp.maximum(jnp.mean(jnp.abs(W)), 1e-05)
            qW = jnp.sign(W) * (jnp.abs(W) > 0.5 * w_scale).astype(W.dtype)
            i_scale = jnp.maximum(jnp.max(jnp.abs(x)), 1e-08) / 127.0
            qx = jnp.clip(jnp.round(x / i_scale), -128.0, 127.0)
            out = jnp.einsum('...i,oi->...o', qx, qW) * (w_scale * i_scale)
            return out + b
        b, s, e = text_embeddings.shape
        vis = bitnet_linear(dinov2_features, W_d2v, b_d2v)
        image_embeds = bitnet_linear(vis, W_img, b_img)
        fused = bitnet_linear(text_embeddings, W_txt, b_txt)
        inv_sqrt_e = 1.0 / math.sqrt(e)
        for Wa, ba in ((W_att0, b_att0), (W_att1, b_att1)):
            kv = bitnet_linear(image_embeds, Wa, ba)
            k = jnp.concatenate([kv, kv], axis=-1)
            scores = jnp.einsum('bse,bpe->bsp', fused, k) * inv_sqrt_e
            attn = jax.nn.softmax(scores, axis=-1)
            fused = fused + 0.1 * jnp.einsum('bsp,bpe->bse', attn, k)
        avg_img = jnp.mean(image_embeds, axis=1, keepdims=True)
        concatenated = jnp.concatenate([fused, jnp.broadcast_to(avg_img, (b, s, e))], axis=-1)
        h = jax.nn.relu(bitnet_linear(concatenated, W_f1, b_f1))
        return bitnet_linear(h, W_f2, b_f2)

    def _L1_ffn_ref(hidden_states, sim_matrix, gates, q_proj, k_proj, v_proj, o_proj):
        import jax, jax.numpy as jnp
        import numpy as np
        import math
        HID, HD, E, MIN_E = (128, 128, 16, 2)
        B, T = (4, 256)
        IS_CAUSAL = True

        def _l2norm(x, axis):
            return x / jnp.sqrt(jnp.sum(x * x, axis=axis, keepdims=True) + 1e-12)

        def _gating(hidden_states, sim_matrix, gates):
            b, t, c = hidden_states.shape
            flat = hidden_states.reshape(b * t, c)
            logits = _l2norm(flat, -1) @ _l2norm(sim_matrix, 0) - jax.nn.sigmoid(gates)
            gated = jax.nn.relu(logits)
            mask = (gated > 0).astype(gated.dtype)
            inactive = jnp.sum(mask, axis=1) == 0
            _, top_idx = jax.lax.top_k(logits, MIN_E)
            fb = jnp.sum(jax.nn.one_hot(top_idx, E, dtype=mask.dtype), axis=1)
            mask = mask + inactive[:, None].astype(mask.dtype) * fb
            masked = jnp.where(mask > 0, gated, -jnp.inf)
            probs = jax.nn.softmax(masked, axis=-1)
            return probs
        b, t, c = hidden_states.shape
        rw = _gating(hidden_states, sim_matrix, gates).reshape(b, t, E)
        q = jnp.einsum('btc,ech,bte->bth', hidden_states, q_proj, rw)
        k = jnp.einsum('btc,ech,bte->bth', hidden_states, k_proj, rw)
        v = jnp.einsum('btc,ech,bte->bth', hidden_states, v_proj, rw)
        scale = 1.0 / math.sqrt(HD)
        scores = jnp.einsum('bqh,bkh->bqk', q, k) * scale
        if IS_CAUSAL:
            causal = jnp.tril(jnp.ones((t, t), dtype=bool))
            scores = jnp.where(causal[None], scores, -jnp.inf)
        attn = jax.nn.softmax(scores, axis=-1)
        ao = jnp.einsum('bqk,bkh->bqh', attn, v)
        out = jnp.einsum('bth,ehc,bte->btc', ao, o_proj, rw)
        return out
    x = x + _L0_xattn_ref(_layernorm(x, axis=-1), ctx_768, L0_xattn_Wq, L0_xattn_bq, L0_xattn_Wk, L0_xattn_bk, L0_xattn_Wv, L0_xattn_bv, L0_xattn_Wo, L0_xattn_bo)
    x = x + _L0_ffn_ref(_layernorm(x, axis=-1), L0_ffn_w_gate, L0_ffn_w_up, L0_ffn_w_down)
    x = x + _L1_xattn_ref(_layernorm(x, axis=-1), ctx_768, L1_xattn_W_d2v, L1_xattn_b_d2v, L1_xattn_W_img, L1_xattn_b_img, L1_xattn_W_txt, L1_xattn_b_txt, L1_xattn_W_att0, L1_xattn_b_att0, L1_xattn_W_att1, L1_xattn_b_att1, L1_xattn_W_f1, L1_xattn_b_f1, L1_xattn_W_f2, L1_xattn_b_f2)
    x = x + _L1_ffn_ref(_layernorm(x, axis=-1), L1_ffn_sim_matrix, L1_ffn_gates, L1_ffn_q_proj, L1_ffn_k_proj, L1_ffn_v_proj, L1_ffn_o_proj)
    return x

_drawn_inputs = setup_inputs


def setup_inputs(seed=0):
    import zlib

    import numpy as np

    out = dict(_drawn_inputs(seed))
    spreads = {'L0_xattn_bq': (0.0, 0.273),
     'L0_xattn_bk': (0.0, 2.0),
     'L0_xattn_bv': (0.0, 0.1),
     'L0_xattn_bo': (0.0, 0.1),
     'L1_xattn_b_d2v': (0.0, 0.8),
     'L1_xattn_b_img': (0.0, 0.8),
     'L1_xattn_b_txt': (0.0, 0.8),
     'L1_xattn_b_att0': (0.0, 2.0),
     'L1_xattn_b_att1': (0.0, 2.0),
     'L1_xattn_b_f1': (0.0, 2.0),
     'L1_xattn_b_f2': (0.0, 2.0),
     'L1_ffn_gates': (0.0, 2.0)}
    factors = {'L1_xattn_W_d2v': 8.0,
     'L1_xattn_W_img': 8.0,
     'L1_xattn_W_txt': 8.0,
     'L1_xattn_W_att0': 8.0,
     'L1_xattn_W_att1': 8.0,
     'L1_xattn_W_f1': 8.0,
     'L1_xattn_W_f2': 8.0,
     'L1_ffn_sim_matrix': 47.231,
     'L1_ffn_q_proj': 48.627,
     'L1_ffn_k_proj': 53.644,
     'L1_ffn_v_proj': 41.574,
     'L1_ffn_o_proj': 40.692}
    for name, (base, spread) in spreads.items():
        noise = np.random.default_rng([zlib.crc32(name.encode()), seed]).standard_normal(out[name].shape)
        drawn = base * np.exp(spread * noise) if base else spread * noise
        out[name] = jnp.asarray(drawn.astype(out[name].dtype))
    for name, factor in factors.items():
        out[name] = (out[name] * factor).astype(out[name].dtype)
    return out
```

```python
from contextlib import ExitStack

import concourse.bass as bass
from concourse import mybir

F32 = mybir.dt.float32
BF16 = mybir.dt.bfloat16
I32 = mybir.dt.int32
ALU = mybir.AluOpType
ACT = mybir.ActivationFunctionType
AX = mybir.AxisListType

EPS_LN = 1e-5
CLAMP = 10000.0
MAGIC = 12582912.0
NEG = -1.0e30
R = 128


def build(nc, x, ctx_kv, Wq, bq, Wk, bk, Wv, bv, Wo, bo, w_gate, w_up, w_down,
          W_d2v, b_d2v, W_img, b_img, W_txt, b_txt, W_att0, b_att0, W_att1, b_att1,
          W_f1, b_f1, W_f2, b_f2, sim_matrix, gates, q_proj, k_proj, v_proj, o_proj, out):
    B, T, C = x.shape
    NK, CK = ctx_kv.shape[1:]
    NT = B * T // R
    TB = T // R
    H = 16
    D = C // H
    HG = 4
    NG = H // HG
    KM = R
    KT = NK - KM
    KP = 32
    KW = KM + KP
    HC = w_gate.shape[0] // R
    FC = W_f1.shape[0] // R
    E = sim_matrix.shape[1]
    HA = W_att0.shape[0]
    NC = B * NK
    SC0 = float(D) ** -0.5
    SC1 = float(C) ** -0.5

    with ExitStack() as stack:
        def sb(name, shape, dt=F32):
            return stack.enter_context(nc.sbuf_tensor(name, shape, dt))

        sems = {}

        def S(name):
            if name not in sems:
                sems[name] = stack.enter_context(nc.semaphore(name))
            return sems[name]

        PS = stack.enter_context(nc.psum_tensor("PS", [R, 8, 512], F32))

        def bank(k, n=512, off=0, rows=R):
            return PS[0:rows, k, off:off + n]

        ident = sb("ident", [R, R])
        identb = sb("identb", [R, R], BF16)
        ones = sb("ones", [R, R])
        headmask = sb("headmask", [R, H])
        causal = sb("causal", [R, R])
        down16 = sb("down16", [R, E])
        half = sb("half", [R, NT])
        X = sb("X", [R, NT, C])
        XN = sb("XN", [R, NT, C])
        XNT = sb("XNT", [R, NT * R])
        XB = sb("XB", [R, NT, C])
        stats = sb("stats", [R, NT, 6])
        mv = sb("mv", [R, NT, 2])
        vare = sb("vare", [R, NT])
        rstd = sb("rstd", [R, NT])
        CM = sb("CM", [R, B, CK])
        CT = sb("CT", [KT, B, CK])
        ctxT = sb("ctxT", [CK, B, NK])
        ctxTail = sb("ctxTail", [CK, B, HG, KP])
        Wq_s = sb("Wq_s", [R, C])
        Wk_s = sb("Wk_s", [CK, C])
        Wv_s = sb("Wv_s", [CK, C])
        Wo_s = sb("Wo_s", [R, C])
        cols = sb("cols", [R, 8])
        bfc = sb("bfc", [R, FC])
        rows_b = sb("rows_b", [R, 3, C])
        QT = sb("QT", [R, NT * R])
        KTs = sb("KTs", [R, B, NK])
        KBD = sb("KBD", [R, B, H, NK])
        VM = sb("VM", [R, B, H, D + 1])
        VT = sb("VT", [R, B, NG, HG, D + 1])
        SCL = sb("SCL", [R, 2, HG, NK])
        mx = sb("mx", [R, 2, HG])
        P0 = sb("P0", [R, 2, HG * KW])
        PT0 = sb("PT0", [R, 2, (HG + 1) * R])
        rec0 = sb("rec0", [R, H])
        ON = sb("ON", [R, H, D])
        OT = sb("OT", [R, R])
        WGi = sb("WGi", [R, 3, HC, C], I32)
        WGf = sb("WGf", [R, 3, HC, C])
        WGT = sb("WGT", [R, 3, HC, R])
        SG = sb("SG", [R, 2, T])
        HH = sb("HH", [R, HC, T])
        WL = [sb("WL0", [R, CK]), sb("WL1", [R, C]), sb("WL2", [R, C]), sb("WL3", [R, C]), sb("WL4", [R, C]),
              sb("WL5", [R, FC * 2 * C]), sb("WL6", [R, FC * R])]
        WQb = [sb(f"WQb{j}", list(WL[j].shape), BF16) for j in range(7)]
        WLt = sb("WLt", [R, FC * 2 * C], BF16)
        WQT = [sb("WQT0", [CK, R], BF16), sb("WQT1", [R, R], BF16), sb("WQT2", [R, R], BF16), sb("WQT3", [R, R], BF16),
               sb("WQT4", [R, R], BF16), sb("WQT5", [R, FC * 2, R], BF16), sb("WQT6", [R, FC, R], BF16)]
        wsum = sb("wsum", [R, 7])
        wsc = sb("wsc", [R, 7])
        wth = sb("wth", [R, 2, 7])
        amax = sb("amax", [R, 6])
        grow = sb("grow", [1, 6])
        isc = sb("isc", [R, 6])
        rinv = sb("rinv", [R, 6])
        osc = sb("osc", [R, 8])
        rounded = sb("rounded", [R, 2 * NC])
        QC = sb("QC", [CK, NC], BF16)
        VIS = sb("VIS", [R, NC])
        QV = sb("QV", [R, NC], BF16)
        IMG = sb("IMG", [R, NC])
        QI = sb("QI", [R, NC], BF16)
        KA = [sb(f"KA{l}", [R, B, NK]) for l in range(2)]
        KKm = [sb(f"KKm{l}", [R, B, R]) for l in range(2)]
        KKt = [sb(f"KKt{l}", [KT, B, R]) for l in range(2)]
        avg = sb("avg", [R, B])
        avga = sb("avga", [R, 2])
        avgr = sb("avgr", [R, B])
        QA = sb("QA", [R, B], BF16)
        f1b = sb("f1b", [R, FC, B])
        FT = sb("FT", [R, NT * R])
        RND = sb("RND", [R, NT * R])
        QX = sb("QX", [R, NT * R], BF16)
        QH = sb("QH", [R, FC, NT * R], BF16)
        HT = KBD[:, :, :, :].rearrange("p b h k -> p (b h k)")[:, 0:FC * NT * R].rearrange("p (k t) -> p k t", k=FC)
        mx1 = sb("mx1", [R, NT])
        nm1 = sb("nm1", [R, NT])
        den1 = sb("den1", [R, NT])
        rd1 = sb("rd1", [R, NT])
        P1 = SCL[:, :, :, :].rearrange("p a h k -> p (a h) k")
        PM1 = QT
        PX1 = sb("PX1", [KT, NT * R])
        WE = sb("WE", [R, E, 3, C])
        OE = sb("OE", [R, E, C])
        SIM = sb("SIM", [R, E])
        SIM2 = sb("SIM2", [R, E])
        simr = sb("simr", [R, E])
        SIMN = sb("SIMN", [R, E])
        sigg = sb("sigg", [R, E])
        sq = sb("sq", [R, C])
        ssq = sb("ssq", [R, NT])
        rn = sb("rn", [R, NT])
        LG = sb("LG", [R, NT, E])
        g1 = sb("g1", [R, NT, E])
        g2 = sb("g2", [R, NT, E])
        g3 = sb("g3", [R, NT, E])
        msk = sb("msk", [R, NT, E])
        fb = sb("fb", [R, NT, E])
        r1 = sb("r1", [R, NT])
        r2 = sb("r2", [R, NT])
        RW = sb("RW", [R, NT, E])
        ACC = sb("ACC", [R, NT, 3, C])
        free = KBD[:, :, :, :].rearrange("p b h k -> p (b h k)")
        qkT = free[:, 0:2 * NT * R].rearrange("p (m t) -> p m t", m=2)
        cmx = sb("cmx", [R, NT])
        cnm = sb("cnm", [R, NT])
        cden = sb("cden", [R, NT])
        crd = sb("crd", [R, NT])
        PC = P0[:, :, :].rearrange("p a k -> p (a k)")[:, 0:2 * T].rearrange("p (a t) -> p a t", a=2)
        PCT = PT0[:, :, :].rearrange("p a k -> p (a k)")[:, 0:2 * T].rearrange("p (a t) -> p a t", a=2)
        AO = free[:, 2 * NT * R:3 * NT * R].rearrange("p (i c) -> p i c", i=NT)
        AOT = free[:, 3 * NT * R:4 * NT * R]

        block = stack.enter_context(nc.Block())
        we_src = [q_proj, k_proj, v_proj]

        @block.sync
        def _(sp):
            for b in range(B):
                sp.dma_start(X[:, b * TB:(b + 1) * TB, :], x[b].rearrange("(i p) c -> p i c", p=R)).then_inc(S("ld_x"), 16)
            sp.dma_start(CM[:, :, :], ctx_kv[:, 0:KM, :].rearrange("b p c -> p b c")).then_inc(S("ld_ctx"), 16)
            sp.dma_start(CT[:, :, :], ctx_kv[:, KM:NK, :].rearrange("b p c -> p b c")).then_inc(S("ld_ctx"), 16)
            sp.dma_start(Wq_s[:, :], Wq).then_inc(S("ld_attn"), 16)
            sp.dma_start(Wk_s[:, :], Wk).then_inc(S("ld_attn"), 16)
            sp.dma_start(Wv_s[:, :], Wv).then_inc(S("ld_attn"), 16)
            for k, v in enumerate((bq, bk)):
                sp.dma_start(cols[:, k:k + 1], v.rearrange("(p o) -> p o", o=1)).then_inc(S("ld_attn"), 16)
            sp.dma_start(rows_b[:, 0, :], bv.rearrange("(o c) -> o c", o=1).to_broadcast([R, C])).then_inc(S("ld_attn"), 16)
            sp.dma_start(Wo_s[:, :], Wo).then_inc(S("ld_wo"), 16)
            sp.dma_start(rows_b[:, 1, :], bo.rearrange("(o c) -> o c", o=1).to_broadcast([R, C])).then_inc(S("ld_wo"), 16)
            sp.dma_start(WGi[:, 0, :, :], w_gate.rearrange("(k p) c -> p k c", p=R)).then_inc(S("ld_ffn"), 16)
            sp.dma_start(WGi[:, 1, :, :], w_up.rearrange("(k p) c -> p k c", p=R)).then_inc(S("ld_ffn"), 16)
            sp.dma_start(WGi[:, 2, :, :], w_down.rearrange("p (k c) -> p k c", c=R)).then_inc(S("ld_ffn"), 16)
            for s in range(0, E, 4):
                for n in range(3):
                    sp.dma_start(WE[:, s:s + 4, n, :], we_src[n][s:s + 4].rearrange("e c h -> c e h")).then_inc(S("ld_we"), 16)
            for s in range(0, E, 4):
                sp.dma_start(OE[:, s:s + 4, :], o_proj[s:s + 4].rearrange("e c h -> c e h")).then_inc(S("ld_oe"), 16)
            for b in range(B):
                sp.wait_ge(S("omixed"), TB * (b + 1) * (E // 4))
                sp.dma_start(out[b].rearrange("(i p) c -> p i c", p=R), X[:, b * TB:(b + 1) * TB, :]).then_inc(S("st_out"), 16)
            sp.wait_ge(S("st_out"), 16 * B)

        @block.gpsimd
        def _(pool):
            pool.memset(ident[:, :], 0.0).then_inc(S("c0"), 1)
            pool.memset(ones[:, :], 1.0).then_inc(S("c0"), 1)
            pool.memset(headmask[:, :], 1.0).then_inc(S("c0"), 1)
            pool.memset(causal[:, :], 0.0).then_inc(S("c0"), 1)
            pool.memset(half[:, :], -0.5).then_inc(S("c0"), 1)
            pool.wait_ge(S("c0"), 5)
            pool.affine_select(out=ident[:, :], in_=ident[:, :], compare_op=ALU.not_equal, fill=1.0, base=0,
                               pattern=[[-1, R]], channel_multiplier=1).then_inc(S("c1"), 1)
            pool.affine_select(out=headmask[:, :], in_=headmask[:, :], compare_op=ALU.is_ge, fill=0.0, base=0,
                               pattern=[[-D, H]], channel_multiplier=1).then_inc(S("c1"), 1)
            pool.wait_ge(S("c1"), 2)
            pool.affine_select(out=headmask[:, :], in_=headmask[:, :], compare_op=ALU.is_ge, fill=0.0, base=D - 1,
                               pattern=[[D, H]], channel_multiplier=-1).then_inc(S("consts"), 1)
            pool.affine_select(out=causal[:, :], in_=causal[:, :], compare_op=ALU.is_ge, fill=NEG, base=0,
                               pattern=[[-1, R]], channel_multiplier=1).then_inc(S("consts"), 1)
            pool.tensor_copy(identb[:, :], ident[:, :]).then_inc(S("consts"), 1)
            pool.iota(down16[:, :], pattern=[[-1, E]], base=E, channel_multiplier=0,
                      allow_small_or_imprecise_dtypes=True).then_inc(S("consts"), 1)

            def rsqrt(dst, src, tmp, eps, ready, done, k, n):
                pool.wait_ge(ready, k)
                pool.tensor_scalar(tmp, src, 1.0, eps, ALU.mult, ALU.add).then_inc(S("p_eps"), 1)
                cnt[0] += 1
                pool.wait_ge(S("p_eps"), cnt[0])
                pool.tensor_tensor(dst, tmp, half[0:n, 0:1].to_broadcast(list(dst.shape)) if dst.shape[1] > NT else
                                   half[0:n, 0:dst.shape[1]], ALU.pow).then_inc(done, 1)
            cnt = [0]

            def ln_rstd(stage):
                for b in range(B):
                    sl = slice(b * TB, (b + 1) * TB)
                    rsqrt(rstd[:, sl], mv[:, sl, 1], vare[:, sl], EPS_LN, S(f"ln{stage}_var"), S(f"ln{stage}_rstd"), b + 1, R)

            pool.wait_ge(S("consts"), 4)
            ln_rstd(1)
            pool.wait_ge(S("sim_sum"), 1)
            pool.tensor_scalar(SIM2[:, :], SIM2[:, :], 1.0, 1e-12, ALU.mult, ALU.add).then_inc(S("p_sim"), 1)
            pool.wait_ge(S("p_sim"), 1)
            for k in range(0, E, NT):
                pool.tensor_tensor(simr[:, k:k + NT], SIM2[:, k:k + NT], half[:, :], ALU.pow).then_inc(S("p_sim"), 1)
            pool.wait_ge(S("p_sim"), 1 + E // NT)
            pool.tensor_tensor(SIMN[:, :], SIM[:, :], simr[:, :], ALU.mult).then_inc(S("simn"), 1)
            ln_rstd(2)
            ln_rstd(3)
            ln_rstd(4)
            for b in range(B):
                sl = slice(b * TB, (b + 1) * TB)
                rsqrt(rn[:, sl], ssq[:, sl], vare[:, sl], 1e-12, S("ssq"), S("rn"), TB * (b + 1), R)

        @block.scalar
        def _(act):
            for j, w in enumerate((W_d2v, W_img, W_txt, W_att0, W_att1)):
                act.dma_start(WL[j][0:w.shape[0], :], w).then_inc(S("ld_wl"), 16)
            act.dma_start(WL[5][:, :].rearrange("p (k c) -> p k c", k=FC), W_f1.rearrange("(k p) c -> p k c", p=R)).then_inc(S("ld_wl"), 16)
            act.dma_start(WL[6][:, :], W_f2).then_inc(S("ld_wl"), 16)
            for k, v in enumerate((b_d2v, b_img, b_txt)):
                act.dma_start(cols[:, 2 + k:3 + k], v.rearrange("(p o) -> p o", o=1)).then_inc(S("ld_bl"), 16)
            for k, v in enumerate((b_att0, b_att1)):
                for d in range(2):
                    act.dma_start(cols[d * HA:(d + 1) * HA, 5 + k:6 + k], v.rearrange("(p o) -> p o", o=1)).then_inc(S("ld_bl"), 16)
            with nc.allow_non_contiguous_dma(reason="a bias of 512 values, one per partition and chunk"):
                act.dma_start(bfc[:, :], b_f1.rearrange("(k p) -> p k", p=R)).then_inc(S("ld_bl"), 16)
            act.dma_start(rows_b[:, 2, :], b_f2.rearrange("(o c) -> o c", o=1).to_broadcast([R, C])).then_inc(S("ld_bl"), 16)
            act.dma_start(SIM[:, :], sim_matrix).then_inc(S("ld_sim"), 16)
            act.dma_start(sigg[:, :], gates.rearrange("(o c) -> o c", o=1).to_broadcast([R, E])).then_inc(S("ld_sim"), 16)

            act.wait_ge(S("ld_sim"), 32)
            act.activation(sigg[:, :], sigg[:, :], ACT.Exp, scale=-1.0).then_inc(S("gate_exp"), 1)

            for n in range(NT * NG + 2):
                if n < NT * NG:
                    act.wait_ge(S("shifted"), n + 1)
                    if n >= 2:
                        act.wait_ge(S("probs_turned"), n - 1)
                    act.activation(P0[:, n % 2, 0:HG * KM].rearrange("p (j k) -> p j k", j=HG), SCL[:, n % 2, :, 0:KM], ACT.Exp)
                    act.activation(P0[:, n % 2, HG * KM:].rearrange("p (j k) -> p j k", j=HG)[:, :, 0:KT], SCL[:, n % 2, :, KM:NK],
                                   ACT.Exp).then_inc(S("probs"), 1)
                if n >= 1 and n - 1 < NT * NG:
                    m = n - 1
                    act.wait_ge(S("probs_turned"), m + 1)
                    if m >= 2:
                        act.wait_ge(S("pv"), m - 1)
                    act.activation(PT0[:, m % 2, :], PS[:, 4:6, :].rearrange("p a b -> p (a b)")[:, 0:(HG + 1) * R],
                                   ACT.Copy).then_inc(S("probsT"), 1)

            for n in range(B * HC):
                act.wait_ge(S("gate"), n + 1)
                if n >= 2:
                    act.wait_ge(S("hid"), n - 1)
                act.activation(SG[:, n % 2, :], bank(2 * (n % HC)), ACT.Silu).then_inc(S("silu"), 1)

            for l in range(2):
                act.wait_ge(S("nm1"), l + 1)
                if l:
                    act.wait_ge(S("p1_turned"), 2)
                for i in range(NT):
                    act.activation(P1[:, i, :], PS[:, i // 2, (i % 2) * NK:(i % 2 + 1) * NK], ACT.Exp, bias=nm1[:, i:i + 1],
                                   scale=SC1, accum_out=den1[:, i:i + 1]).then_inc(S("p1"), 1)
                act.wait_ge(S("p1_turned"), 2 * (l + 1))
                for b in range(B):
                    act.activation(PX1[:, b * T:(b + 1) * T], bank(6 + b, rows=KT), ACT.Copy).then_inc(S("p1_tail"), 1)

            act.wait_ge(S("f1b"), 1)
            for n in range(B * FC):
                b, k = divmod(n, FC)
                act.wait_ge(S("h_sum"), n + 1)
                act.activation(HT[:, k, b * T:(b + 1) * T], bank(n % 4), ACT.Relu, bias=f1b[:, k, b:b + 1],
                               scale=osc[:, 5:6]).then_inc(S("h"), 1)
            act.wait_ge(S("sc5"), 1)
            for k in range(FC):
                act.activation(HT[:, k, :], HT[:, k, :], ACT.Copy, scale=rinv[:, 5:6], bias=MAGIC).then_inc(S("h_rnd"), 1)

            for i in range(NT):
                act.wait_ge(S("ln4_xn"), i + 1)
                if i:
                    act.wait_ge(S("ssq"), i)
                act.activation(sq[:, :], XN[:, i, :], ACT.Square, accum_out=ssq[:, i:i + 1]).then_inc(S("ssq"), 1)
            act.wait_ge(S("gshift"), 1)
            act.activation(g3[:, :, :], g2[:, :, :], ACT.Exp).then_inc(S("gexp"), 1)

            for n in range(NT):
                q = n % TB
                act.wait_ge(S("cnm"), n + 1)
                if n >= 2:
                    act.wait_ge(S("pc_turned"), n - 1)
                act.activation(PC[:, n % 2, 0:(q + 1) * R], bank(4 + n % 2, (q + 1) * R), ACT.Exp, bias=cnm[:, n:n + 1],
                               scale=SC1, accum_out=cden[:, n:n + 1]).then_inc(S("pc"), 1)
                act.wait_ge(S("pc_turned"), n + 1)
                if n >= 2:
                    act.wait_ge(S("cpv"), n - 1)
                act.activation(PCT[:, n % 2, 0:(q + 1) * R], bank(6, (q + 1) * R), ACT.Copy).then_inc(S("pcT"), 1)

        @block.tensor
        def _(pe):
            def turn(dst, src, n=R, idn=ident):
                return pe.transpose(dst, src, idn[0:n, 0:n])

            def ln_turn(stage, banks):
                for b in range(B):
                    for i in range(TB):
                        t = b * TB + i
                        pe.wait_ge(S(f"ln{stage}_xn"), t + 1)
                        last = turn(bank(banks[b], R, i * R), XN[:, t, :])
                    last.then_inc(S(f"ln{stage}_T"), 1)

            pe.wait_ge(S("consts"), 4)
            pe.wait_ge(S("ld_ctx"), 32)
            for b in range(B):
                turn(bank(0, KM, b * NK, CK), CM[:, b, :])
                last = turn(bank(0, KT, b * NK + KM, CK), CT[:, b, :], KT)
            last.then_inc(S("ctxT_ps"), 1)
            ln_turn(1, [1, 2])
            pe.wait_ge(S("ld_attn"), 16 * 6)
            pe.wait_ge(S("ctxT"), 3)
            pe.matmul(bank(3, NC), Wk_s[:, :], ctxT[:, :, :].rearrange("p b k -> p (b k)"), start=True, stop=True).then_inc(S("k_ps"), 1)
            for b in range(B):
                pe.matmul(bank(4, C, b * C), ctxT[:, b, 0:KM], Wv_s[:, :], start=True, stop=True)
                last = pe.matmul(bank(5, C, b * C), ctxTail[:, b, :, :].rearrange("p j k -> p (j k)"), Wv_s[:, :], start=True, stop=True)
            last.then_inc(S("v_ps"), 1)
            for b in range(B):
                pe.wait_ge(S("ln1_XT"), b + 1)
                pe.matmul(bank(6 + b), Wq_s[:, :], XNT[:, b * T:(b + 1) * T], start=True, stop=True).then_inc(S("q_ps"), 1)

            pe.wait_ge(S("kbd"), 2)
            pe.wait_ge(S("vaug"), 1)
            pe.wait_ge(S("ld_wo"), 32)

            def scores(n):
                i, g = divmod(n, NG)
                b = i // TB
                pe.wait_ge(S("q"), b + 1)
                if n >= 2:
                    pe.wait_ge(S("clipped"), n - 1)
                for a in range(2):
                    last = pe.matmul(bank(2 * (n % 2) + a, 2 * NK), QT[:, i * R:(i + 1) * R],
                                     KBD[:, b, HG * g + 2 * a:HG * g + 2 * a + 2, :].rearrange("p h k -> p (h k)"), start=True, stop=True)
                last.then_inc(S("scores"), 1)

            def turn_probs(n):
                pe.wait_ge(S("probs"), n + 1)
                if n >= 1:
                    pe.wait_ge(S("probsT"), n)
                for j in range(HG):
                    turn(bank(4, R, j * R), P0[:, n % 2, j * KM:(j + 1) * KM])
                turn(bank(5, R), P0[:, n % 2, HG * KM:]).then_inc(S("probs_turned"), 1)

            def pv(n):
                i, g = divmod(n, NG)
                b = i // TB
                pe.wait_ge(S("probsT"), n + 1)
                if g == 0 and i >= 1:
                    pe.wait_ge(S("on"), i)
                w = D + 1
                pe.matmul(bank(6, HG * w, g * HG * w), PT0[:, n % 2, HG * R:], VT[:, b, g, :, :].rearrange("p j d -> p (j d)"),
                          start=True, stop=False, skip_group_check=True)
                for j in range(HG):
                    last = pe.matmul(bank(6, w, (g * HG + j) * w), PT0[:, n % 2, j * R:(j + 1) * R], VM[:, b, g * HG + j, :],
                                     start=False, stop=j == HG - 1, skip_group_check=True)
                last.then_inc(S("pv"), 1)

            def turn_heads(i):
                pe.wait_ge(S("on"), i + 1)
                if i >= 1:
                    pe.wait_ge(S("x1"), i)
                turn(bank(7, R), ON[:, :, :].rearrange("p h d -> p (h d)")).then_inc(S("oT_ps"), 1)

            def project(i):
                pe.wait_ge(S("oT"), i + 1)
                pe.matmul(bank(7, C, R), OT[:, :], Wo_s[:, :], start=True, stop=True).then_inc(S("attn"), 1)

            for n in range(NT * NG + 5):
                if n < NT * NG:
                    scores(n)
                if 1 <= n <= NT * NG:
                    turn_probs(n - 1)
                if 2 <= n <= NT * NG + 1:
                    pv(n - 2)
                if n >= 8 and (n - 8) % NG == 0:
                    project((n - 8) // NG)
                if n >= 6 and (n - 6) % NG == 0 and (n - 6) // NG < NT:
                    turn_heads((n - 6) // NG)

            pe.wait_ge(S("wg_f"), 1)
            for m in range(3):
                for k in range(HC):
                    last = turn(bank(m, R, k * R), WGf[:, m, k, :])
            last.then_inc(S("wgT_ps"), 1)
            pe.wait_ge(S("wabs"), 1)
            pe.matmul(bank(3, 7), ones[:, :], wsum[:, :], start=True, stop=True).then_inc(S("wsum_ps"), 1)
            pe.matmul(bank(4, E), ones[:, :], SIM2[:, :], start=True, stop=True).then_inc(S("simsum_ps"), 1)
            pe.wait_ge(S("wter"), 1)
            def bview(k, n, off, rows=R):
                return bank(k).bitcast(BF16)[0:rows, off:off + n]
            for j in range(5):
                o = WL[j].shape[1]
                turn(bview(5, R, j * R, o), WQb[j][:, 0:o], R, identb)
            for k in range(FC * 2):
                turn(bview(6, R, k * R), WQb[5][:, k * R:(k + 1) * R], R, identb)
            for k in range(FC):
                last = turn(bview(7, R, k * R), WQb[6][:, k * R:(k + 1) * R], R, identb)
            last.then_inc(S("wterT_ps"), 1)

            def spread_max(k, src_ready):
                pe.wait_ge(src_ready, 1)
                pe.transpose(bank(4, R, 0, 1), amax[:, k:k + 1], ident[:, :]).then_inc(S(f"mxT{k}"), 1)
                pe.wait_ge(S(f"mxr{k}"), 1)
                pe.matmul(bank(4, 1), ones[0:1, :], grow[0:1, k:k + 1], start=True, stop=True).then_inc(S(f"mxb{k}"), 1)

            pe.wait_ge(S("wterT"), 3)
            pe.wait_ge(S("wsc"), 1)
            spread_max(0, S("amax0"))
            pe.wait_ge(S("qx0"), 1)
            pe.matmul(bank(3, NC), WQT[0][:, :], QC[:, :], start=True, stop=True).then_inc(S("bn0"), 1)
            spread_max(1, S("amax1"))
            pe.wait_ge(S("qx1"), 1)
            pe.matmul(bank(3, NC), WQT[1][:, :], QV[:, :], start=True, stop=True).then_inc(S("bn1"), 1)
            spread_max(2, S("amax2"))
            pe.wait_ge(S("qx2"), 1)
            for l in range(2):
                pe.matmul(bank(5 + l, NC), WQT[3 + l][:, :], QI[:, :], start=True, stop=True).then_inc(S("bn_kv"), 1)
            for l in range(2):
                pe.wait_ge(S("ka"), l + 1)
                for b in range(B):
                    turn(bank(3, R, (2 * l + b) * R), KA[l][:, b, 0:KM])
                    last = turn(bank(7, R, (2 * l + b) * R, KT), KA[l][:, b, KM:NK])
            last.then_inc(S("kk_ps"), 1)

            pe.wait_ge(S("wgT"), 3)
            for b in range(B):
                if b == 0:
                    pe.wait_ge(S("kk"), 2)
                for i in range(TB):
                    t = b * TB + i
                    pe.wait_ge(S("ln2_xn"), t + 1)
                    if i == 0 and b:
                        pe.wait_ge(S("ln2_XT"), b)
                    last = turn(bank(6, R, i * R), XN[:, t, :])
                last.then_inc(S("ln2_T"), 1)
                pe.wait_ge(S("ln2_XT"), b + 1)
                for k in range(HC):
                    n = b * HC + k
                    if b:
                        pe.wait_ge(S("hid"), n - HC + 1)
                    for m in range(2):
                        last = pe.matmul(bank(2 * k + m), WGT[:, m, k, :], XNT[:, b * T:(b + 1) * T], start=True, stop=True)
                    last.then_inc(S("gate"), 1)
                if b:
                    pe.wait_ge(S("x2"), b)
                for i in range(TB):
                    for k in range(HC):
                        pe.wait_ge(S("hid"), b * HC + k + 1)
                        last = pe.matmul(bank(7, C, i * R), HH[:, k, i * R:(i + 1) * R], WGT[:, 2, k, :], start=k == 0, stop=k == HC - 1)
                last.then_inc(S("ffn"), 1)

            ln_turn(3, [0, 1])
            spread_max(3, S("amax3"))
            for b in range(B):
                pe.wait_ge(S("qx3"), b + 1)
                if b == 0:
                    pe.wait_ge(S("ln3_XT"), 2)
                pe.matmul(bank(b), WQT[2][:, :], QX[:, b * T:(b + 1) * T], start=True, stop=True).then_inc(S("bn_txt"), 1)
            for l in range(2):
                pe.wait_ge(S("fused"), 2 * (l + 1))
                for i in range(NT):
                    last = pe.matmul(bank(i // 2, NK, (i % 2) * NK), FT[:, i * R:(i + 1) * R], KA[l][:, i // TB, :], start=True, stop=True)
                last.then_inc(S("s1"), 1)
                for b in range(B):
                    for i in range(TB):
                        t = b * TB + i
                        pe.wait_ge(S("p1n"), l * NT + t + 1)
                        turn(bank(4 + b, R, i * R), P1[:, t, 0:KM])
                        last = turn(bank(6 + b, R, i * R, KT), P1[:, t, KM:NK])
                    last.then_inc(S("p1_turned"), 1)
                for b in range(B):
                    pe.wait_ge(S("p1_main"), 2 * l + b + 1)
                    pe.wait_ge(S("p1_tail"), 2 * l + b + 1)
                    pe.matmul(bank(b), KKm[l][:, b, :], PM1[:, b * T:(b + 1) * T], start=True, stop=False)
                    pe.matmul(bank(b), KKt[l][:, b, :], PX1[:, b * T:(b + 1) * T], start=False, stop=True).then_inc(S("upd"), 1)
            spread_max(4, S("amax4"))
            pe.wait_ge(S("qa"), 1)
            for k in range(FC):
                last = pe.matmul(bank(5, B, k * B), WQT[5][:, 2 * k + 1, :], QA[:, :], start=True, stop=True)
            last.then_inc(S("bn_avg"), 1)
            for n in range(B * FC):
                b, k = divmod(n, FC)
                pe.wait_ge(S("qx4"), b + 1)
                if n >= 4:
                    pe.wait_ge(S("h"), n - 3)
                pe.matmul(bank(n % 4), WQT[5][:, 2 * k, :], QX[:, b * T:(b + 1) * T], start=True, stop=True).then_inc(S("h_sum"), 1)
            spread_max(5, S("amax5"))
            pe.wait_ge(S("qh"), FC)
            for i in range(NT):
                for k in range(FC):
                    last = pe.matmul(bank(i // TB, C, (i % TB) * R), QH[:, k, i * R:(i + 1) * R], WQT[6][:, k, :], start=k == 0, stop=k == FC - 1)
                if i % TB == TB - 1:
                    last.then_inc(S("bn_f2"), 1)

            ln_turn(4, [2, 3])
            pe.wait_ge(S("simn"), 1)
            for i in range(NT):
                pe.wait_ge(S("ln4_XT"), i // TB + 1)
                last = pe.matmul(bank(7, E, i * E), XNT[:, i * R:(i + 1) * R], SIMN[:, :], start=True, stop=True)
            last.then_inc(S("logits"), 1)
            pe.wait_ge(S("ld_we"), 16 * 12)
            n = 0
            for i in range(NT):
                for e in range(E):
                    if n >= 4:
                        pe.wait_ge(S("mixed"), n - 3)
                    pe.matmul(bank(n % 4, 3 * C), XNT[:, i * R:(i + 1) * R], WE[:, e, :, :].rearrange("p m h -> p (m h)"),
                              start=True, stop=True).then_inc(S("expert"), 1)
                    n += 1
            for i in range(NT):
                for m in range(2):
                    pe.wait_ge(S("mixed"), E * (i + 1))
                    if i % TB == 0 and i:
                        pe.wait_ge(S("qkT"), 2)
                    last = turn(bank(6 + m, R, (i % TB) * R), ACC[:, i, m, :])
                if i % TB == TB - 1:
                    last.then_inc(S("qkT_ps"), 1)
            pe.wait_ge(S("qkT"), 4)

            def cscore(n):
                b, q = divmod(n, TB)
                if n >= 2:
                    pe.wait_ge(S("pc"), n - 1)
                pe.matmul(bank(4 + n % 2, (q + 1) * R), qkT[:, 0, n * R:(n + 1) * R], qkT[:, 1, b * T:b * T + (q + 1) * R],
                          start=True, stop=True).then_inc(S("cscore"), 1)

            cscore(0)
            for n in range(NT):
                b, q = divmod(n, TB)
                if n + 1 < NT:
                    cscore(n + 1)
                pe.wait_ge(S("pc"), n + 1)
                if n:
                    pe.wait_ge(S("pcT"), n)
                for k in range(q + 1):
                    last = turn(bank(6, R, k * R), PC[:, n % 2, k * R:(k + 1) * R])
                last.then_inc(S("pc_turned"), 1)
                pe.wait_ge(S("pcT"), n + 1)
                if n:
                    pe.wait_ge(S("ao"), n)
                for k in range(q + 1):
                    last = pe.matmul(bank(7, C), PCT[:, n % 2, k * R:(k + 1) * R], ACC[:, b * TB + k, 2, :], start=k == 0, stop=k == q)
                last.then_inc(S("cpv"), 1)
            for b in range(B):
                if b:
                    pe.wait_ge(S("aoT"), 1)
                for i in range(TB):
                    pe.wait_ge(S("ao"), b * TB + i + 1)
                    last = turn(bank(5, R, i * R), AO[:, b * TB + i, :])
                last.then_inc(S("aoT_ps"), 1)
            pe.wait_ge(S("ld_oe"), 16 * 4)
            n = 0
            for i in range(NT):
                pe.wait_ge(S("aoT"), i // TB + 1)
                for e in range(0, E, 4):
                    if n >= 4:
                        pe.wait_ge(S("omixed"), n - 3)
                    pe.matmul(bank(n % 4), AOT[:, i * R:(i + 1) * R], OE[:, e:e + 4, :].rearrange("p m h -> p (m h)"),
                              start=True, stop=True).then_inc(S("oexpert"), 1)
                    n += 1

        @block.vector
        def _(v):
            chain = [0]

            def link(ins):
                chain[0] += 1
                ins.then_inc(S("v_chain"), 1)
                v.wait_ge(S("v_chain"), chain[0])

            def ln_stats(stage, i):
                link(v.bn_stats(stats[:, i, :], X[:, i, :]))
                a = v.bn_aggr(mv[:, i, :], stats[:, i, :])
                if i % TB == TB - 1:
                    a.then_inc(S(f"ln{stage}_var"), 1)
                else:
                    link(a)

            def ln_norm(stage, i):
                v.wait_ge(S(f"ln{stage}_rstd"), i // TB + 1)
                v.tensor_scalar(XN[:, i, :], X[:, i, :], mv[:, i, 0:1], rstd[:, i:i + 1], ALU.subtract, ALU.mult)\
                    .then_inc(S(f"ln{stage}_xn"), 1)

            def ln_out(stage, b, k):
                v.wait_ge(S(f"ln{stage}_T"), b + 1)
                v.tensor_copy(XNT[:, b * T:(b + 1) * T], bank(k)).then_inc(S(f"ln{stage}_XT"), 1)

            link(v.memset(P0[:, :, :], 0.0))
            link(v.memset(VM[:, :, :, :], 1.0))
            link(v.memset(VT[:, :, :, :, :], 0.0))
            for j in range(HG):
                link(v.memset(VT[j * KP:(j + 1) * KP, :, :, j, D:D + 1], 1.0))
            link(v.memset(ctxTail[:, :, :, :], 0.0))
            link(v.memset(wsum[:, :], 0.0))
            link(v.memset(WQb[3][:, :], 0.0))
            link(v.memset(WQb[4][:, :], 0.0))
            for b in range(B):
                v.wait_ge(S("ld_x"), 16 * B)
                for i in range(b * TB, (b + 1) * TB):
                    ln_stats(1, i)
            v.wait_ge(S("ctxT_ps"), 1)
            cps = bank(0, NC, 0, CK).rearrange("p (b k) -> p b k", b=B)
            v.tensor_copy(ctxT[:, :, :], cps).then_inc(S("ctxT"), 1)
            for b in range(B):
                v.tensor_copy(ctxTail[:, b, :, 0:KT], cps[:, b, KM:NK].unsqueeze(1).to_broadcast([CK, HG, KT])).then_inc(S("ctxT"), 1)
            for b in range(B):
                for i in range(b * TB, (b + 1) * TB):
                    ln_norm(1, i)
            for b in range(B):
                ln_out(1, b, 1 + b)
            v.wait_ge(S("ld_attn"), 16 * 6)
            v.wait_ge(S("k_ps"), 1)
            v.wait_ge(S("consts"), 4)
            link(v.tensor_scalar(KTs[:, :, :].rearrange("p b k -> p (b k)"), bank(3, NC), cols[:, 1:2], None, ALU.add))
            for b in range(B):
                v.tensor_tensor(KBD[:, b, :, :], KTs[:, b, :].unsqueeze(1).to_broadcast([R, H, NK]),
                                headmask[:, :].unsqueeze(2).to_broadcast([R, H, NK]), ALU.mult).then_inc(S("kbd"), 1)
            v.wait_ge(S("v_ps"), 1)
            bvr = rows_b[:, 0, :].rearrange("p (h d) -> p h d", h=H)
            for b in range(B):
                v.tensor_tensor(VM[:, b, :, 0:D], bank(4, C, b * C).rearrange("p (h d) -> p h d", h=H), bvr, ALU.add)
                for j in range(HG):
                    q = slice(j * KP, (j + 1) * KP)
                    src = bank(5, C, b * C).rearrange("p (g j d) -> p g j d", g=NG, j=HG)
                    last = v.tensor_tensor(VT[q, b, :, j, 0:D], src[q, :, j, :],
                                           rows_b[:, 0, :].rearrange("p (g j d) -> p g j d", g=NG, j=HG)[q, :, j, :], ALU.add)
            last.then_inc(S("vaug"), 1)
            for b in range(B):
                v.wait_ge(S("q_ps"), b + 1)
                v.tensor_scalar(QT[:, b * T:(b + 1) * T], bank(6 + b), cols[:, 0:1], SC0, ALU.add, ALU.mult).then_inc(S("q"), 1)
            v.wait_ge(S("ld_wo"), 32)
            v.tensor_tensor(XB[:, :, :], X[:, :, :], rows_b[:, 1, :].unsqueeze(1).to_broadcast([R, NT, C]), ALU.add).then_inc(S("xb"), 1)
            v.wait_ge(S("xb"), 1)

            def clip(n):
                v.wait_ge(S("scores"), n + 1)
                if n >= 2:
                    v.wait_ge(S("probs"), n - 1)
                src = PS[:, 2 * (n % 2):2 * (n % 2) + 2, 0:2 * NK]
                v.tensor_scalar(SCL[:, n % 2, :, :].rearrange("p (a h) k -> p a (h k)", a=2), src, CLAMP, -CLAMP, ALU.min, ALU.max)\
                    .then_inc(S("clipped"), 1)
                v.wait_ge(S("clipped"), n + 1)
                link(v.tensor_reduce(mx[:, n % 2, :], SCL[:, n % 2, :, :], AX.X, ALU.max))
                v.tensor_tensor(SCL[:, n % 2, :, :], SCL[:, n % 2, :, :], mx[:, n % 2, :].unsqueeze(2).to_broadcast([R, HG, NK]),
                                ALU.subtract).then_inc(S("shifted"), 1)

            def normalise(i):
                v.wait_ge(S("pv"), NG * (i + 1))
                if i:
                    v.wait_ge(S("oT_ps"), i)
                o = bank(6, H * (D + 1)).rearrange("p (h d) -> p h d", h=H)
                link(v.reciprocal(rec0[:, :].unsqueeze(2), o[:, :, D:D + 1]))
                v.tensor_tensor(ON[:, :, :], o[:, :, 0:D], rec0[:, :].unsqueeze(2).to_broadcast([R, H, D]), ALU.mult).then_inc(S("on"), 1)

            def take_heads(i):
                v.wait_ge(S("oT_ps"), i + 1)
                v.tensor_copy(OT[:, :], bank(7, R)).then_inc(S("oT"), 1)

            def add_residual(i):
                v.wait_ge(S("attn"), i + 1)
                v.tensor_tensor(X[:, i, :], bank(7, C, R), XB[:, i, :], ALU.add).then_inc(S("x1"), 1)
                v.wait_ge(S("x1"), i + 1)
                ln_stats(2, i)

            for n in range(NT * NG + 5):
                if n < NT * NG:
                    clip(n)
                if n >= 5 and (n - 5) % NG == 0 and (n - 5) // NG < NT:
                    normalise((n - 5) // NG)
                if n >= 7 and (n - 7) % NG == 0 and (n - 7) // NG < NT:
                    take_heads((n - 7) // NG)
                if n >= 8 and (n - 8) % NG == 0:
                    add_residual((n - 8) // NG)


            v.wait_ge(S("ld_ffn"), 48)
            v.tensor_scalar(WGf[:, :, :, :].rearrange("p a k c -> p (a k c)"), WGi[:, :, :, :].rearrange("p a k c -> p (a k c)"),
                            1.0 / 127.0, None, ALU.mult).then_inc(S("wg_f"), 1)
            v.wait_ge(S("ld_wl"), 16 * 7)
            v.wait_ge(S("ld_sim"), 32)
            v.wait_ge(S("ld_bl"), 16 * 9)
            for j in range(7):
                rws = HA if j in (3, 4) else R
                v.tensor_reduce(wsum[0:rws, j:j + 1], WL[j][0:rws, :], AX.X, ALU.add, apply_absolute_value=True)
            v.tensor_tensor(SIM2[:, :], SIM[:, :], SIM[:, :], ALU.mult).then_inc(S("wabs"), 1)
            v.wait_ge(S("wgT_ps"), 1)
            for m in range(3):
                v.tensor_copy(WGT[:, m, :, :].rearrange("p k c -> p (k c)"), bank(m, HC * R)).then_inc(S("wgT"), 1)
            v.wait_ge(S("wsum_ps"), 1)
            for j in range(7):
                rws = HA if j in (3, 4) else R
                last = v.tensor_scalar(wsc[:, j:j + 1], bank(3, 1, j), 1.0 / (rws * WL[j].shape[1]), 1e-5, ALU.mult, ALU.max)
            last.then_inc(S("wsc"), 1)
            v.wait_ge(S("wsc"), 1)
            v.tensor_scalar(wth[:, 0, :], wsc[:, :], 0.5, None, ALU.mult)
            link(v.tensor_scalar(wth[:, 1, :], wsc[:, :], -0.5, None, ALU.mult))
            v.wait_ge(S("simsum_ps"), 1)
            v.tensor_copy(SIM2[:, :], bank(4, E)).then_inc(S("sim_sum"), 1)
            for j in range(7):
                rws = HA if j in (3, 4) else R
                w = WL[j].shape[1]
                link(v.tensor_scalar(WLt[0:rws, 0:w], WL[j][0:rws, :], wth[0:rws, 1, j:j + 1], None, ALU.is_lt))
                last = v.scalar_tensor_tensor(WQb[j][0:rws, :], WL[j][0:rws, :], wth[0:rws, 0, j:j + 1], WLt[0:rws, 0:w], ALU.is_gt, ALU.subtract)
                if j < 6:
                    link(last)
            last.then_inc(S("wter"), 1)
            v.wait_ge(S("wterT_ps"), 1)

            def bview(k, n, off, rows=R):
                return bank(k).bitcast(BF16)[0:rows, off:off + n]
            for j in range(5):
                if j in (3, 4):
                    for d in range(2):
                        v.tensor_copy(WQT[j][:, d * HA:(d + 1) * HA], bview(5, HA, j * R))
                else:
                    o = WL[j].shape[1]
                    last = v.tensor_copy(WQT[j][:, :], bview(5, R, j * R, o))
            last.then_inc(S("wterT"), 1)
            v.tensor_copy(WQT[5][:, :, :].rearrange("p k c -> p (k c)"), bview(6, FC * 2 * R, 0)).then_inc(S("wterT"), 1)
            v.tensor_copy(WQT[6][:, :, :].rearrange("p k c -> p (k c)"), bview(7, FC * R, 0)).then_inc(S("wterT"), 1)
            v.wait_ge(S("gate_exp"), 1)
            link(v.tensor_scalar(sigg[:, :], sigg[:, :], 1.0, None, ALU.add))
            link(v.reciprocal(sigg[:, :], sigg[:, :]))

            def scale_of(k):
                v.wait_ge(S(f"mxT{k}"), 1)
                v.tensor_reduce(grow[0:1, k:k + 1], bank(4, R, 0, 1), AX.X, ALU.max).then_inc(S(f"mxr{k}"), 1)
                v.wait_ge(S(f"mxb{k}"), 1)
                link(v.tensor_scalar(isc[:, k:k + 1], bank(4, 1), 1e-8, 1.0 / 127.0, ALU.max, ALU.mult))
                v.reciprocal(rinv[:, k:k + 1], isc[:, k:k + 1]).then_inc(S(f"sc{k}"), 1)
                v.wait_ge(S(f"sc{k}"), 1)

            def quantise(dst, src, tmp, k, done):
                link(v.tensor_scalar(tmp, src, rinv[0:src.shape[0], k:k + 1], MAGIC, ALU.mult, ALU.add))
                v.tensor_scalar(dst, tmp, MAGIC, 127.0, ALU.subtract, ALU.min).then_inc(done, 1)

            v.memset(amax[:, :], 0.0).then_inc(S("am0"), 1)
            v.wait_ge(S("am0"), 1)
            cT = ctxT[:, :, :].rearrange("p b k -> p (b k)")
            v.tensor_reduce(amax[0:CK, 0:1], cT, AX.X, ALU.max, apply_absolute_value=True).then_inc(S("amax0"), 1)
            scale_of(0)
            quantise(QC[:, :], cT, rounded[0:CK, 0:NC], 0, S("qx0"))
            link(v.tensor_tensor(osc[:, 0:1], isc[:, 0:1], wsc[:, 0:1], ALU.mult))
            v.wait_ge(S("bn0"), 1)
            link(v.tensor_scalar(VIS[:, :], bank(3, NC), osc[:, 0:1], cols[:, 2:3], ALU.mult, ALU.add))
            v.tensor_reduce(amax[:, 1:2], VIS[:, :], AX.X, ALU.max, apply_absolute_value=True).then_inc(S("amax1"), 1)
            scale_of(1)
            quantise(QV[:, :], VIS[:, :], rounded[:, 0:NC], 1, S("qx1"))
            link(v.tensor_tensor(osc[:, 1:2], isc[:, 1:2], wsc[:, 1:2], ALU.mult))
            v.wait_ge(S("bn1"), 1)
            link(v.tensor_scalar(IMG[:, :], bank(3, NC), osc[:, 1:2], cols[:, 3:4], ALU.mult, ALU.add))
            v.tensor_reduce(amax[:, 2:3], IMG[:, :], AX.X, ALU.max, apply_absolute_value=True).then_inc(S("amax2"), 1)
            link(v.tensor_reduce(avg[:, :], IMG[:, :].rearrange("p (b k) -> p b k", b=B), AX.X, ALU.add))
            link(v.tensor_scalar(avg[:, :], avg[:, :], 1.0 / NK, None, ALU.mult))
            scale_of(2)
            quantise(QI[:, :], IMG[:, :], rounded[:, 0:NC], 2, S("qx2"))
            for l in range(2):
                link(v.tensor_tensor(osc[:, 3 + l:4 + l], isc[:, 2:3], wsc[:, 3 + l:4 + l], ALU.mult))
            for l in range(2):
                v.wait_ge(S("bn_kv"), l + 1)
                v.tensor_scalar(KA[l][:, :, :].rearrange("p b k -> p (b k)"), bank(5 + l, NC), osc[:, 3 + l:4 + l],
                                cols[:, 5 + l:6 + l], ALU.mult, ALU.add).then_inc(S("ka"), 1)
            v.wait_ge(S("kk_ps"), 1)
            for l in range(2):
                v.tensor_copy(KKm[l][:, :, :].rearrange("p b c -> p (b c)"), bank(3, B * R, 2 * l * R))
                v.tensor_copy(KKt[l][:, :, :].rearrange("p b c -> p (b c)"), bank(7, B * R, 2 * l * R, KT)).then_inc(S("kk"), 1)

            for i in range(NT):
                ln_norm(2, i)
            for b in range(B):
                v.wait_ge(S("ln2_T"), b + 1)
                v.tensor_copy(XNT[:, b * T:(b + 1) * T], bank(6)).then_inc(S("ln2_XT"), 1)
                for k in range(HC):
                    n = b * HC + k
                    v.wait_ge(S("silu"), n + 1)
                    if b:
                        v.wait_ge(S("ffn"), b)
                    v.tensor_tensor(HH[:, k, :], SG[:, n % 2, :], bank(2 * k + 1), ALU.mult).then_inc(S("hid"), 1)
                v.wait_ge(S("ffn"), b + 1)
                xb = X[:, b * TB:(b + 1) * TB, :].rearrange("p i c -> p (i c)")
                v.tensor_tensor(xb, xb, bank(7), ALU.add).then_inc(S("x2"), 1)
                v.wait_ge(S("x2"), b + 1)
                for i in range(b * TB, (b + 1) * TB):
                    ln_stats(3, i)

            for i in range(NT):
                ln_norm(3, i)
            v.wait_ge(S("ln3_xn"), NT)
            v.tensor_reduce(amax[:, 3:4], XN[:, :, :].rearrange("p i c -> p (i c)"), AX.X, ALU.max, apply_absolute_value=True).then_inc(S("amax3"), 1)
            for b in range(B):
                ln_out(3, b, b)
            v.tensor_tensor(XB[:, :, :], X[:, :, :], rows_b[:, 2, :].unsqueeze(1).to_broadcast([R, NT, C]), ALU.add).then_inc(S("xb"), 1)
            scale_of(3)
            link(v.tensor_tensor(osc[:, 2:3], isc[:, 3:4], wsc[:, 2:3], ALU.mult))
            v.wait_ge(S("ln3_XT"), 2)
            for b in range(B):
                sl = slice(b * T, (b + 1) * T)
                quantise(QX[:, sl], XNT[:, sl], RND[:, sl], 3, S("qx3"))
            for b in range(B):
                v.wait_ge(S("bn_txt"), b + 1)
                v.tensor_scalar(FT[:, b * T:(b + 1) * T], bank(b), osc[:, 2:3], cols[:, 4:5], ALU.mult, ALU.add).then_inc(S("fused"), 1)
            for l in range(2):
                v.wait_ge(S("s1"), l + 1)
                link(v.tensor_reduce(mx1[:, :], PS[:, 0:4, 0:2 * NK].rearrange("p a (i k) -> p a i k", i=2), AX.X, ALU.max))
                v.tensor_scalar(nm1[:, :], mx1[:, :], -SC1, None, ALU.mult).then_inc(S("nm1"), 1)
                for i in range(NT):
                    v.wait_ge(S("p1"), l * NT + i + 1)
                    link(v.reciprocal(rd1[:, i:i + 1], den1[:, i:i + 1]))
                    v.tensor_scalar(P1[:, i, :], P1[:, i, :], rd1[:, i:i + 1], 0.1, ALU.mult, ALU.mult).then_inc(S("p1n"), 1)
                for b in range(B):
                    v.wait_ge(S("p1_turned"), 2 * l + b + 1)
                    v.tensor_copy(PM1[:, b * T:(b + 1) * T], bank(4 + b)).then_inc(S("p1_main"), 1)
                for b in range(B):
                    v.wait_ge(S("upd"), 2 * l + b + 1)
                    ft = FT[:, b * T:(b + 1) * T]
                    v.tensor_tensor(ft, ft, bank(b), ALU.add).then_inc(S("fused"), 1)
                    v.wait_ge(S("fused"), 2 * (l + 1) + b + 1)
            v.tensor_reduce(avga[:, 0:1], FT[:, :], AX.X, ALU.max, apply_absolute_value=True)
            link(v.tensor_reduce(avga[:, 1:2], avg[:, :], AX.X, ALU.max, apply_absolute_value=True))
            v.tensor_reduce(amax[:, 4:5], avga[:, :], AX.X, ALU.max).then_inc(S("amax4"), 1)
            scale_of(4)
            link(v.tensor_tensor(osc[:, 5:6], isc[:, 4:5], wsc[:, 5:6], ALU.mult))
            quantise(QA[:, :], avg[:, :], avgr[:, :], 4, S("qa"))
            for b in range(B):
                sl = slice(b * T, (b + 1) * T)
                quantise(QX[:, sl], FT[:, sl], RND[:, sl], 4, S("qx4"))
            v.wait_ge(S("bn_avg"), 1)
            for k in range(FC):
                last = v.tensor_scalar(f1b[:, k, :], bank(5, B, k * B), osc[:, 5:6], bfc[:, k:k + 1], ALU.mult, ALU.add)
            last.then_inc(S("f1b"), 1)
            v.wait_ge(S("h"), B * FC)
            v.tensor_reduce(amax[:, 5:6], HT[:, :, :].rearrange("p k t -> p (k t)"), AX.X, ALU.max).then_inc(S("amax5"), 1)
            scale_of(5)
            link(v.tensor_tensor(osc[:, 6:7], isc[:, 5:6], wsc[:, 6:7], ALU.mult))
            for k in range(FC):
                v.wait_ge(S("h_rnd"), k + 1)
                v.tensor_scalar(QH[:, k, :], HT[:, k, :], MAGIC, 127.0, ALU.subtract, ALU.min).then_inc(S("qh"), 1)
            v.wait_ge(S("xb"), 2)
            for b in range(B):
                v.wait_ge(S("bn_f2"), b + 1)
                sl = slice(b * TB, (b + 1) * TB)
                link(v.scalar_tensor_tensor(X[:, sl, :].rearrange("p i c -> p (i c)"), bank(b), osc[:, 6:7],
                                            XB[:, sl, :].rearrange("p i c -> p (i c)"), ALU.mult, ALU.add))
                for i in range(b * TB, (b + 1) * TB):
                    ln_stats(4, i)

            for i in range(NT):
                ln_norm(4, i)
            for b in range(B):
                ln_out(4, b, 2 + b)
            v.wait_ge(S("logits"), 1)
            v.wait_ge(S("rn"), 2)

            def wide(col):
                return col.unsqueeze(2).to_broadcast([R, NT, E])
            lg = bank(7, NT * E).rearrange("p (i e) -> p i e", e=E)
            link(v.tensor_tensor(g1[:, :, :], lg, wide(rn[:, :]), ALU.mult))
            link(v.tensor_tensor(LG[:, :, :], g1[:, :, :], sigg[:, :].unsqueeze(1).to_broadcast([R, NT, E]), ALU.subtract))
            link(v.tensor_reduce(r1[:, :], LG[:, :, :], AX.X, ALU.max))
            link(v.tensor_scalar(r2[:, :], r1[:, :], 0.0, None, ALU.is_le))
            link(v.tensor_scalar(msk[:, :, :], LG[:, :, :], 0.0, None, ALU.is_gt))
            link(v.memset(fb[:, :, :], 0.0))
            link(v.tensor_copy(g2[:, :, :], LG[:, :, :]))
            d16 = down16[:, :].unsqueeze(1).to_broadcast([R, NT, E])
            for rnd in range(2):
                link(v.tensor_reduce(rn[:, :], g2[:, :, :], AX.X, ALU.max))
                link(v.tensor_tensor(g1[:, :, :], g2[:, :, :], wide(rn[:, :]), ALU.is_ge))
                link(v.tensor_tensor(g1[:, :, :], g1[:, :, :], d16, ALU.mult))
                link(v.tensor_reduce(rn[:, :], g1[:, :, :], AX.X, ALU.max))
                link(v.tensor_tensor(g1[:, :, :], g1[:, :, :], wide(rn[:, :]), ALU.is_ge))
                link(v.tensor_tensor(fb[:, :, :], fb[:, :, :], g1[:, :, :], ALU.add))
                link(v.scalar_tensor_tensor(g2[:, :, :].rearrange("p i e -> p (i e)"), g1[:, :, :].rearrange("p i e -> p (i e)"), NEG,
                                            g2[:, :, :].rearrange("p i e -> p (i e)"), ALU.mult, ALU.add))
            link(v.tensor_tensor(fb[:, :, :], fb[:, :, :], wide(r2[:, :]), ALU.mult))
            link(v.tensor_tensor(msk[:, :, :], msk[:, :, :], fb[:, :, :], ALU.add))
            link(v.tensor_scalar(r1[:, :], r1[:, :], 0.0, None, ALU.max))
            link(v.tensor_scalar(g2[:, :, :], LG[:, :, :], 0.0, None, ALU.max))
            v.tensor_tensor(g2[:, :, :], g2[:, :, :], wide(r1[:, :]), ALU.subtract).then_inc(S("gshift"), 1)
            v.wait_ge(S("gexp"), 1)
            link(v.tensor_tensor(g3[:, :, :], g3[:, :, :], msk[:, :, :], ALU.mult))
            link(v.tensor_reduce(r2[:, :], g3[:, :, :], AX.X, ALU.add))
            link(v.reciprocal(r1[:, :], r2[:, :]))
            link(v.tensor_tensor(RW[:, :, :], g3[:, :, :], wide(r1[:, :]), ALU.mult))
            n = 0
            for i in range(NT):
                acc = ACC[:, i, :, :].rearrange("p m c -> p (m c)")
                for e in range(E):
                    v.wait_ge(S("expert"), n + 1)
                    if e:
                        v.wait_ge(S("mixed"), n)
                        v.scalar_tensor_tensor(acc, bank(n % 4, 3 * C), RW[:, i, e:e + 1], acc, ALU.mult, ALU.add).then_inc(S("mixed"), 1)
                    else:
                        v.tensor_scalar(acc, bank(n % 4, 3 * C), RW[:, i, e:e + 1], None, ALU.mult).then_inc(S("mixed"), 1)
                    n += 1
            for b in range(B):
                v.wait_ge(S("qkT_ps"), b + 1)
                for m in range(2):
                    v.tensor_copy(qkT[:, m, b * T:(b + 1) * T], bank(6 + m)).then_inc(S("qkT"), 1)
            for n in range(NT):
                q = n % TB
                v.wait_ge(S("cscore"), n + 1)
                dg = bank(4 + n % 2, R, q * R)
                link(v.tensor_tensor(dg, dg, causal[:, :], ALU.add))
                link(v.tensor_reduce(cmx[:, n:n + 1], bank(4 + n % 2, (q + 1) * R), AX.X, ALU.max))
                v.tensor_scalar(cnm[:, n:n + 1], cmx[:, n:n + 1], -SC1, None, ALU.mult).then_inc(S("cnm"), 1)
                if n:
                    m = n - 1
                    v.wait_ge(S("cpv"), m + 1)
                    link(v.reciprocal(crd[:, m:m + 1], cden[:, m:m + 1]))
                    v.tensor_scalar(AO[:, m, :], bank(7, C), crd[:, m:m + 1], None, ALU.mult).then_inc(S("ao"), 1)
            m = NT - 1
            v.wait_ge(S("cpv"), m + 1)
            link(v.reciprocal(crd[:, m:m + 1], cden[:, m:m + 1]))
            v.tensor_scalar(AO[:, m, :], bank(7, C), crd[:, m:m + 1], None, ALU.mult).then_inc(S("ao"), 1)
            for b in range(B):
                v.wait_ge(S("aoT_ps"), b + 1)
                v.tensor_copy(AOT[:, b * T:(b + 1) * T], bank(5)).then_inc(S("aoT"), 1)
            n = 0
            for i in range(NT):
                for g in range(E // 4):
                    v.wait_ge(S("oexpert"), n + 1)
                    for j in range(4):
                        e = 4 * g + j
                        last = v.scalar_tensor_tensor(X[:, i, :], bank(n % 4, C, j * C), RW[:, i, e:e + 1], X[:, i, :], ALU.mult, ALU.add)
                        if j < 3:
                            link(last)
                    last.then_inc(S("omixed"), 1)
                    n += 1
                    v.wait_ge(S("omixed"), n)


_INS = ['x', 'ctx_768', 'L0_xattn_Wq', 'L0_xattn_bq', 'L0_xattn_Wk', 'L0_xattn_bk', 'L0_xattn_Wv', 'L0_xattn_bv',
        'L0_xattn_Wo', 'L0_xattn_bo', 'L0_ffn_w_gate', 'L0_ffn_w_up', 'L0_ffn_w_down', 'L1_xattn_W_d2v',
        'L1_xattn_b_d2v', 'L1_xattn_W_img', 'L1_xattn_b_img', 'L1_xattn_W_txt', 'L1_xattn_b_txt', 'L1_xattn_W_att0',
        'L1_xattn_b_att0', 'L1_xattn_W_att1', 'L1_xattn_b_att1', 'L1_xattn_W_f1', 'L1_xattn_b_f1', 'L1_xattn_W_f2',
        'L1_xattn_b_f2', 'L1_ffn_sim_matrix', 'L1_ffn_gates', 'L1_ffn_q_proj', 'L1_ffn_k_proj', 'L1_ffn_v_proj',
        'L1_ffn_o_proj']


def kernel(**inputs):
    import numpy as _np
    import concourse.bacc as _bacc
    from concourse import mybir as _mybir
    from concourse.bass_utils import run_bass_kernel_spmd as _run

    nc = _bacc.Bacc("TRN2", target_bir_lowering=False, num_devices=1)
    arrays, args = {}, []
    for name in _INS:
        a = _np.ascontiguousarray(inputs[name])
        arrays[f"in_{name}"] = a
        args.append(nc.dram_tensor(f"in_{name}", a.shape, _mybir.dt.from_np(a.dtype), kind="ExternalInput").ap())
    shape = tuple(inputs['x'].shape)
    args.append(nc.dram_tensor("out_0", shape, _mybir.dt.float32, kind="ExternalOutput").ap())
    build(nc, *args)
    r = _run(nc, [arrays], core_ids=[0])
    return r.results[0]["out_0"]
```

```python
from contextlib import ExitStack

import concourse.bass as bass
from concourse import mybir

F32 = mybir.dt.float32
BF16 = mybir.dt.bfloat16
F32R = mybir.dt.float32r
I32 = mybir.dt.int32
ALU = mybir.AluOpType
ACT = mybir.ActivationFunctionType
AX = mybir.AxisListType

EPS_LN = 1e-5
CLAMP = 10000.0
MAGIC = 12582912.0
NEG = -1.0e30
R = 128


def build(nc, x, ctx_kv, Wq, bq, Wk, bk, Wv, bv, Wo, bo, w_gate, w_up, w_down,
          W_d2v, b_d2v, W_img, b_img, W_txt, b_txt, W_att0, b_att0, W_att1, b_att1,
          W_f1, b_f1, W_f2, b_f2, sim_matrix, gates, q_proj, k_proj, v_proj, o_proj, out):
    B, T, C = x.shape
    NK, CK = ctx_kv.shape[1:]
    NT = B * T // R
    TB = T // R
    H = 16
    D = C // H
    HG = 4
    NG = H // HG
    NX = 3
    NS = 4
    KM = R
    KT = NK - KM
    KP = 32
    KW = KM + KP
    HC = w_gate.shape[0] // R
    FC = W_f1.shape[0] // R
    E = sim_matrix.shape[1]
    HA = W_att0.shape[0]
    NC = B * NK
    SC0 = float(D) ** -0.5
    SC1 = float(C) ** -0.5

    with ExitStack() as stack:
        def sb(name, shape, dt=F32):
            return stack.enter_context(nc.sbuf_tensor(name, shape, dt))

        early = ExitStack()

        def eb(name, shape, dt=F32):
            return early.enter_context(nc.sbuf_tensor(name, shape, dt))

        sems = {}

        def S(name):
            if name not in sems:
                sems[name] = stack.enter_context(nc.semaphore(name))
            return sems[name]

        def low_ready(m):
            if m < 2 * E:
                return S("xlo"), m + 1
            if m % 2:
                return S("xlo_gpsimd"), (m - 2 * E + 1) // 2
            return S("xlo"), 2 * E + (m - 2 * E) // 2 + 1

        PS = stack.enter_context(nc.psum_tensor("PS", [R, 8, 512], F32))

        def bank(k, n=512, off=0, rows=R):
            return PS[0:rows, k, off:off + n]

        ident = sb("ident", [R, R])
        identb = sb("identb", [R, R], BF16)
        ones = sb("ones", [R, R])
        headmask = sb("headmask", [R, H])
        causal = sb("causal", [R, R])
        down16 = sb("down16", [R, E])
        half = sb("half", [R, NT])
        X = sb("X", [R, NT, C])
        XN = sb("XN", [R, NT, C])
        XNT = sb("XNT", [R, NT * R])
        XB = sb("XB", [R, NT, C])
        stats = sb("stats", [R, NT, 6])
        mv = sb("mv", [R, NT, 2])
        vare = sb("vare", [R, NT])
        rstd = sb("rstd", [R, NT])
        SEL = sb("SEL", [96, E, R], BF16)
        WE = sb("WE", [R, E, 3, C])
        OE = sb("OE", [R, E, C])
        SIM = sb("SIM", [R, E])
        SIM2 = sb("SIM2", [R, E])
        simr = sb("simr", [R, E])
        SIMN = sb("SIMN", [R, E])
        sigg = sb("sigg", [R, E])
        sq = sb("sq", [R, C])
        ssq = sb("ssq", [R, NT])
        rn = sb("rn", [R, NT])
        LG = sb("LG", [R, NT, E])
        g1 = sb("g1", [R, NT, E])
        g2 = sb("g2", [R, NT, E])
        g3 = sb("g3", [R, NT, E])
        msk = sb("msk", [R, NT, E])
        fb = sb("fb", [R, NT, E])
        r1 = sb("r1", [R, NT])
        r2 = sb("r2", [R, NT])
        RW = sb("RW", [R, NT, E])
        CM = eb("CM", [R, B, CK])
        CT = eb("CT", [KT, B, CK])
        ctxT = eb("ctxT", [CK, B, NK])
        ctxTail = eb("ctxTail", [CK, B, HG, KP])
        Wq_s = eb("Wq_s", [R, C])
        Wk_s = eb("Wk_s", [CK, C])
        Wv_s = eb("Wv_s", [CK, C])
        Wo_s = eb("Wo_s", [R, C])
        cols = eb("cols", [R, 8])
        bfc = eb("bfc", [R, FC])
        rows_b = eb("rows_b", [R, 3, C])
        QT = eb("QT", [R, NT * R])
        KTs = eb("KTs", [R, B, NK])
        KBD = eb("KBD", [R, B, H, NK])
        VM = eb("VM", [R, B, H, D + 1])
        VT = eb("VT", [R, B, NG, HG, D + 1])
        SCL = eb("SCL", [R, NS, HG, NK])
        mx = eb("mx", [R, NS, HG])
        P0 = eb("P0", [R, 2, HG * KW])
        PT0 = eb("PT0", [R, 2, (HG + 1) * R])
        rec0 = eb("rec0", [R, H])
        ON = eb("ON", [R, H, D])
        OT = eb("OT", [R, R])
        WGi = eb("WGi", [R, 3, HC, C], I32)
        WGf = eb("WGf", [R, 3, HC, C])
        WGT = eb("WGT", [R, 3, HC, R])
        SG = eb("SG", [R, 2, T])
        HH = eb("HH", [R, HC, T])
        WL = [eb("WL0", [R, CK]), eb("WL1", [R, C]), eb("WL2", [R, C]), eb("WL3", [R, C]), eb("WL4", [R, C]),
              eb("WL5", [R, FC * 2 * C]), eb("WL6", [R, FC * R])]
        WQb = [eb(f"WQb{j}", list(WL[j].shape), BF16) for j in range(7)]
        WLt = eb("WLt", [R, FC * 2 * C], BF16)
        WQT = [eb("WQT0", [CK, R], BF16), eb("WQT1", [R, R], BF16), eb("WQT2", [R, R], BF16), eb("WQT3", [R, R], BF16),
               eb("WQT4", [R, R], BF16), eb("WQT5", [R, FC * 2, R], BF16), eb("WQT6", [R, FC, R], BF16)]
        wsum = eb("wsum", [R, 7])
        wsc = eb("wsc", [R, 7])
        wth = eb("wth", [R, 2, 7])
        amax = eb("amax", [R, 6])
        grow = eb("grow", [1, 6])
        isc = eb("isc", [R, 6])
        rinv = eb("rinv", [R, 6])
        osc = eb("osc", [R, 8])
        rounded = eb("rounded", [R, 2 * NC])
        QC = eb("QC", [CK, NC], BF16)
        VIS = eb("VIS", [R, NC])
        QV = eb("QV", [R, NC], BF16)
        IMG = eb("IMG", [R, NC])
        QI = eb("QI", [R, NC], BF16)
        KA = [eb(f"KA{l}", [R, B, NK]) for l in range(2)]
        KKm = [eb(f"KKm{l}", [R, B, R]) for l in range(2)]
        KKt = [eb(f"KKt{l}", [KT, B, R]) for l in range(2)]
        avg = eb("avg", [R, B])
        avga = eb("avga", [R, 2])
        avgr = eb("avgr", [R, B])
        QA = eb("QA", [R, B], BF16)
        f1b = eb("f1b", [R, FC, B])
        FT = eb("FT", [R, NT * R])
        RND = eb("RND", [R, NT * R])
        QX = eb("QX", [R, NT * R], BF16)
        QH = eb("QH", [R, FC, NT * R], BF16)
        HT = KBD[:, :, :, :].rearrange("p b h k -> p (b h k)")[:, 0:FC * NT * R].rearrange("p (k t) -> p k t", k=FC)
        mx1 = eb("mx1", [R, NT])
        nm1 = eb("nm1", [R, NT])
        den1 = eb("den1", [R, NT])
        rd1 = eb("rd1", [R, NT])
        P1 = SCL[:, 0:NT // HG, :, :].rearrange("p a h k -> p (a h) k")
        PM1 = QT
        PX1 = eb("PX1", [KT, NT * R])
        early.close()
        WEh = sb("WEh", [R, E, 3, C], F32R)
        WEl = sb("WEl", [R, E, 3, C], F32R)
        OEh = sb("OEh", [R, E, C], F32R)
        OEl = sb("OEl", [R, E, C], F32R)
        XE = sb("XE", [R, NX, T])
        XEh = sb("XEh", [R, NX, T], F32R)
        XEl = sb("XEl", [R, NX, T], F32R)
        RWS = sb("RWS", [R, NT, 96], BF16)
        RWT = sb("RWT", [96, NT * R], BF16)
        qkT = sb("qkT", [R, 2, NT * R])
        VC = sb("VC", [R, T])
        VV = sb("VV", [R, NT, C])
        AOT = sb("AOT", [R, NT * R])
        OC = sb("OC", [R, T])
        cmx = sb("cmx", [R, NT])
        cnm = sb("cnm", [R, NT])
        cden = sb("cden", [R, NT])
        crd = sb("crd", [R, NT])
        PC = sb("PC", [R, 2, T])
        PCT = sb("PCT", [R, 2, T])
        AO = XB

        block = stack.enter_context(nc.Block())
        we_src = [q_proj, k_proj, v_proj]

        @block.sync
        def _(sp):
            for b in range(B):
                sp.dma_start(X[:, b * TB:(b + 1) * TB, :], x[b].rearrange("(i p) c -> p i c", p=R)).then_inc(S("ld_x"), 16)
            sp.dma_start(CM[:, :, :], ctx_kv[:, 0:KM, :].rearrange("b p c -> p b c")).then_inc(S("ld_ctx"), 16)
            sp.dma_start(CT[:, :, :], ctx_kv[:, KM:NK, :].rearrange("b p c -> p b c")).then_inc(S("ld_ctx"), 16)
            sp.dma_start(Wq_s[:, :], Wq).then_inc(S("ld_attn"), 16)
            sp.dma_start(Wk_s[:, :], Wk).then_inc(S("ld_attn"), 16)
            sp.dma_start(Wv_s[:, :], Wv).then_inc(S("ld_attn"), 16)
            for k, v in enumerate((bq, bk)):
                sp.dma_start(cols[:, k:k + 1], v.rearrange("(p o) -> p o", o=1)).then_inc(S("ld_attn"), 16)
            sp.dma_start(rows_b[:, 0, :], bv.rearrange("(o c) -> o c", o=1).to_broadcast([R, C])).then_inc(S("ld_attn"), 16)
            sp.dma_start(Wo_s[:, :], Wo).then_inc(S("ld_wo"), 16)
            sp.dma_start(rows_b[:, 1, :], bo.rearrange("(o c) -> o c", o=1).to_broadcast([R, C])).then_inc(S("ld_wo"), 16)
            sp.dma_start(WGi[:, 0, :, :], w_gate.rearrange("(k p) c -> p k c", p=R)).then_inc(S("ld_ffn"), 16)
            sp.dma_start(WGi[:, 1, :, :], w_up.rearrange("(k p) c -> p k c", p=R)).then_inc(S("ld_ffn"), 16)
            sp.dma_start(WGi[:, 2, :, :], w_down.rearrange("p (k c) -> p k c", c=R)).then_inc(S("ld_ffn"), 16)
            for s in range(0, E, 4):
                for n in range(3):
                    sp.dma_start(WE[:, s:s + 4, n, :], we_src[n][s:s + 4].rearrange("e c h -> c e h")).then_inc(S("ld_we"), 16)
            for s in range(0, E, 4):
                sp.dma_start(OE[:, s:s + 4, :], o_proj[s:s + 4].rearrange("e c h -> c e h")).then_inc(S("ld_oe"), 16)
            for b in range(B):
                sp.wait_ge(S("out_ready"), b + 1)
                sp.dma_start(out[b].rearrange("(i p) c -> p i c", p=R), X[:, b * TB:(b + 1) * TB, :]).then_inc(S("st_out"), 16)
            sp.wait_ge(S("st_out"), 16 * B)

        @block.gpsimd
        def _(pool):
            pool.memset(ident[:, :], 0.0).then_inc(S("c0"), 1)
            pool.memset(ones[:, :], 1.0).then_inc(S("c0"), 1)
            pool.memset(headmask[:, :], 1.0).then_inc(S("c0"), 1)
            pool.memset(causal[:, :], 0.0).then_inc(S("c0"), 1)
            pool.memset(half[:, :], -0.5).then_inc(S("c0"), 1)
            pool.wait_ge(S("c0"), 5)
            pool.affine_select(out=ident[:, :], in_=ident[:, :], compare_op=ALU.not_equal, fill=1.0, base=0,
                               pattern=[[-1, R]], channel_multiplier=1).then_inc(S("c1"), 1)
            pool.affine_select(out=headmask[:, :], in_=headmask[:, :], compare_op=ALU.is_ge, fill=0.0, base=0,
                               pattern=[[-D, H]], channel_multiplier=1).then_inc(S("c1"), 1)
            pool.wait_ge(S("c1"), 2)
            pool.affine_select(out=headmask[:, :], in_=headmask[:, :], compare_op=ALU.is_ge, fill=0.0, base=D - 1,
                               pattern=[[D, H]], channel_multiplier=-1).then_inc(S("consts"), 1)
            pool.affine_select(out=causal[:, :], in_=causal[:, :], compare_op=ALU.is_ge, fill=NEG, base=0,
                               pattern=[[-1, R]], channel_multiplier=1).then_inc(S("consts"), 1)
            pool.tensor_copy(identb[:, :], ident[:, :]).then_inc(S("consts"), 1)
            pool.iota(down16[:, :], pattern=[[-1, E]], base=E, channel_multiplier=0,
                      allow_small_or_imprecise_dtypes=True).then_inc(S("consts"), 1)

            pool.memset(SEL[:, :, :], 0.0).then_inc(S("sel0"), 1)
            pool.wait_ge(S("sel0"), 1)
            for k in range(3):
                part = SEL[32 * k:32 * k + 32, :, :]
                pool.affine_select(out=part, in_=part, compare_op=ALU.not_equal, fill=1.0, base=0,
                                   pattern=[[-1, E], [0, R]], channel_multiplier=1).then_inc(S("sel"), 1)
                pool.wait_ge(S("sel"), k + 1)

            def rsqrt(dst, src, tmp, eps, ready, done, k, n):
                pool.wait_ge(ready, k)
                pool.tensor_scalar(tmp, src, 1.0, eps, ALU.mult, ALU.add).then_inc(S("p_eps"), 1)
                cnt[0] += 1
                pool.wait_ge(S("p_eps"), cnt[0])
                pool.tensor_tensor(dst, tmp, half[0:n, 0:1].to_broadcast(list(dst.shape)) if dst.shape[1] > NT else
                                   half[0:n, 0:dst.shape[1]], ALU.pow).then_inc(done, 1)
            cnt = [0]

            def ln_batch(stage, b):
                sl = slice(b * TB, (b + 1) * TB)
                rsqrt(rstd[:, sl], mv[:, sl, 1], vare[:, sl], EPS_LN, S(f"ln{stage}_var"), S(f"ln{stage}_rstd"), b + 1, R)

            def ln_rstd(stage):
                for b in range(B):
                    ln_batch(stage, b)

            pool.wait_ge(S("consts"), 4)
            ln_rstd(1)

            for n in range(NT * NG):
                pool.wait_ge(S("rowmax"), n + 1)
                pool.tensor_tensor(SCL[:, n % NS, :, :], SCL[:, n % NS, :, :], mx[:, n % NS, :].unsqueeze(2).to_broadcast([R, HG, NK]),
                                   ALU.subtract).then_inc(S("shifted"), 1)
                if n == NG * TB + 8:
                    ln_batch(2, 0)
            pool.wait_ge(S("sim_sum"), 1)
            pool.tensor_scalar(SIM2[:, :], SIM2[:, :], 1.0, 1e-12, ALU.mult, ALU.add).then_inc(S("p_sim"), 1)
            pool.wait_ge(S("p_sim"), 1)
            for k in range(0, E, NT):
                pool.tensor_tensor(simr[:, k:k + NT], SIM2[:, k:k + NT], half[:, :], ALU.pow).then_inc(S("p_sim"), 1)
            pool.wait_ge(S("p_sim"), 1 + E // NT)
            pool.tensor_tensor(SIMN[:, :], SIM[:, :], simr[:, :], ALU.mult).then_inc(S("simn"), 1)
            ln_batch(2, 1)
            ln_rstd(3)
            ln_rstd(4)
            for b in range(B):
                sl = slice(b * TB, (b + 1) * TB)
                rsqrt(rn[:, sl], ssq[:, sl], vare[:, sl], 1e-12, S("ssq"), S("rn"), TB * (b + 1), R)

            def low_part(m):
                pool.wait_ge(S("xhi"), m + 1)
                if m >= NX:
                    pool.wait_ge(S("expert"), m - NX + 1)
                pool.tensor_tensor(XEl[:, m % NX, :], XE[:, m % NX, :], XEh[:, m % NX, :].bitcast(F32), ALU.subtract).then_inc(S("xlo_gpsimd"), 1)

            for e in range(E):
                pool.wait_ge(S("w_hi"), e + 1)
                pool.tensor_tensor(WEl[:, e, :, :], WE[:, e, :, :], WEh[:, e, :, :].bitcast(F32), ALU.subtract).then_inc(S("w_lo"), 1)
            for e in range(0, E, 4):
                pool.wait_ge(S("o_hi"), e // 4 + 1)
                pool.tensor_tensor(OEl[:, e:e + 4, :], OE[:, e:e + 4, :], OEh[:, e:e + 4, :].bitcast(F32), ALU.subtract).then_inc(S("o_lo"), 1)
            for m in range(2 * E + 1, 4 * E, 2):
                low_part(m)

        @block.scalar
        def _(act):
            for j, w in enumerate((W_d2v, W_img, W_txt, W_att0, W_att1)):
                act.dma_start(WL[j][0:w.shape[0], :], w).then_inc(S("ld_wl"), 16)
            act.dma_start(WL[5][:, :].rearrange("p (k c) -> p k c", k=FC), W_f1.rearrange("(k p) c -> p k c", p=R)).then_inc(S("ld_wl"), 16)
            act.dma_start(WL[6][:, :], W_f2).then_inc(S("ld_wl"), 16)
            for k, v in enumerate((b_d2v, b_img, b_txt)):
                act.dma_start(cols[:, 2 + k:3 + k], v.rearrange("(p o) -> p o", o=1)).then_inc(S("ld_bl"), 16)
            for k, v in enumerate((b_att0, b_att1)):
                for d in range(2):
                    act.dma_start(cols[d * HA:(d + 1) * HA, 5 + k:6 + k], v.rearrange("(p o) -> p o", o=1)).then_inc(S("ld_bl"), 16)
            with nc.allow_non_contiguous_dma(reason="a bias of 512 values, one per partition and chunk"):
                act.dma_start(bfc[:, :], b_f1.rearrange("(k p) -> p k", p=R)).then_inc(S("ld_bl"), 16)
            act.dma_start(rows_b[:, 2, :], b_f2.rearrange("(o c) -> o c", o=1).to_broadcast([R, C])).then_inc(S("ld_bl"), 16)
            act.dma_start(SIM[:, :], sim_matrix).then_inc(S("ld_sim"), 16)
            act.dma_start(sigg[:, :], gates.rearrange("(o c) -> o c", o=1).to_broadcast([R, E])).then_inc(S("ld_sim"), 16)

            act.wait_ge(S("ld_sim"), 32)
            act.activation(sigg[:, :], sigg[:, :], ACT.Exp, scale=-1.0).then_inc(S("gate_exp"), 1)

            for n in range(NT * NG + 2):
                if n < NT * NG:
                    act.wait_ge(S("shifted"), n + 1)
                    if n >= 2:
                        act.wait_ge(S("probs_turned"), n - 1)
                    act.activation(P0[:, n % 2, 0:HG * KM].rearrange("p (j k) -> p j k", j=HG), SCL[:, n % NS, :, 0:KM], ACT.Exp)
                    act.activation(P0[:, n % 2, HG * KM:].rearrange("p (j k) -> p j k", j=HG)[:, :, 0:KT], SCL[:, n % NS, :, KM:NK],
                                   ACT.Exp).then_inc(S("probs"), 1)
                if n >= 1 and n - 1 < NT * NG:
                    m = n - 1
                    act.wait_ge(S("probs_turned"), m + 1)
                    if m >= 2:
                        act.wait_ge(S("pv"), m - 1)
                    act.activation(PT0[:, m % 2, :], PS[:, 4:6, :].rearrange("p a b -> p (a b)")[:, 0:(HG + 1) * R],
                                   ACT.Copy).then_inc(S("probsT"), 1)

            for n in range(B * HC):
                act.wait_ge(S("gate"), n + 1)
                if n >= 2:
                    act.wait_ge(S("hid"), n - 1)
                act.activation(SG[:, n % 2, :], bank(2 * (n % 2)), ACT.Silu).then_inc(S("silu"), 1)

            for l in range(2):
                act.wait_ge(S("nm1"), l + 1)
                if l:
                    act.wait_ge(S("p1_turned"), 2)
                for i in range(NT):
                    act.activation(P1[:, i, :], PS[:, i // 2, (i % 2) * NK:(i % 2 + 1) * NK], ACT.Exp, bias=nm1[:, i:i + 1],
                                   scale=SC1, accum_out=den1[:, i:i + 1]).then_inc(S("p1"), 1)
                act.wait_ge(S("p1_turned"), 2 * (l + 1))
                for b in range(B):
                    act.activation(PX1[:, b * T:(b + 1) * T], bank(6 + b, rows=KT), ACT.Copy).then_inc(S("p1_tail"), 1)

            act.wait_ge(S("f1b"), 1)
            for n in range(B * FC):
                b, k = divmod(n, FC)
                act.wait_ge(S("h_sum"), n + 1)
                act.activation(HT[:, k, b * T:(b + 1) * T], bank(n % 4), ACT.Relu, bias=f1b[:, k, b:b + 1],
                               scale=osc[:, 5:6]).then_inc(S("h"), 1)
            act.wait_ge(S("sc"), 6)
            for k in range(FC):
                act.activation(HT[:, k, :], HT[:, k, :], ACT.Copy, scale=rinv[:, 5:6], bias=MAGIC).then_inc(S("h_rnd"), 1)

            for i in range(NT):
                act.wait_ge(S("ln4_xn"), i + 1)
                if i:
                    act.wait_ge(S("ssq"), i)
                act.activation(sq[:, :], XN[:, i, :], ACT.Square, accum_out=ssq[:, i:i + 1]).then_inc(S("ssq"), 1)
            act.wait_ge(S("gshift"), 1)
            act.activation(g3[:, :, :], g2[:, :, :], ACT.Exp).then_inc(S("gexp"), 1)

            def high_part(m):
                act.wait_ge(S("xe"), m + 1)
                if m >= NX:
                    act.wait_ge(S("expert"), m - NX + 1)
                act.activation(XEh[:, m % NX, :], XE[:, m % NX, :], ACT.Copy).then_inc(S("xhi"), 1)

            def weight_high(e):
                act.activation(WEh[:, e, :, :], WE[:, e, :, :], ACT.Copy).then_inc(S("w_hi"), 1)

            def causal_scalar(b, t):
                k0 = 3 * b
                if 1 <= t < TB + 1:
                    q = t - 1
                    n = b * TB + q
                    act.wait_ge(S("pc_turned"), n + 1)
                    if n >= 2:
                        act.wait_ge(S("cpv"), n - 1)
                    act.activation(PCT[:, n % 2, 0:(q + 1) * R], bank(k0 + 1, (q + 1) * R), ACT.Copy).then_inc(S("pcT"), 1)
                if t < TB:
                    n = b * TB + t
                    act.wait_ge(S("cnm"), n + 1)
                    if n >= 2:
                        act.wait_ge(S("pc_turned"), n - 1)
                    act.activation(PC[:, n % 2, 0:(t + 1) * R], bank(k0, (t + 1) * R), ACT.Exp, bias=cnm[:, n:n + 1],
                                   scale=SC1, accum_out=cden[:, n:n + 1]).then_inc(S("pc"), 1)
                if t == 0:
                    act.wait_ge(S("v_turned"), b + 1)
                    act.activation(VV[:, b * TB:(b + 1) * TB, :].rearrange("p i c -> p (i c)"), bank(k0 + 2), ACT.Copy).then_inc(S("vv"), 1)

            act.wait_ge(S("ld_we"), 16 * 12)
            act.wait_ge(S("ld_oe"), 16 * 4)
            act.wait_ge(S("bn_f2"), 2)
            for e in range(2):
                weight_high(e)
            high_part(0)
            for m in range(4 * E):
                ph, e = divmod(m, E)
                if m + 1 < 4 * E:
                    high_part(m + 1)
                if ph == 0 and e + 2 < E:
                    weight_high(e + 2)
                if ph == 1 and e % 4 == 0:
                    act.activation(OEh[:, e:e + 4, :], OE[:, e:e + 4, :], ACT.Copy).then_inc(S("o_hi"), 1)
                if ph in (1, 2) and e == 0:
                    b = ph - 1
                    act.wait_ge(S("expert"), m)
                    act.activation(qkT[:, 0, b * T:(b + 1) * T], bank(3 * b), ACT.Copy).then_inc(S("qkv_out"), 1)
                    if b:
                        act.wait_ge(S("v_turned"), b)
                    act.activation(VC[:, :], bank(3 * b + 2), ACT.Copy).then_inc(S("qkv_out"), 1)
                if ph in (1, 2) and 1 <= e <= TB + 4:
                    causal_scalar(ph - 1, e - 1)
                if ph == 3 and e == 0:
                    act.wait_ge(S("expert"), m)
                    act.activation(OC[:, :], bank(0), ACT.Copy).then_inc(S("oc"), 1)
            act.wait_ge(S("expert"), 4 * E)
            act.wait_ge(S("oc_turned"), 1)
            act.activation(OC[:, :], bank(1), ACT.Copy).then_inc(S("oc"), 1)

        @block.tensor
        def _(pe):
            def turn(dst, src, n=R, idn=ident):
                return pe.transpose(dst, src, idn[0:n, 0:n])

            def ln_turn(stage, banks):
                for b in range(B):
                    for i in range(TB):
                        t = b * TB + i
                        pe.wait_ge(S(f"ln{stage}_xn"), t + 1)
                        last = turn(bank(banks[b], R, i * R), XN[:, t, :])
                    last.then_inc(S(f"ln{stage}_T"), 1)

            pe.wait_ge(S("consts"), 4)
            pe.wait_ge(S("ld_ctx"), 32)
            for b in range(B):
                turn(bank(0, KM, b * NK, CK), CM[:, b, :])
                last = turn(bank(0, KT, b * NK + KM, CK), CT[:, b, :], KT)
            last.then_inc(S("ctxT_ps"), 1)
            ln_turn(1, [1, 2])
            pe.wait_ge(S("ld_attn"), 16 * 6)
            pe.wait_ge(S("ctxT"), 3)
            pe.matmul(bank(3, NC), Wk_s[:, :], ctxT[:, :, :].rearrange("p b k -> p (b k)"), start=True, stop=True).then_inc(S("k_ps"), 1)
            for b in range(B):
                pe.matmul(bank(4, C, b * C), ctxT[:, b, 0:KM], Wv_s[:, :], start=True, stop=True)
                last = pe.matmul(bank(5, C, b * C), ctxTail[:, b, :, :].rearrange("p j k -> p (j k)"), Wv_s[:, :], start=True, stop=True)
            last.then_inc(S("v_ps"), 1)
            for b in range(B):
                pe.wait_ge(S("ln1_XT"), b + 1)
                pe.matmul(bank(6 + b), Wq_s[:, :], XNT[:, b * T:(b + 1) * T], start=True, stop=True).then_inc(S("q_ps"), 1)

            pe.wait_ge(S("wabs"), 1)
            pe.matmul(bank(3, 7), ones[:, :], wsum[:, :], start=True, stop=True).then_inc(S("wsum_ps"), 1)
            pe.matmul(bank(4, E), ones[:, :], SIM2[:, :], start=True, stop=True).then_inc(S("simsum_ps"), 1)

            pe.wait_ge(S("sim_sum"), 1)
            pe.wait_ge(S("kbd"), 2)
            pe.wait_ge(S("vaug"), 1)
            pe.wait_ge(S("ld_wo"), 32)

            def scores(n):
                i, g = divmod(n, NG)
                b = i // TB
                pe.wait_ge(S("q"), b + 1)
                if n >= 2:
                    pe.wait_ge(S("clipped"), n - 1)
                for a in range(2):
                    last = pe.matmul(bank(2 * (n % 2) + a, 2 * NK), QT[:, i * R:(i + 1) * R],
                                     KBD[:, b, HG * g + 2 * a:HG * g + 2 * a + 2, :].rearrange("p h k -> p (h k)"), start=True, stop=True)
                last.then_inc(S("scores"), 1)

            def turn_probs(n):
                pe.wait_ge(S("probs"), n + 1)
                if n >= 1:
                    pe.wait_ge(S("probsT"), n)
                for j in range(HG):
                    turn(bank(4, R, j * R), P0[:, n % 2, j * KM:(j + 1) * KM])
                turn(bank(5, R), P0[:, n % 2, HG * KM:]).then_inc(S("probs_turned"), 1)

            def pv(n):
                i, g = divmod(n, NG)
                b = i // TB
                pe.wait_ge(S("probsT"), n + 1)
                if g == 0 and i >= 1:
                    pe.wait_ge(S("on"), i)
                w = D + 1
                pe.matmul(bank(6, HG * w, g * HG * w), PT0[:, n % 2, HG * R:], VT[:, b, g, :, :].rearrange("p j d -> p (j d)"),
                          start=True, stop=False, skip_group_check=True)
                for j in range(HG):
                    last = pe.matmul(bank(6, w, (g * HG + j) * w), PT0[:, n % 2, j * R:(j + 1) * R], VM[:, b, g * HG + j, :],
                                     start=False, stop=j == HG - 1, skip_group_check=True)
                last.then_inc(S("pv"), 1)

            def turn_heads(i):
                pe.wait_ge(S("on"), i + 1)
                if i >= 1:
                    pe.wait_ge(S("x1"), i)
                turn(bank(7, R), ON[:, :, :].rearrange("p h d -> p (h d)")).then_inc(S("oT_ps"), 1)

            def project(i):
                pe.wait_ge(S("oT"), i + 1)
                pe.matmul(bank(7, C, R), OT[:, :], Wo_s[:, :], start=True, stop=True).then_inc(S("attn"), 1)

            for n in range(NT * NG + 8):
                if n < NT * NG:
                    scores(n)
                if 3 <= n < NT * NG + 3:
                    turn_probs(n - 3)
                if 4 <= n < NT * NG + 4:
                    pv(n - 4)
                if n >= 9 and (n - 9) % NG == 0 and (n - 9) // NG < NT:
                    turn_heads((n - 9) // NG)
                if n >= 11 and (n - 11) % NG == 0:
                    project((n - 11) // NG)

            pe.wait_ge(S("wg_f"), 1)
            for m in range(3):
                for k in range(HC):
                    last = turn(bank(m, R, k * R), WGf[:, m, k, :])
            last.then_inc(S("wgT_ps"), 1)
            pe.wait_ge(S("wter"), 7)
            def bview(k, n, off, rows=R):
                return bank(k).bitcast(BF16)[0:rows, off:off + n]
            for j in range(5):
                o = WL[j].shape[1]
                turn(bview(5, R, j * R, o), WQb[j][:, 0:o], R, identb)
            for k in range(FC * 2):
                turn(bview(6, R, k * R), WQb[5][:, k * R:(k + 1) * R], R, identb)
            for k in range(FC):
                last = turn(bview(7, R, k * R), WQb[6][:, k * R:(k + 1) * R], R, identb)
            last.then_inc(S("wterT_ps"), 1)

            def column_turn(k):
                pe.wait_ge(S("amax"), k + 1)
                pe.transpose(bank(6, R, 0, 1), amax[:, k:k + 1], ident[:, :]).then_inc(S("mxT"), 1)

            def spread(k):
                pe.wait_ge(S("mxr"), k + 1)
                pe.matmul(bank(6, 1), ones[0:1, :], grow[0:1, k:k + 1], start=True, stop=True).then_inc(S("mxb"), 1)

            def spread_max(k):
                column_turn(k)
                spread(k)

            def context_step(t):
                if t in (0, 3, 6):
                    column_turn(t // 3)
                if t in (1, 4, 7):
                    spread(t // 3)
                if t == 2:
                    pe.wait_ge(S("qx0"), 1)
                    pe.matmul(bank(7, NC), WQT[0][:, :], QC[:, :], start=True, stop=True).then_inc(S("bn0"), 1)
                if t == 5:
                    pe.wait_ge(S("qx1"), 1)
                    pe.matmul(bank(7, NC), WQT[1][:, :], QV[:, :], start=True, stop=True).then_inc(S("bn1"), 1)
                if t == 8:
                    pe.wait_ge(S("qx2"), 1)
                    for l in range(2):
                        pe.matmul(bank(7 - l, NC), WQT[3 + l][:, :], QI[:, :], start=True, stop=True).then_inc(S("bn_kv"), 1)
                if t == 9:
                    pe.wait_ge(S("ka"), 2)
                    for l in range(2):
                        for b in range(B):
                            turn(bank(6, R, (2 * l + b) * R), KA[l][:, b, 0:KM])
                            last = turn(bank(7, R, (2 * l + b) * R, KT), KA[l][:, b, KM:NK])
                    last.then_inc(S("kk_ps"), 1)

            pe.wait_ge(S("wterT"), 3)
            pe.wait_ge(S("wsc"), 1)

            pe.wait_ge(S("wgT"), 3)
            for b in range(B):
                for t in range(HC + 2):
                    if t == 0:
                        if b:
                            pe.wait_ge(S("ln2_XT"), b)
                        for i in range(TB):
                            pe.wait_ge(S("ln2_xn"), b * TB + i + 1)
                            last = turn(bank(4, R, i * R), XN[:, b * TB + i, :])
                        last.then_inc(S("ln2_T"), 1)
                        pe.wait_ge(S("ln2_XT"), b + 1)
                    elif t <= HC:
                        k = t - 1
                        n = b * HC + k
                        if n >= 2:
                            pe.wait_ge(S("hid"), n - 1)
                        for m in range(2):
                            last = pe.matmul(bank(2 * (n % 2) + m), WGT[:, m, k, :], XNT[:, b * T:(b + 1) * T], start=True, stop=True)
                        last.then_inc(S("gate"), 1)
                    else:
                        if b:
                            pe.wait_ge(S("x2"), b)
                        pe.wait_ge(S("hid"), (b + 1) * HC)
                        for i in range(TB):
                            for k in range(HC):
                                last = pe.matmul(bank(5, C, i * R), HH[:, k, i * R:(i + 1) * R], WGT[:, 2, k, :], start=k == 0, stop=k == HC - 1)
                        last.then_inc(S("ffn"), 1)
                    context_step(b * (HC + 2) + t)

            pe.wait_ge(S("kk"), 2)
            ln_turn(3, [0, 1])
            spread_max(3)
            for b in range(B):
                pe.wait_ge(S("qx3"), b + 1)
                if b == 0:
                    pe.wait_ge(S("ln3_XT"), 2)
                pe.matmul(bank(b), WQT[2][:, :], QX[:, b * T:(b + 1) * T], start=True, stop=True).then_inc(S("bn_txt"), 1)
            for l in range(2):
                pe.wait_ge(S("fused"), 2 * (l + 1))
                for i in range(NT):
                    last = pe.matmul(bank(i // 2, NK, (i % 2) * NK), FT[:, i * R:(i + 1) * R], KA[l][:, i // TB, :], start=True, stop=True)
                last.then_inc(S("s1"), 1)
                for b in range(B):
                    for i in range(TB):
                        t = b * TB + i
                        pe.wait_ge(S("p1n"), l * NT + t + 1)
                        turn(bank(4 + b, R, i * R), P1[:, t, 0:KM])
                        last = turn(bank(6 + b, R, i * R, KT), P1[:, t, KM:NK])
                    last.then_inc(S("p1_turned"), 1)
                for b in range(B):
                    pe.wait_ge(S("p1_main"), 2 * l + b + 1)
                    pe.wait_ge(S("p1_tail"), 2 * l + b + 1)
                    pe.matmul(bank(b), KKm[l][:, b, :], PM1[:, b * T:(b + 1) * T], start=True, stop=False)
                    pe.matmul(bank(b), KKt[l][:, b, :], PX1[:, b * T:(b + 1) * T], start=False, stop=True).then_inc(S("upd"), 1)
            spread_max(4)
            pe.wait_ge(S("qa"), 1)
            for k in range(FC):
                last = pe.matmul(bank(5, B, k * B), WQT[5][:, 2 * k + 1, :], QA[:, :], start=True, stop=True)
            last.then_inc(S("bn_avg"), 1)
            for n in range(B * FC):
                b, k = divmod(n, FC)
                pe.wait_ge(S("qx4"), b + 1)
                if n >= 4:
                    pe.wait_ge(S("h"), n - 3)
                pe.matmul(bank(n % 4), WQT[5][:, 2 * k, :], QX[:, b * T:(b + 1) * T], start=True, stop=True).then_inc(S("h_sum"), 1)
            spread_max(5)
            pe.wait_ge(S("qh"), FC)
            for i in range(NT):
                for k in range(FC):
                    last = pe.matmul(bank(i // TB, C, (i % TB) * R), QH[:, k, i * R:(i + 1) * R], WQT[6][:, k, :], start=k == 0, stop=k == FC - 1)
                if i % TB == TB - 1:
                    last.then_inc(S("bn_f2"), 1)

            ln_turn(4, [2, 3])
            pe.wait_ge(S("simn"), 1)
            for i in range(NT):
                pe.wait_ge(S("ln4_XT"), i // TB + 1)
                last = pe.matmul(bank(7, E, i * E), XNT[:, i * R:(i + 1) * R], SIMN[:, :], start=True, stop=True)
            last.then_inc(S("logits"), 1)
            def weights_row(m):
                b, e = m // E % 2, m % E
                if m >= 2:
                    pe.wait_ge(S("xe"), m - 1)
                pe.matmul(bank(6 + m % 2), SEL[:, e, :], RWT[:, b * T:(b + 1) * T], start=True, stop=True).then_inc(S("wrow"), 1)

            def product(k, hi, lo, m, first, end):
                xh, xl = XEh[:, m % NX, :], XEl[:, m % NX, :]
                pe.matmul(bank(k), hi, xh, start=first, stop=False)
                pe.matmul(bank(k), lo, xh, start=False, stop=False)
                return pe.matmul(bank(k), hi, xl, start=False, stop=end)

            def expert(m):
                ph, e = divmod(m, E)
                if ph == 0:
                    pe.wait_ge(S("w_lo"), e + 1)
                if ph == 2 and e % 4 == 0:
                    pe.wait_ge(S("o_lo"), e // 4 + 1)
                pe.wait_ge(*low_ready(m))
                first, end = e == 0, e == E - 1
                if ph < 2:
                    for q in range(3):
                        last = product(3 * ph + q, WEh[:, e, q, :], WEl[:, e, q, :], m, first, end)
                else:
                    last = product(ph - 2, OEh[:, e, :], OEl[:, e, :], m, first, end)
                last.then_inc(S("expert"), 1)

            def turn_out(b):
                pe.wait_ge(S("oc"), b + 1)
                for i in range(TB):
                    last = turn(bank(2 - 2 * b, R, i * R), OC[:, i * R:(i + 1) * R])
                last.then_inc(S("oc_turned"), 1)

            def causal_step(b, t):
                k0 = 3 * b
                if 2 <= t < TB + 2:
                    q = t - 2
                    n = b * TB + q
                    pe.wait_ge(S("pcT"), n + 1)
                    pe.wait_ge(S("vv"), b + 1)
                    if q:
                        pe.wait_ge(S("ao"), n)
                    for k in range(q + 1):
                        last = pe.matmul(bank(k0 + 2, C), PCT[:, n % 2, k * R:(k + 1) * R], VV[:, b * TB + k, :], start=k == 0, stop=k == q)
                    last.then_inc(S("cpv"), 1)
                if 1 <= t < TB + 1:
                    q = t - 1
                    n = b * TB + q
                    pe.wait_ge(S("pc"), n + 1)
                    if q:
                        pe.wait_ge(S("pcT"), n)
                    for k in range(q + 1):
                        last = turn(bank(k0 + 1, R, k * R), PC[:, n % 2, k * R:(k + 1) * R])
                    last.then_inc(S("pc_turned"), 1)
                if t < TB:
                    n = b * TB + t
                    if t == 0:
                        pe.wait_ge(S("qkv_out"), 3 * (b + 1))
                    pe.matmul(bank(k0, (t + 1) * R), qkT[:, 0, n * R:(n + 1) * R], qkT[:, 1, b * T:b * T + (t + 1) * R],
                              start=True, stop=True).then_inc(S("cscore"), 1)
                if t == 0:
                    for i in range(TB):
                        last = turn(bank(k0 + 2, R, i * R), VC[:, i * R:(i + 1) * R])
                    last.then_inc(S("v_turned"), 1)
                if t == TB + 3:
                    pe.wait_ge(S("ao"), (b + 1) * TB)
                    for i in range(TB):
                        last = turn(bank(k0 + 1, R, i * R), AO[:, b * TB + i, :])
                    last.then_inc(S("aoT_ps"), 1)

            pe.wait_ge(S("rw_parts"), 1)
            for i in range(NT):
                last = turn(bank(6).bitcast(BF16)[0:96, i * R:(i + 1) * R], RWS[:, i, :], R, identb)
            last.then_inc(S("rwT_ps"), 1)
            pe.wait_ge(S("rwT"), 1)
            pe.wait_ge(S("sel"), 3)
            for m in range(3):
                weights_row(m)
            for m in range(4 * E):
                ph, e = divmod(m, E)
                if m + 3 < 4 * E:
                    weights_row(m + 3)
                expert(m)
                if ph in (1, 2) and 1 <= e <= TB + 4:
                    causal_step(ph - 1, e - 1)
                if ph == 3 and e == 1:
                    turn_out(0)
            turn_out(1)

        @block.vector
        def _(v):
            chain = [0]

            def link(ins):
                chain[0] += 1
                ins.then_inc(S("v_chain"), 1)
                v.wait_ge(S("v_chain"), chain[0])

            def ln_stats(stage, i):
                link(v.bn_stats(stats[:, i, :], X[:, i, :]))
                a = v.bn_aggr(mv[:, i, :], stats[:, i, :])
                if i % TB == TB - 1:
                    a.then_inc(S(f"ln{stage}_var"), 1)
                else:
                    link(a)

            def ln_norm(stage, i):
                v.wait_ge(S(f"ln{stage}_rstd"), i // TB + 1)
                v.tensor_scalar(XN[:, i, :], X[:, i, :], mv[:, i, 0:1], rstd[:, i:i + 1], ALU.subtract, ALU.mult)\
                    .then_inc(S(f"ln{stage}_xn"), 1)

            def ln_out(stage, b, k):
                v.wait_ge(S(f"ln{stage}_T"), b + 1)
                v.tensor_copy(XNT[:, b * T:(b + 1) * T], bank(k)).then_inc(S(f"ln{stage}_XT"), 1)

            link(v.memset(P0[:, :, :], 0.0))
            link(v.memset(VM[:, :, :, :], 1.0))
            link(v.memset(VT[:, :, :, :, :], 0.0))
            for j in range(HG):
                link(v.memset(VT[j * KP:(j + 1) * KP, :, :, j, D:D + 1], 1.0))
            link(v.memset(ctxTail[:, :, :, :], 0.0))
            link(v.memset(wsum[:, :], 0.0))
            link(v.memset(WQb[3][:, :], 0.0))
            link(v.memset(WQb[4][:, :], 0.0))
            for b in range(B):
                v.wait_ge(S("ld_x"), 16 * B)
                for i in range(b * TB, (b + 1) * TB):
                    ln_stats(1, i)
            v.wait_ge(S("ctxT_ps"), 1)
            cps = bank(0, NC, 0, CK).rearrange("p (b k) -> p b k", b=B)
            v.tensor_copy(ctxT[:, :, :], cps).then_inc(S("ctxT"), 1)
            for b in range(B):
                v.tensor_copy(ctxTail[:, b, :, 0:KT], cps[:, b, KM:NK].unsqueeze(1).to_broadcast([CK, HG, KT])).then_inc(S("ctxT"), 1)
            for b in range(B):
                for i in range(b * TB, (b + 1) * TB):
                    ln_norm(1, i)
            for b in range(B):
                ln_out(1, b, 1 + b)
            v.wait_ge(S("ld_attn"), 16 * 6)
            v.wait_ge(S("k_ps"), 1)
            v.wait_ge(S("consts"), 4)
            link(v.tensor_scalar(KTs[:, :, :].rearrange("p b k -> p (b k)"), bank(3, NC), cols[:, 1:2], None, ALU.add))
            for b in range(B):
                v.tensor_tensor(KBD[:, b, :, :], KTs[:, b, :].unsqueeze(1).to_broadcast([R, H, NK]),
                                headmask[:, :].unsqueeze(2).to_broadcast([R, H, NK]), ALU.mult).then_inc(S("kbd"), 1)
            v.wait_ge(S("v_ps"), 1)
            bvr = rows_b[:, 0, :].rearrange("p (h d) -> p h d", h=H)
            for b in range(B):
                v.tensor_tensor(VM[:, b, :, 0:D], bank(4, C, b * C).rearrange("p (h d) -> p h d", h=H), bvr, ALU.add)
                for j in range(HG):
                    q = slice(j * KP, (j + 1) * KP)
                    src = bank(5, C, b * C).rearrange("p (g j d) -> p g j d", g=NG, j=HG)
                    last = v.tensor_tensor(VT[q, b, :, j, 0:D], src[q, :, j, :],
                                           rows_b[:, 0, :].rearrange("p (g j d) -> p g j d", g=NG, j=HG)[q, :, j, :], ALU.add)
            last.then_inc(S("vaug"), 1)
            for b in range(B):
                v.wait_ge(S("q_ps"), b + 1)
                v.tensor_scalar(QT[:, b * T:(b + 1) * T], bank(6 + b), cols[:, 0:1], SC0, ALU.add, ALU.mult).then_inc(S("q"), 1)
            v.wait_ge(S("ld_wo"), 32)
            v.tensor_tensor(XB[:, :, :], X[:, :, :], rows_b[:, 1, :].unsqueeze(1).to_broadcast([R, NT, C]), ALU.add).then_inc(S("xb"), 1)
            v.wait_ge(S("xb"), 1)

            v.wait_ge(S("ld_wl"), 16 * 7)
            v.wait_ge(S("ld_sim"), 32)
            v.wait_ge(S("ld_bl"), 16 * 9)
            for j in range(7):
                rws = HA if j in (3, 4) else R
                v.tensor_reduce(wsum[0:rws, j:j + 1], WL[j][0:rws, :], AX.X, ALU.add, apply_absolute_value=True)
            v.tensor_tensor(SIM2[:, :], SIM[:, :], SIM[:, :], ALU.mult).then_inc(S("wabs"), 1)
            v.wait_ge(S("wsum_ps"), 1)
            for j in range(7):
                rws = HA if j in (3, 4) else R
                last = v.tensor_scalar(wsc[:, j:j + 1], bank(3, 1, j), 1.0 / (rws * WL[j].shape[1]), 1e-5, ALU.mult, ALU.max)
            last.then_inc(S("wsc"), 1)
            v.wait_ge(S("wsc"), 1)
            v.tensor_scalar(wth[:, 0, :], wsc[:, :], 0.5, None, ALU.mult)
            v.tensor_scalar(wth[:, 1, :], wsc[:, :], -0.5, None, ALU.mult).then_inc(S("wth"), 1)
            v.wait_ge(S("simsum_ps"), 1)
            v.tensor_copy(SIM2[:, :], bank(4, E)).then_inc(S("sim_sum"), 1)

            def clip(n):
                v.wait_ge(S("scores"), n + 1)
                if n >= NS:
                    v.wait_ge(S("probs"), n - NS + 1)
                src = PS[:, 2 * (n % 2):2 * (n % 2) + 2, 0:2 * NK]
                v.tensor_scalar(SCL[:, n % NS, :, :].rearrange("p (a h) k -> p a (h k)", a=2), src, CLAMP, -CLAMP, ALU.min, ALU.max)\
                    .then_inc(S("clipped"), 1)

            def row_max(n):
                v.wait_ge(S("clipped"), n + 1)
                v.tensor_reduce(mx[:, n % NS, :], SCL[:, n % NS, :, :], AX.X, ALU.max).then_inc(S("rowmax"), 1)

            def normalise(i):
                v.wait_ge(S("pv"), NG * (i + 1))
                if i:
                    v.wait_ge(S("oT_ps"), i)
                o = bank(6, H * (D + 1)).rearrange("p (h d) -> p h d", h=H)
                link(v.reciprocal(rec0[:, :].unsqueeze(2), o[:, :, D:D + 1]))
                v.tensor_tensor(ON[:, :, :], o[:, :, 0:D], rec0[:, :].unsqueeze(2).to_broadcast([R, H, D]), ALU.mult).then_inc(S("on"), 1)

            def take_heads(i):
                v.wait_ge(S("oT_ps"), i + 1)
                v.tensor_copy(OT[:, :], bank(7, R)).then_inc(S("oT"), 1)

            def add_residual(i):
                v.wait_ge(S("attn"), i + 1)
                v.tensor_tensor(X[:, i, :], bank(7, C, R), XB[:, i, :], ALU.add).then_inc(S("x1"), 1)
                v.wait_ge(S("x1"), i + 1)
                ln_stats(2, i)

            def ternary(j):
                rws = HA if j in (3, 4) else R
                w = WL[j].shape[1]
                link(v.tensor_scalar(WLt[0:rws, 0:w], WL[j][0:rws, :], wth[0:rws, 1, j:j + 1], None, ALU.is_lt))
                v.scalar_tensor_tensor(WQb[j][0:rws, :], WL[j][0:rws, :], wth[0:rws, 0, j:j + 1], WLt[0:rws, 0:w],
                                       ALU.is_gt, ALU.subtract).then_inc(S("wter"), 1)
                v.wait_ge(S("wter"), j + 1)

            for n in range(NT * NG + 8):
                if n >= 8 and (n - 8) % NG == 0 and (n - 8) // NG < NT:
                    normalise((n - 8) // NG)
                if n < NT * NG:
                    clip(n)
                if 1 <= n <= NT * NG:
                    row_max(n - 1)
                if n >= 10 and (n - 10) % NG == 0 and (n - 10) // NG < NT:
                    take_heads((n - 10) // NG)
                if n >= 11 and (n - 11) % NG == 0:
                    add_residual((n - 11) // NG)
                if n % 4 == 1 and n // 4 < 7:
                    ternary(n // 4)
                if NG * TB + 11 <= n < NG * TB + 11 + TB:
                    ln_norm(2, n - NG * TB - 11)
            for i in range(TB, NT):
                ln_norm(2, i)

            v.wait_ge(S("ld_ffn"), 48)
            v.tensor_scalar(WGf[:, :, :, :].rearrange("p a k c -> p (a k c)"), WGi[:, :, :, :].rearrange("p a k c -> p (a k c)"),
                            1.0 / 127.0, None, ALU.mult).then_inc(S("wg_f"), 1)
            v.wait_ge(S("wgT_ps"), 1)
            for m in range(3):
                v.tensor_copy(WGT[:, m, :, :].rearrange("p k c -> p (k c)"), bank(m, HC * R)).then_inc(S("wgT"), 1)
            v.wait_ge(S("wterT_ps"), 1)

            def bview(k, n, off, rows=R):
                return bank(k).bitcast(BF16)[0:rows, off:off + n]
            for j in range(5):
                if j in (3, 4):
                    for d in range(2):
                        v.tensor_copy(WQT[j][:, d * HA:(d + 1) * HA], bview(5, HA, j * R))
                else:
                    o = WL[j].shape[1]
                    last = v.tensor_copy(WQT[j][:, :], bview(5, R, j * R, o))
            last.then_inc(S("wterT"), 1)
            v.tensor_copy(WQT[5][:, :, :].rearrange("p k c -> p (k c)"), bview(6, FC * 2 * R, 0)).then_inc(S("wterT"), 1)
            v.tensor_copy(WQT[6][:, :, :].rearrange("p k c -> p (k c)"), bview(7, FC * R, 0)).then_inc(S("wterT"), 1)
            v.wait_ge(S("gate_exp"), 1)
            link(v.tensor_scalar(sigg[:, :], sigg[:, :], 1.0, None, ALU.add))
            link(v.reciprocal(sigg[:, :], sigg[:, :]))

            def largest(k):
                v.wait_ge(S("mxT"), k + 1)
                v.tensor_reduce(grow[0:1, k:k + 1], bank(6, R, 0, 1), AX.X, ALU.max).then_inc(S("mxr"), 1)

            def step_size(k):
                v.wait_ge(S("mxb"), k + 1)
                link(v.tensor_scalar(isc[:, k:k + 1], bank(6, 1), 1e-8, 1.0 / 127.0, ALU.max, ALU.mult))
                v.reciprocal(rinv[:, k:k + 1], isc[:, k:k + 1]).then_inc(S("sc"), 1)
                v.wait_ge(S("sc"), k + 1)

            def quantise(dst, src, tmp, k, done):
                link(v.tensor_scalar(tmp, src, rinv[0:src.shape[0], k:k + 1], MAGIC, ALU.mult, ALU.add))
                v.tensor_scalar(dst, tmp, MAGIC, 127.0, ALU.subtract, ALU.min).then_inc(done, 1)

            v.memset(amax[:, :], 0.0).then_inc(S("am0"), 1)
            v.wait_ge(S("am0"), 1)
            cT = ctxT[:, :, :].rearrange("p b k -> p (b k)")
            v.tensor_reduce(amax[0:CK, 0:1], cT, AX.X, ALU.max, apply_absolute_value=True).then_inc(S("amax"), 1)

            def context_step(t):
                if t in (0, 3, 6):
                    largest(t // 3)
                if t == 1:
                    step_size(0)
                    quantise(QC[:, :], cT, rounded[0:CK, 0:NC], 0, S("qx0"))
                    link(v.tensor_tensor(osc[:, 0:1], isc[:, 0:1], wsc[:, 0:1], ALU.mult))
                if t == 2:
                    v.wait_ge(S("bn0"), 1)
                    link(v.tensor_scalar(VIS[:, :], bank(7, NC), osc[:, 0:1], cols[:, 2:3], ALU.mult, ALU.add))
                    v.tensor_reduce(amax[:, 1:2], VIS[:, :], AX.X, ALU.max, apply_absolute_value=True).then_inc(S("amax"), 1)
                if t == 4:
                    step_size(1)
                    quantise(QV[:, :], VIS[:, :], rounded[:, 0:NC], 1, S("qx1"))
                    link(v.tensor_tensor(osc[:, 1:2], isc[:, 1:2], wsc[:, 1:2], ALU.mult))
                if t == 5:
                    v.wait_ge(S("bn1"), 1)
                    link(v.tensor_scalar(IMG[:, :], bank(7, NC), osc[:, 1:2], cols[:, 3:4], ALU.mult, ALU.add))
                    v.tensor_reduce(amax[:, 2:3], IMG[:, :], AX.X, ALU.max, apply_absolute_value=True).then_inc(S("amax"), 1)
                    link(v.tensor_reduce(avg[:, :], IMG[:, :].rearrange("p (b k) -> p b k", b=B), AX.X, ALU.add))
                    link(v.tensor_scalar(avg[:, :], avg[:, :], 1.0 / NK, None, ALU.mult))
                if t == 7:
                    step_size(2)
                    quantise(QI[:, :], IMG[:, :], rounded[:, 0:NC], 2, S("qx2"))
                    for l in range(2):
                        link(v.tensor_tensor(osc[:, 3 + l:4 + l], isc[:, 2:3], wsc[:, 3 + l:4 + l], ALU.mult))
                if t == 8:
                    for l in range(2):
                        v.wait_ge(S("bn_kv"), l + 1)
                        v.tensor_scalar(KA[l][:, :, :].rearrange("p b k -> p (b k)"), bank(7 - l, NC), osc[:, 3 + l:4 + l],
                                        cols[:, 5 + l:6 + l], ALU.mult, ALU.add).then_inc(S("ka"), 1)
                if t == 9:
                    v.wait_ge(S("kk_ps"), 1)
                    for l in range(2):
                        v.tensor_copy(KKm[l][:, :, :].rearrange("p b c -> p (b c)"), bank(6, B * R, 2 * l * R))
                        v.tensor_copy(KKt[l][:, :, :].rearrange("p b c -> p (b c)"), bank(7, B * R, 2 * l * R, KT)).then_inc(S("kk"), 1)

            for b in range(B):
                for t in range(HC + 2):
                    if t == 0:
                        v.wait_ge(S("ln2_T"), b + 1)
                        v.tensor_copy(XNT[:, b * T:(b + 1) * T], bank(4)).then_inc(S("ln2_XT"), 1)
                    elif t <= HC:
                        k = t - 1
                        n = b * HC + k
                        v.wait_ge(S("silu"), n + 1)
                        if b:
                            v.wait_ge(S("ffn"), b)
                        v.tensor_tensor(HH[:, k, :], SG[:, n % 2, :], bank(2 * (n % 2) + 1), ALU.mult).then_inc(S("hid"), 1)
                    else:
                        v.wait_ge(S("ffn"), b + 1)
                        xb = X[:, b * TB:(b + 1) * TB, :].rearrange("p i c -> p (i c)")
                        v.tensor_tensor(xb, xb, bank(5), ALU.add).then_inc(S("x2"), 1)
                        v.wait_ge(S("x2"), b + 1)
                        for i in range(b * TB, (b + 1) * TB):
                            ln_stats(3, i)
                    context_step(b * (HC + 2) + t)

            for i in range(NT):
                ln_norm(3, i)
            v.wait_ge(S("ln3_xn"), NT)
            v.tensor_reduce(amax[:, 3:4], XN[:, :, :].rearrange("p i c -> p (i c)"), AX.X, ALU.max, apply_absolute_value=True).then_inc(S("amax"), 1)
            for b in range(B):
                ln_out(3, b, b)
            v.tensor_tensor(XB[:, :, :], X[:, :, :], rows_b[:, 2, :].unsqueeze(1).to_broadcast([R, NT, C]), ALU.add).then_inc(S("xb"), 1)
            largest(3)
            step_size(3)
            link(v.tensor_tensor(osc[:, 2:3], isc[:, 3:4], wsc[:, 2:3], ALU.mult))
            v.wait_ge(S("ln3_XT"), 2)
            for b in range(B):
                sl = slice(b * T, (b + 1) * T)
                quantise(QX[:, sl], XNT[:, sl], RND[:, sl], 3, S("qx3"))
            for b in range(B):
                v.wait_ge(S("bn_txt"), b + 1)
                v.tensor_scalar(FT[:, b * T:(b + 1) * T], bank(b), osc[:, 2:3], cols[:, 4:5], ALU.mult, ALU.add).then_inc(S("fused"), 1)
            for l in range(2):
                v.wait_ge(S("s1"), l + 1)
                link(v.tensor_reduce(mx1[:, :], PS[:, 0:4, 0:2 * NK].rearrange("p a (i k) -> p a i k", i=2), AX.X, ALU.max))
                v.tensor_scalar(nm1[:, :], mx1[:, :], -SC1, None, ALU.mult).then_inc(S("nm1"), 1)
                for i in range(NT):
                    v.wait_ge(S("p1"), l * NT + i + 1)
                    link(v.reciprocal(rd1[:, i:i + 1], den1[:, i:i + 1]))
                    v.tensor_scalar(P1[:, i, :], P1[:, i, :], rd1[:, i:i + 1], 0.1, ALU.mult, ALU.mult).then_inc(S("p1n"), 1)
                for b in range(B):
                    v.wait_ge(S("p1_turned"), 2 * l + b + 1)
                    v.tensor_copy(PM1[:, b * T:(b + 1) * T], bank(4 + b)).then_inc(S("p1_main"), 1)
                for b in range(B):
                    v.wait_ge(S("upd"), 2 * l + b + 1)
                    ft = FT[:, b * T:(b + 1) * T]
                    v.tensor_tensor(ft, ft, bank(b), ALU.add).then_inc(S("fused"), 1)
                    v.wait_ge(S("fused"), 2 * (l + 1) + b + 1)
            v.tensor_reduce(avga[:, 0:1], FT[:, :], AX.X, ALU.max, apply_absolute_value=True)
            link(v.tensor_reduce(avga[:, 1:2], avg[:, :], AX.X, ALU.max, apply_absolute_value=True))
            v.tensor_reduce(amax[:, 4:5], avga[:, :], AX.X, ALU.max).then_inc(S("amax"), 1)
            largest(4)
            step_size(4)
            link(v.tensor_tensor(osc[:, 5:6], isc[:, 4:5], wsc[:, 5:6], ALU.mult))
            quantise(QA[:, :], avg[:, :], avgr[:, :], 4, S("qa"))
            for b in range(B):
                sl = slice(b * T, (b + 1) * T)
                quantise(QX[:, sl], FT[:, sl], RND[:, sl], 4, S("qx4"))
            v.wait_ge(S("bn_avg"), 1)
            for k in range(FC):
                last = v.tensor_scalar(f1b[:, k, :], bank(5, B, k * B), osc[:, 5:6], bfc[:, k:k + 1], ALU.mult, ALU.add)
            last.then_inc(S("f1b"), 1)
            v.wait_ge(S("h"), B * FC)
            v.tensor_reduce(amax[:, 5:6], HT[:, :, :].rearrange("p k t -> p (k t)"), AX.X, ALU.max).then_inc(S("amax"), 1)
            largest(5)
            step_size(5)
            link(v.tensor_tensor(osc[:, 6:7], isc[:, 5:6], wsc[:, 6:7], ALU.mult))
            for k in range(FC):
                v.wait_ge(S("h_rnd"), k + 1)
                v.tensor_scalar(QH[:, k, :], HT[:, k, :], MAGIC, 127.0, ALU.subtract, ALU.min).then_inc(S("qh"), 1)
            v.wait_ge(S("xb"), 2)
            for b in range(B):
                v.wait_ge(S("bn_f2"), b + 1)
                sl = slice(b * TB, (b + 1) * TB)
                link(v.scalar_tensor_tensor(X[:, sl, :].rearrange("p i c -> p (i c)"), bank(b), osc[:, 6:7],
                                            XB[:, sl, :].rearrange("p i c -> p (i c)"), ALU.mult, ALU.add))
                for i in range(b * TB, (b + 1) * TB):
                    ln_stats(4, i)

            for i in range(NT):
                ln_norm(4, i)
            for b in range(B):
                ln_out(4, b, 2 + b)
            v.wait_ge(S("logits"), 1)
            v.wait_ge(S("rn"), 2)

            def wide(col):
                return col.unsqueeze(2).to_broadcast([R, NT, E])
            lg = bank(7, NT * E).rearrange("p (i e) -> p i e", e=E)
            link(v.tensor_tensor(g1[:, :, :], lg, wide(rn[:, :]), ALU.mult))
            link(v.tensor_tensor(LG[:, :, :], g1[:, :, :], sigg[:, :].unsqueeze(1).to_broadcast([R, NT, E]), ALU.subtract))
            link(v.tensor_reduce(r1[:, :], LG[:, :, :], AX.X, ALU.max))
            link(v.tensor_scalar(r2[:, :], r1[:, :], 0.0, None, ALU.is_le))
            link(v.tensor_scalar(msk[:, :, :], LG[:, :, :], 0.0, None, ALU.is_gt))
            link(v.memset(fb[:, :, :], 0.0))
            link(v.tensor_copy(g2[:, :, :], LG[:, :, :]))
            d16 = down16[:, :].unsqueeze(1).to_broadcast([R, NT, E])
            for rnd in range(2):
                link(v.tensor_reduce(rn[:, :], g2[:, :, :], AX.X, ALU.max))
                link(v.tensor_tensor(g1[:, :, :], g2[:, :, :], wide(rn[:, :]), ALU.is_ge))
                link(v.tensor_tensor(g1[:, :, :], g1[:, :, :], d16, ALU.mult))
                link(v.tensor_reduce(rn[:, :], g1[:, :, :], AX.X, ALU.max))
                link(v.tensor_tensor(g1[:, :, :], g1[:, :, :], wide(rn[:, :]), ALU.is_ge))
                link(v.tensor_tensor(fb[:, :, :], fb[:, :, :], g1[:, :, :], ALU.add))
                link(v.scalar_tensor_tensor(g2[:, :, :].rearrange("p i e -> p (i e)"), g1[:, :, :].rearrange("p i e -> p (i e)"), NEG,
                                            g2[:, :, :].rearrange("p i e -> p (i e)"), ALU.mult, ALU.add))
            link(v.tensor_tensor(fb[:, :, :], fb[:, :, :], wide(r2[:, :]), ALU.mult))
            link(v.tensor_tensor(msk[:, :, :], msk[:, :, :], fb[:, :, :], ALU.add))
            link(v.tensor_scalar(r1[:, :], r1[:, :], 0.0, None, ALU.max))
            link(v.tensor_scalar(g2[:, :, :], LG[:, :, :], 0.0, None, ALU.max))
            v.tensor_tensor(g2[:, :, :], g2[:, :, :], wide(r1[:, :]), ALU.subtract).then_inc(S("gshift"), 1)
            v.wait_ge(S("gexp"), 1)
            link(v.tensor_tensor(g3[:, :, :], g3[:, :, :], msk[:, :, :], ALU.mult))
            link(v.tensor_reduce(r2[:, :], g3[:, :, :], AX.X, ALU.add))
            link(v.reciprocal(r1[:, :], r2[:, :]))
            v.tensor_tensor(RW[:, :, :], g3[:, :, :], wide(r1[:, :]), ALU.mult).then_inc(S("rw"), 1)

            v.wait_ge(S("rw"), 1)
            rws = [RWS[:, :, 32 * k:32 * k + E] for k in range(3)]
            link(v.memset(RWS[:, :, :], 0.0))
            link(v.tensor_copy(rws[0], RW[:, :, :]))
            link(v.tensor_tensor(g1[:, :, :], RW[:, :, :], rws[0], ALU.subtract))
            link(v.tensor_copy(rws[1], g1[:, :, :]))
            v.tensor_tensor(rws[2], g1[:, :, :], rws[1], ALU.subtract).then_inc(S("rw_parts"), 1)
            v.wait_ge(S("rwT_ps"), 1)
            v.tensor_copy(RWT[:, :], bank(6).bitcast(BF16)[0:96, :]).then_inc(S("rwT"), 1)

            def weigh(m):
                ph = m // E
                b = ph % 2
                src = XNT if ph < 2 else AOT
                v.wait_ge(S("wrow"), m + 1)
                if ph >= 2 and m % E == 0:
                    v.wait_ge(S("aoT"), b + 1)
                if m >= NX:
                    v.wait_ge(*low_ready(m - NX))
                v.tensor_tensor(XE[:, m % NX, :], src[:, b * T:(b + 1) * T], bank(6 + m % 2), ALU.mult).then_inc(S("xe"), 1)

            def low_part(m):
                if m >= 2 * E and m % 2:
                    return
                v.wait_ge(S("xhi"), m + 1)
                if m >= NX:
                    v.wait_ge(S("expert"), m - NX + 1)
                v.tensor_tensor(XEl[:, m % NX, :], XE[:, m % NX, :], XEh[:, m % NX, :].bitcast(F32), ALU.subtract).then_inc(S("xlo"), 1)

            def causal_vector(b, t):
                k0 = 3 * b
                if 3 <= t < TB + 3:
                    n = b * TB + t - 3
                    v.wait_ge(S("cpv"), n + 1)
                    link(v.reciprocal(crd[:, n:n + 1], cden[:, n:n + 1]))
                    v.tensor_scalar(AO[:, n, :], bank(k0 + 2, C), crd[:, n:n + 1], None, ALU.mult).then_inc(S("ao"), 1)
                if t < TB:
                    n = b * TB + t
                    v.wait_ge(S("cscore"), n + 1)
                    dg = bank(k0, R, t * R)
                    link(v.tensor_tensor(dg, dg, causal[:, :], ALU.add))
                    link(v.tensor_reduce(cmx[:, n:n + 1], bank(k0, (t + 1) * R), AX.X, ALU.max))
                    v.tensor_scalar(cnm[:, n:n + 1], cmx[:, n:n + 1], -SC1, None, ALU.mult).then_inc(S("cnm"), 1)
                if t == TB + 3:
                    v.wait_ge(S("aoT_ps"), b + 1)
                    v.tensor_copy(AOT[:, b * T:(b + 1) * T], bank(k0 + 1)).then_inc(S("aoT"), 1)

            def add_out(b):
                v.wait_ge(S("oc_turned"), b + 1)
                xb = X[:, b * TB:(b + 1) * TB, :].rearrange("p i c -> p (i c)")
                v.tensor_tensor(xb, xb, bank(2 - 2 * b), ALU.add).then_inc(S("out_ready"), 1)

            weigh(0)
            weigh(1)
            low_part(0)
            for m in range(4 * E):
                ph, e = divmod(m, E)
                if m + 2 < 4 * E:
                    weigh(m + 2)
                if m + 1 < 4 * E:
                    low_part(m + 1)
                if ph in (1, 2) and e == 0:
                    v.wait_ge(S("expert"), m)
                    v.tensor_copy(qkT[:, 1, (ph - 1) * T:ph * T], bank(3 * (ph - 1) + 1)).then_inc(S("qkv_out"), 1)
                if ph in (1, 2) and 1 <= e <= TB + 4:
                    causal_vector(ph - 1, e - 1)
                if ph == 3 and e == 2:
                    add_out(0)
            add_out(1)


_INS = ['x', 'ctx_768', 'L0_xattn_Wq', 'L0_xattn_bq', 'L0_xattn_Wk', 'L0_xattn_bk', 'L0_xattn_Wv', 'L0_xattn_bv',
        'L0_xattn_Wo', 'L0_xattn_bo', 'L0_ffn_w_gate', 'L0_ffn_w_up', 'L0_ffn_w_down', 'L1_xattn_W_d2v',
        'L1_xattn_b_d2v', 'L1_xattn_W_img', 'L1_xattn_b_img', 'L1_xattn_W_txt', 'L1_xattn_b_txt', 'L1_xattn_W_att0',
        'L1_xattn_b_att0', 'L1_xattn_W_att1', 'L1_xattn_b_att1', 'L1_xattn_W_f1', 'L1_xattn_b_f1', 'L1_xattn_W_f2',
        'L1_xattn_b_f2', 'L1_ffn_sim_matrix', 'L1_ffn_gates', 'L1_ffn_q_proj', 'L1_ffn_k_proj', 'L1_ffn_v_proj',
        'L1_ffn_o_proj']


def kernel(**inputs):
    import numpy as _np
    import concourse.bacc as _bacc
    from concourse import mybir as _mybir
    from concourse.bass_utils import run_bass_kernel_spmd as _run

    nc = _bacc.Bacc("TRN2", target_bir_lowering=False, num_devices=1)
    arrays, args = {}, []
    for name in _INS:
        a = _np.ascontiguousarray(inputs[name])
        arrays[f"in_{name}"] = a
        args.append(nc.dram_tensor(f"in_{name}", a.shape, _mybir.dt.from_np(a.dtype), kind="ExternalInput").ap())
    shape = tuple(inputs['x'].shape)
    args.append(nc.dram_tensor("out_0", shape, _mybir.dt.float32, kind="ExternalOutput").ap())
    build(nc, *args)
    r = _run(nc, [arrays], core_ids=[0])
    return r.results[0]["out_0"]
```

```python
from contextlib import ExitStack

import concourse.bass as bass
from concourse import mybir

F32 = mybir.dt.float32
BF16 = mybir.dt.bfloat16
F32R = mybir.dt.float32r
I32 = mybir.dt.int32
ALU = mybir.AluOpType
ACT = mybir.ActivationFunctionType
AX = mybir.AxisListType

EPS_LN = 1e-5
CLAMP = 10000.0
MAGIC = 12582912.0
NEG = -1.0e30
R = 128


def build(nc, x, ctx_kv, Wq, bq, Wk, bk, Wv, bv, Wo, bo, w_gate, w_up, w_down,
          W_d2v, b_d2v, W_img, b_img, W_txt, b_txt, W_att0, b_att0, W_att1, b_att1,
          W_f1, b_f1, W_f2, b_f2, sim_matrix, gates, q_proj, k_proj, v_proj, o_proj, out):
    B, T, C = x.shape
    NK, CK = ctx_kv.shape[1:]
    NT = B * T // R
    TB = T // R
    H = 16
    D = C // H
    HG = 4
    NG = H // HG
    NX = 3
    NS = 4
    KM = R
    KT = NK - KM
    KP = 32
    KW = KM + KP
    VW = HG * (D + 1)
    VR = 3
    HC = w_gate.shape[0] // R
    FC = W_f1.shape[0] // R
    E = sim_matrix.shape[1]
    HA = W_att0.shape[0]
    NC = B * NK
    SC0 = float(D) ** -0.5
    SC1 = float(C) ** -0.5

    with ExitStack() as stack:
        def sb(name, shape, dt=F32):
            return stack.enter_context(nc.sbuf_tensor(name, shape, dt))

        early = ExitStack()

        def eb(name, shape, dt=F32):
            return early.enter_context(nc.sbuf_tensor(name, shape, dt))

        attn_only = ExitStack()

        def ab(name, shape, dt=F32):
            return attn_only.enter_context(nc.sbuf_tensor(name, shape, dt))

        sems = {}

        def S(name):
            if name not in sems:
                sems[name] = stack.enter_context(nc.semaphore(name))
            return sems[name]

        def low_ready(m):
            if m < 2 * E:
                return S("xlo"), m + 1
            if m % 2:
                return S("xlo_gpsimd"), (m - 2 * E + 1) // 2
            return S("xlo"), 2 * E + (m - 2 * E) // 2 + 1

        PS = stack.enter_context(nc.psum_tensor("PS", [R, 8, 512], F32))

        def bank(k, n=512, off=0, rows=R):
            return PS[0:rows, k, off:off + n]

        max_bank = [7, 6, 6, 2, 6, 6]

        causal_at = [(1, 2, 3, 4, 5, 6, 7, 8, 9), (1, 2, 3, 5, 6, 8, 9, 10, 11)]

        def score_bank(b, q):
            return (0, 3 - 2 * (q % 2))[b]

        def value_bank(b, q):
            return (2, 5 - 3 * (q % 2))[b]

        stack_bank = [6, 7, 4, 5]

        ident = sb("ident", [R, R])
        identb = sb("identb", [R, R], BF16)
        ones = sb("ones", [R, R])
        headmask = sb("headmask", [R, HG])
        causal = sb("causal", [R, R])
        down16 = sb("down16", [R, E])
        half = sb("half", [R, NT])
        X = sb("X", [R, NT, C])
        XN = sb("XN", [R, NT, C])
        XNT = sb("XNT", [R, NT * R])
        XB = sb("XB", [R, NT, C])
        stats = sb("stats", [R, NT, 6])
        mv = sb("mv", [R, NT, 2])
        vare = sb("vare", [R, NT])
        rstd = sb("rstd", [R, NT])
        SEL = sb("SEL", [96, E, R], BF16)
        WE = sb("WE", [R, E, 3, C])
        OE = sb("OE", [R, E, C])
        SIM = sb("SIM", [R, E])
        SIM2 = sb("SIM2", [R, E])
        simr = sb("simr", [R, E])
        SIMN = sb("SIMN", [R, E])
        sigg = sb("sigg", [R, E])
        sq = sb("sq", [R, C])
        ssq = sb("ssq", [R, NT])
        rn = sb("rn", [R, NT])
        LG = sb("LG", [R, NT, E])
        g1 = sb("g1", [R, NT, E])
        g2 = sb("g2", [R, NT, E])
        g3 = sb("g3", [R, NT, E])
        msk = sb("msk", [R, NT, E])
        fb = sb("fb", [R, NT, E])
        r1 = sb("r1", [R, NT])
        r2 = sb("r2", [R, NT])
        r3 = sb("r3", [R, NT])
        gs = sb("gs", [R, NT, E])
        RWS = sb("RWS", [R, NT, 96], BF16)
        RW = sb("RW", [R, NT, E])
        CM = eb("CM", [R, B, CK])
        CT = eb("CT", [KT, B, CK])
        ctxT = eb("ctxT", [CK, B, NK])
        ctxTail = eb("ctxTail", [CK, B, HG, KP])
        Wq_s = eb("Wq_s", [R, C])
        Wk_s = eb("Wk_s", [CK, C])
        Wv_s = eb("Wv_s", [CK, C])
        Wo_s = eb("Wo_s", [R, C])
        cols = eb("cols", [R, 8])
        bfc = eb("bfc", [R, FC])
        rows_b = eb("rows_b", [R, 3, C])
        WGi = eb("WGi", [R, 3, HC, C], I32)
        WGf = eb("WGf", [R, 3, HC, C])
        SG = eb("SG", [R, 2, T])
        HH = eb("HH", [R, HC, T])
        WGT = eb("WGT", [R, 3, HC, R])
        WL = [eb("WL0", [R, CK]), eb("WL1", [R, C]), eb("WL2", [R, C]), eb("WL3", [R, C]), eb("WL4", [R, C]),
              eb("WL5", [R, FC * 2 * C]), eb("WL6", [R, FC * R])]
        WQb = [eb(f"WQb{j}", list(WL[j].shape), BF16) for j in range(7)]
        WLt = eb("WLt", [R, FC * 2 * C], BF16)
        WQTs = eb("WQTs", [R, 4, R], BF16)
        WQT = [eb("WQT0", [CK, R], BF16)] + [WQTs[:, j, :] for j in range(4)] + [eb("WQT5", [R, FC * 2, R], BF16), eb("WQT6", [R, FC, R], BF16)]
        wsum = eb("wsum", [R, 7])
        wsc = eb("wsc", [R, 7])
        wth = eb("wth", [R, 2, 7])
        amax = eb("amax", [R, 6])
        grow = eb("grow", [1, 6])
        isc = eb("isc", [R, 6])
        rinv = eb("rinv", [R, 6])
        osc = eb("osc", [R, 8])
        rounded = eb("rounded", [R, NC])
        QC = eb("QC", [CK, NC], BF16)
        VIS = eb("VIS", [R, NC])
        QV = eb("QV", [R, NC], BF16)
        IMG = eb("IMG", [R, NC])
        QI = eb("QI", [R, NC], BF16)
        KA = [eb(f"KA{l}", [R, B, NK]) for l in range(2)]
        KKm = [eb(f"KKm{l}", [R, B, R]) for l in range(2)]
        KKt = [eb(f"KKt{l}", [KT, B, R]) for l in range(2)]
        avg = eb("avg", [R, B])
        avga = eb("avga", [R, 1 + B])
        xmx = eb("xmx", [R, B])
        hmx = eb("hmx", [R, B * FC])
        avgr = eb("avgr", [R, B])
        QA = eb("QA", [R, B], BF16)
        f1b = eb("f1b", [R, FC, B])
        QT = WGf[:, :, :, :].rearrange("p a k c -> p (a k c)")[:, 0:NT * R]
        QTh = ab("QTh", [R, NT * R], F32R)
        QTl = ab("QTl", [R, NT * R], F32R)
        QS = ab("QS", [R, NG, NT * R], F32R)
        KTs = ab("KTs", [R, B, NK])
        KTh = ab("KTh", [R, B, NK], F32R)
        KTl = ab("KTl", [R, B, NK], F32R)
        KS = ab("KS", [R, NG, B, NK], F32R)
        KBD = ab("KBD", [R, B, NG, HG, NK], F32R)
        STACK = ab("STACK", [R, NG, 10, KP], F32R)
        VM = ab("VM", [R, B, NG, HG, VW])
        VT = ab("VT", [R, B, NG, VW])
        SCL = ab("SCL", [R, NS, HG, NK])
        mx = ab("mx", [R, NS, HG])
        P0 = ab("P0", [R, 2, HG * KW])
        PT0 = ab("PT0", [R, 2, (HG + 1) * R])
        rec0 = ab("rec0", [R, H])
        ON = ab("ON", [R, H, D])
        OT = ab("OT", [R, R])
        attn_only.close()
        FT = eb("FT", [R, NT * R])
        RND = eb("RND", [R, NT * R])
        QX = eb("QX", [R, NT * R], BF16)
        QH = eb("QH", [R, FC, NT * R], BF16)
        HT = eb("HT", [R, FC, NT * R])
        mx1 = eb("mx1", [R, NT])
        nm1 = eb("nm1", [R, NT])
        den1 = eb("den1", [R, NT])
        rd1 = eb("rd1", [R, NT])
        P1 = eb("P1", [R, NT, NK])
        PM1 = eb("PM1", [R, NT * R])
        PX1 = eb("PX1", [KT, NT * R])
        early.close()
        WEh = sb("WEh", [R, E, 3, C], F32R)
        WEl = sb("WEl", [R, E, 3, C], F32R)
        OEh = sb("OEh", [R, E, C], F32R)
        OEl = sb("OEl", [R, E, C], F32R)
        XE = sb("XE", [R, NX, T])
        XEh = sb("XEh", [R, NX, T], F32R)
        XEl = sb("XEl", [R, NX, T], F32R)
        RWT = sb("RWT", [96, NT * R], BF16)
        qkT = sb("qkT", [R, 2, NT * R])
        VC = sb("VC", [R, T])
        VV = sb("VV", [R, NT, C])
        AOT = sb("AOT", [R, NT * R])
        OC = sb("OC", [R, T])
        cmx = sb("cmx", [R, NT])
        cnm = sb("cnm", [R, NT])
        cden = sb("cden", [R, NT])
        crd = sb("crd", [R, NT])
        PC = sb("PC", [R, 2, T])
        PCT = sb("PCT", [R, 2, T])
        AO = XB

        block = stack.enter_context(nc.Block())
        we_src = [q_proj, k_proj, v_proj]

        @block.sync
        def _(sp):
            for b in range(B):
                sp.dma_start(X[:, b * TB:(b + 1) * TB, :], x[b].rearrange("(i p) c -> p i c", p=R)).then_inc(S("ld_x"), 16)
            sp.dma_start(CM[:, :, :], ctx_kv[:, 0:KM, :].rearrange("b p c -> p b c")).then_inc(S("ld_ctx"), 16)
            sp.dma_start(CT[:, :, :], ctx_kv[:, KM:NK, :].rearrange("b p c -> p b c")).then_inc(S("ld_ctx"), 16)
            sp.dma_start(Wq_s[:, :], Wq).then_inc(S("ld_attn"), 16)
            sp.dma_start(Wk_s[:, :], Wk).then_inc(S("ld_attn"), 16)
            sp.dma_start(Wv_s[:, :], Wv).then_inc(S("ld_attn"), 16)
            for k, v in enumerate((bq, bk)):
                sp.dma_start(cols[:, k:k + 1], v.rearrange("(p o) -> p o", o=1)).then_inc(S("ld_attn"), 16)
            sp.dma_start(rows_b[:, 0, :], bv.rearrange("(o c) -> o c", o=1).to_broadcast([R, C])).then_inc(S("ld_attn"), 16)
            sp.dma_start(Wo_s[:, :], Wo).then_inc(S("ld_wo"), 16)
            sp.dma_start(rows_b[:, 1, :], bo.rearrange("(o c) -> o c", o=1).to_broadcast([R, C])).then_inc(S("ld_wo"), 16)
            for k, v in enumerate((b_d2v, b_img, b_txt)):
                sp.dma_start(cols[:, 2 + k:3 + k], v.rearrange("(p o) -> p o", o=1)).then_inc(S("ld_bl"), 16)
            for k, v in enumerate((b_att0, b_att1)):
                for d in range(2):
                    sp.dma_start(cols[d * HA:(d + 1) * HA, 5 + k:6 + k], v.rearrange("(p o) -> p o", o=1)).then_inc(S("ld_bl"), 16)
            with nc.allow_non_contiguous_dma(reason="a bias of 512 values, one per partition and chunk"):
                sp.dma_start(bfc[:, :], b_f1.rearrange("(k p) -> p k", p=R)).then_inc(S("ld_bl"), 16)
            sp.dma_start(rows_b[:, 2, :], b_f2.rearrange("(o c) -> o c", o=1).to_broadcast([R, C])).then_inc(S("ld_bl"), 16)
            sp.dma_start(SIM[:, :], sim_matrix).then_inc(S("ld_sim"), 16)
            sp.dma_start(sigg[:, :], gates.rearrange("(o c) -> o c", o=1).to_broadcast([R, E])).then_inc(S("ld_sim"), 16)
            sp.dma_start(WGi[:, 0, :, :], w_gate.rearrange("(k p) c -> p k c", p=R)).then_inc(S("ld_ffn"), 16)
            sp.dma_start(WGi[:, 1, :, :], w_up.rearrange("(k p) c -> p k c", p=R)).then_inc(S("ld_ffn"), 16)
            sp.dma_start(WGi[:, 2, :, :], w_down.rearrange("p (k c) -> p k c", c=R)).then_inc(S("ld_ffn"), 16)
            for s in range(0, E, 4):
                for n in range(3):
                    sp.dma_start(WE[:, s:s + 4, n, :], we_src[n][s:s + 4].rearrange("e c h -> c e h")).then_inc(S("ld_we"), 16)
            for s in range(0, E, 4):
                sp.dma_start(OE[:, s:s + 4, :], o_proj[s:s + 4].rearrange("e c h -> c e h")).then_inc(S("ld_oe"), 16)
            for b in range(B):
                sp.wait_ge(S("out_ready"), b + 1)
                sp.dma_start(out[b].rearrange("(i p) c -> p i c", p=R), X[:, b * TB:(b + 1) * TB, :]).then_inc(S("st_out"), 16)
            sp.wait_ge(S("st_out"), 16 * B)

        @block.gpsimd
        def _(pool):
            chain = [0]

            def link(ins):
                chain[0] += 1
                ins.then_inc(S("p_chain"), 1)
                pool.wait_ge(S("p_chain"), chain[0])

            pool.memset(ident[:, :], 0.0).then_inc(S("p_chain"), 1)
            pool.memset(ones[:, :], 1.0).then_inc(S("p_chain"), 1)
            pool.memset(headmask[:, :], 1.0).then_inc(S("p_chain"), 1)
            pool.memset(causal[:, :], 0.0).then_inc(S("p_chain"), 1)
            chain[0] += 4
            link(pool.memset(half[:, :], -0.5))
            link(pool.affine_select(out=ident[:, :], in_=ident[:, :], compare_op=ALU.not_equal, fill=1.0, base=0,
                                    pattern=[[-1, R]], channel_multiplier=1))
            pool.tensor_copy(identb[:, :], ident[:, :]).then_inc(S("consts"), 1)
            for c in range(4):
                hm = headmask[c * KP:(c + 1) * KP, :]
                link(pool.affine_select(out=hm, in_=hm, compare_op=ALU.is_ge, fill=0.0, base=0,
                                        pattern=[[-D, HG]], channel_multiplier=1))
                link(pool.affine_select(out=hm, in_=hm, compare_op=ALU.is_ge, fill=0.0, base=D - 1,
                                        pattern=[[D, HG]], channel_multiplier=-1))
            pool.affine_select(out=causal[:, :], in_=causal[:, :], compare_op=ALU.is_ge, fill=NEG, base=0,
                               pattern=[[-1, R]], channel_multiplier=1).then_inc(S("consts"), 1)
            pool.iota(down16[:, :], pattern=[[-1, E]], base=E, channel_multiplier=0,
                      allow_small_or_imprecise_dtypes=True).then_inc(S("consts"), 1)

            def rsqrt(dst, src, tmp, eps, ready, done, k, n):
                pool.wait_ge(ready, k)
                link(pool.tensor_scalar(tmp, src, 1.0, eps, ALU.mult, ALU.add))
                pool.tensor_tensor(dst, tmp, half[0:n, 0:1].to_broadcast(list(dst.shape)) if dst.shape[1] > NT else
                                   half[0:n, 0:dst.shape[1]], ALU.pow).then_inc(done, 1)

            def ln_batch(stage, b):
                sl = slice(b * TB, (b + 1) * TB)
                rsqrt(rstd[:, sl], mv[:, sl, 1], vare[:, sl], EPS_LN, S(f"ln{stage}_var"), S(f"ln{stage}_rstd"), b + 1, R)

            def ln_rstd(stage):
                for b in range(B):
                    ln_batch(stage, b)

            pool.wait_ge(S("consts"), 3)
            ln_rstd(1)

            def spread_keys(b, g):
                pool.tensor_tensor(KBD[:, b, g, :, :], KS[:, g, b, :].unsqueeze(1).to_broadcast([R, HG, NK]).bitcast(F32),
                                   headmask[:, :].unsqueeze(2).to_broadcast([R, HG, NK]), ALU.mult).then_inc(S("kbd_gpsimd"), 1)

            link(pool.memset(RWS[:, :, :], 0.0))
            link(pool.memset(SEL[:, :, :], 0.0))
            for k in range(3):
                part = SEL[32 * k:32 * k + 32, :, :]
                link(pool.affine_select(out=part, in_=part, compare_op=ALU.not_equal, fill=1.0, base=0,
                                        pattern=[[-1, E], [0, R]], channel_multiplier=1))
            for g in (1, 3):
                pool.wait_ge(S("k_stack"), g + 1)
                spread_keys(0, g)

            for n in range(NT * NG):
                pool.wait_ge(S("rowmax"), n + 1)
                pool.tensor_tensor(SCL[:, n % NS, :, :], SCL[:, n % NS, :, :], mx[:, n % NS, :].unsqueeze(2).to_broadcast([R, HG, NK]),
                                   ALU.subtract).then_inc(S("shifted"), 1)
                if n == 4:
                    pool.wait_ge(S("ld_wo"), 32)
                    pool.tensor_tensor(XB[:, :, :], X[:, :, :], rows_b[:, 1, :].unsqueeze(1).to_broadcast([R, NT, C]), ALU.add).then_inc(S("xb"), 1)
                if n in (6, 8, 10, 12):
                    spread_keys(1, (n - 6) // 2)
                if n == NG * TB + 8:
                    ln_batch(2, 0)
            pool.wait_ge(S("sim_sum"), 1)
            link(pool.tensor_scalar(SIM2[:, :], SIM2[:, :], 1.0, 1e-12, ALU.mult, ALU.add))
            for k in range(0, E, NT):
                link(pool.tensor_tensor(simr[:, k:k + NT], SIM2[:, k:k + NT], half[:, :], ALU.pow))
            pool.tensor_tensor(SIMN[:, :], SIM[:, :], simr[:, :], ALU.mult).then_inc(S("simn"), 1)
            ln_batch(2, 1)
            ln_rstd(3)
            pool.wait_ge(S("ld_bl"), 16 * 9)
            pool.wait_ge(S("x2"), B)
            pool.tensor_tensor(XB[:, :, :], X[:, :, :], rows_b[:, 2, :].unsqueeze(1).to_broadcast([R, NT, C]), ALU.add).then_inc(S("xb"), 1)

            def row_roots(b):
                sl = slice(b * TB, (b + 1) * TB)
                rsqrt(rn[:, sl], ssq[:, sl], vare[:, sl], 1e-12, S("ssq"), S("rn"), TB * (b + 1), R)

            ln_batch(4, 0)
            row_roots(0)

            def low_part(m):
                pool.wait_ge(S("xhi"), m + 1)
                if m >= NX:
                    pool.wait_ge(S("expert"), m - NX + 1)
                pool.tensor_tensor(XEl[:, m % NX, :], XE[:, m % NX, :], XEh[:, m % NX, :].bitcast(F32), ALU.subtract).then_inc(S("xlo_gpsimd"), 1)

            for e in range(E):
                if e == 2:
                    ln_batch(4, 1)
                if e == 6:
                    row_roots(1)
                pool.wait_ge(S("w_hi"), e + 1)
                pool.tensor_tensor(WEl[:, e, :, :], WE[:, e, :, :], WEh[:, e, :, :].bitcast(F32), ALU.subtract).then_inc(S("w_lo"), 1)
            for e in range(0, E, 4):
                pool.wait_ge(S("o_hi"), e // 4 + 1)
                pool.tensor_tensor(OEl[:, e:e + 4, :], OE[:, e:e + 4, :], OEh[:, e:e + 4, :].bitcast(F32), ALU.subtract).then_inc(S("o_lo"), 1)
            for m in range(2 * E + 1, 4 * E, 2):
                low_part(m)

        @block.scalar
        def _(act):
            def bview(k, n, off, rows=R):
                return bank(k).bitcast(BF16)[0:rows, off:off + n]

            act.wait_ge(S("consts"), 1)
            for k, keep in enumerate((1, 1, 0, 0, 1, 1, 0, 1, 0, 1)):
                last = act.activation(STACK[:, :, k, :], ident[:, :].rearrange("p (g q) -> p g q", g=NG), ACT.Copy, scale=float(keep))
            last.then_inc(S("stack"), 1)

            act.dma_start(WL[5][:, :].rearrange("p (k c) -> p k c", k=FC), W_f1.rearrange("(k p) c -> p k c", p=R)).then_inc(S("ld_wl"), 16)
            act.dma_start(WL[6][:, :], W_f2).then_inc(S("ld_wl"), 16)
            for j, w in enumerate((W_d2v, W_img, W_txt)):
                act.dma_start(WL[j][:, :], w).then_inc(S("ld_wl"), 16)
            for j, w in enumerate((W_att0, W_att1)):
                for d in range(2):
                    act.dma_start(WL[3 + j][d * HA:(d + 1) * HA, :], w).then_inc(S("ld_wl"), 16)

            def magnitudes(j):
                act.wait_ge(S("ld_wl"), 16 * 9)
                if j:
                    act.wait_ge(S("wabs"), j)
                act.activation(WLt[:, 0:WL[j].shape[1]], WL[j][:, :], ACT.Abs, accum_out=wsum[:, j:j + 1]).then_inc(S("wabs"), 1)

            def query_stack(b, g, k):
                act.wait_ge(S("q_stack"), NG * b + g + 1)
                act.activation(QS[:, g, b * T:(b + 1) * T], bank(k), ACT.Copy).then_inc(S("qs"), 1)

            act.wait_ge(S("keys"), 1)
            act.activation(KTh[:, :, :], KTs[:, :, :], ACT.Copy).then_inc(S("k_hi"), 1)
            for b in range(B):
                act.wait_ge(S("q"), b + 1)
                act.activation(QTh[:, b * T:(b + 1) * T], QT[:, b * T:(b + 1) * T], ACT.Copy).then_inc(S("q_hi"), 1)
                if b == 0:
                    for g in range(NG):
                        act.wait_ge(S("k_stack_ps"), g + 1)
                        act.activation(KS[:, g, :, :].rearrange("p b k -> p (b k)"), bank(g, NC), ACT.Copy).then_inc(S("k_stack"), 1)
            for b in range(B):
                for g in range(NG):
                    query_stack(b, g, stack_bank[g])

            act.wait_ge(S("ld_sim"), 32)
            act.activation(sigg[:, :], sigg[:, :], ACT.Exp, scale=-1.0).then_inc(S("gate_exp"), 1)

            for n in range(NT * NG + 2):
                if n < NT * NG:
                    act.wait_ge(S("shifted"), n + 1)
                    if n >= 2:
                        act.wait_ge(S("probs_turned"), n - 1)
                    act.activation(P0[:, n % 2, 0:HG * KM].rearrange("p (j k) -> p j k", j=HG), SCL[:, n % NS, :, 0:KM], ACT.Exp)
                    act.activation(P0[:, n % 2, HG * KM:].rearrange("p (j k) -> p j k", j=HG)[:, :, 0:KT], SCL[:, n % NS, :, KM:NK],
                                   ACT.Exp).then_inc(S("probs"), 1)
                if 1 <= n < 5:
                    for j in ((0, 1, 2), (3, 4), (5,), (6,))[n - 1]:
                        magnitudes(j)
                if n >= 1 and n - 1 < NT * NG:
                    m = n - 1
                    act.wait_ge(S("probs_turned"), m + 1)
                    if m >= 2:
                        act.wait_ge(S("pv"), m - 1)
                    act.activation(PT0[:, m % 2, :], PS[:, 4:6, :].rearrange("p a b -> p (a b)")[:, 0:(HG + 1) * R],
                                   ACT.Copy).then_inc(S("probsT"), 1)

            act.wait_ge(S("wgT_ps"), 1)
            for m in range(3):
                act.activation(WGT[:, m, :, :].rearrange("p k c -> p (k c)"), bank(m, HC * R), ACT.Copy).then_inc(S("wgT"), 1)
            act.wait_ge(S("wterT_ps"), 1)
            act.activation(WQT[0][:, :], bview(3, R, 0, CK), ACT.Copy)
            act.activation(WQTs[:, :, :].rearrange("p j c -> p (j c)"), bview(3, 4 * R, R), ACT.Copy).then_inc(S("wterT"), 1)

            def take_tokens(stage, b, k):
                act.wait_ge(S(f"ln{stage}_T"), b + 1)
                act.activation(XNT[:, b * T:(b + 1) * T], bank(k), ACT.Copy).then_inc(S(f"ln{stage}_XT"), 1)

            take_tokens(2, 0, 4)
            act.wait_ge(S("wterT_ps"), 2)
            act.activation(WQT[5][:, :, :].rearrange("p k c -> p (k c)"), bview(0, FC * 2 * R, 0), ACT.Copy).then_inc(S("wterT"), 1)
            act.activation(WQT[6][:, :, :].rearrange("p k c -> p (k c)"), bview(1, FC * R, 0), ACT.Copy).then_inc(S("wterT"), 1)

            for n in range(B * HC):
                act.wait_ge(S("gate"), n + 1)
                if n >= 2:
                    act.wait_ge(S("hid"), n - 1)
                act.activation(SG[:, n % 2, :], bank(2 * (n % 2)), ACT.Silu).then_inc(S("silu"), 1)
                if n == HC - 1:
                    take_tokens(2, 1, 4)
            take_tokens(3, 0, 4)
            take_tokens(3, 1, 5)
            act.wait_ge(S("kk_ps"), 1)
            for l in range(2):
                act.activation(KKm[l][:, :, :].rearrange("p b c -> p (b c)"), bank(6, B * R, 2 * l * R), ACT.Copy)
                act.activation(KKt[l][:, :, :].rearrange("p b c -> p (b c)"), bank(7, B * R, 2 * l * R, KT), ACT.Copy).then_inc(S("kk"), 1)

            for l in range(2):
                for b in range(B):
                    act.wait_ge(S("nm1"), 2 * l + b + 1)
                    if l:
                        act.wait_ge(S("p1_turned"), b + 1)
                    for i in range(TB):
                        t = b * TB + i
                        last = act.activation(P1[:, t, :], PS[:, 2 * b + i // 2, (i % 2) * NK:(i % 2 + 1) * NK], ACT.Exp, bias=nm1[:, t:t + 1],
                                              scale=SC1, accum_out=den1[:, t:t + 1])
                    last.then_inc(S("p1"), 1)
                for b in range(B):
                    act.wait_ge(S("p1_turned"), 2 * l + b + 1)
                    act.activation(PX1[:, b * T:(b + 1) * T], bank(6 + b, rows=KT), ACT.Copy).then_inc(S("p1_tail"), 1)

            act.wait_ge(S("f1b"), 1)
            for n in range(B * FC):
                b, k = divmod(n, FC)
                act.wait_ge(S("h_sum"), n + 1)
                act.activation(HT[:, k, b * T:(b + 1) * T], bank(n % 4), ACT.Relu, bias=f1b[:, k, b:b + 1],
                               scale=osc[:, 5:6]).then_inc(S("h"), 1)
            act.wait_ge(S("sc"), 6)
            for n in range(B * FC):
                b, k = divmod(n, FC)
                if n % 3:
                    ht = HT[:, k, b * T:(b + 1) * T]
                    act.activation(ht, ht, ACT.Copy, scale=rinv[:, 5:6], bias=MAGIC).then_inc(S("h_rnd"), 1)

            def squares(b):
                for i in range(b * TB, (b + 1) * TB):
                    act.wait_ge(S("ln4_xn"), i + 1)
                    if i:
                        act.wait_ge(S("ssq"), i)
                    act.activation(sq[:, :], XN[:, i, :], ACT.Square, accum_out=ssq[:, i:i + 1]).then_inc(S("ssq"), 1)

            def gate_exponentials(b):
                act.wait_ge(S("gshift"), b + 1)
                act.activation(g3[:, b * TB:(b + 1) * TB, :], gs[:, b * TB:(b + 1) * TB, :], ACT.Exp).then_inc(S("gexp"), 1)

            squares(0)
            gate_exponentials(0)

            def high_part(m):
                act.wait_ge(S("xe"), m + 1)
                if m >= NX:
                    act.wait_ge(S("expert"), m - NX + 1)
                act.activation(XEh[:, m % NX, :], XE[:, m % NX, :], ACT.Copy).then_inc(S("xhi"), 1)

            def weight_high(e):
                act.activation(WEh[:, e, :, :], WE[:, e, :, :], ACT.Copy).then_inc(S("w_hi"), 1)

            def causal_scalar(b, t):
                k0 = 3 * b
                if 2 <= t < TB + 2:
                    q = t - 2
                    n = b * TB + q
                    act.wait_ge(S("pc_turned"), n + 1)
                    if n >= 2:
                        act.wait_ge(S("cpv"), n - 1)
                    act.activation(PCT[:, n % 2, 0:(q + 1) * R], bank(k0 + 1, (q + 1) * R), ACT.Copy).then_inc(S("pcT"), 1)
                if 1 <= t < TB + 1:
                    q = t - 1
                    n = b * TB + q
                    act.wait_ge(S("cnm"), n + 1)
                    if n >= 2:
                        act.wait_ge(S("pc_turned"), n - 1)
                    act.activation(PC[:, n % 2, 0:(q + 1) * R], bank(score_bank(b, q), (q + 1) * R), ACT.Exp, bias=cnm[:, n:n + 1],
                                   scale=SC1, accum_out=cden[:, n:n + 1]).then_inc(S("pc"), 1)
                if t == 0:
                    act.wait_ge(S("v_turned"), b + 1)
                    act.activation(VV[:, b * TB:(b + 1) * TB, :].rearrange("p i c -> p (i c)"), bank(k0 + 2), ACT.Copy).then_inc(S("vv"), 1)

            act.wait_ge(S("ld_we"), 16 * 12)
            act.wait_ge(S("ld_oe"), 16 * 4)
            act.wait_ge(S("bn_f2"), 2)
            for e in range(2):
                weight_high(e)
            high_part(0)
            for m in range(4 * E):
                ph, e = divmod(m, E)
                if m + 1 < 4 * E:
                    high_part(m + 1)
                if m == 3:
                    squares(1)
                if m == 7:
                    gate_exponentials(1)
                if ph == 0 and e + 2 < E:
                    weight_high(e + 2)
                if ph == 1 and e % 4 == 0:
                    act.activation(OEh[:, e:e + 4, :], OE[:, e:e + 4, :], ACT.Copy).then_inc(S("o_hi"), 1)
                if ph in (1, 2) and e == 0:
                    b = ph - 1
                    act.wait_ge(S("expert"), m)
                    act.activation(qkT[:, 0, b * T:(b + 1) * T], bank(3 * b), ACT.Copy).then_inc(S("qkv_out"), 1)
                    if b:
                        act.wait_ge(S("v_turned"), b)
                    act.activation(VC[:, :], bank(3 * b + 2), ACT.Copy).then_inc(S("qkv_out"), 1)
                if ph in (1, 2) and e in causal_at[ph - 1]:
                    causal_scalar(ph - 1, causal_at[ph - 1].index(e))
                if ph == 3 and e == 0:
                    act.wait_ge(S("expert"), m)
                    act.activation(OC[:, :], bank(0), ACT.Copy).then_inc(S("oc"), 1)
            act.wait_ge(S("expert"), 4 * E)
            act.wait_ge(S("oc_turned"), 1)
            act.activation(OC[:, :], bank(1), ACT.Copy).then_inc(S("oc"), 1)

        @block.tensor
        def _(pe):
            def turn(dst, src, n=R, idn=ident):
                return pe.transpose(dst, src, idn[0:n, 0:n])

            def ln_turn_batch(stage, b, k):
                for i in range(TB):
                    t = b * TB + i
                    pe.wait_ge(S(f"ln{stage}_xn"), t + 1)
                    last = turn(bank(k, R, i * R), XN[:, t, :])
                last.then_inc(S(f"ln{stage}_T"), 1)

            def ln_turn(stage, banks):
                for b in range(B):
                    ln_turn_batch(stage, b, banks[b])

            pe.wait_ge(S("consts"), 3)
            pe.wait_ge(S("ld_ctx"), 32)
            for b in range(B):
                turn(bank(0, KM, b * NK, CK), CM[:, b, :])
                last = turn(bank(0, KT, b * NK + KM, CK), CT[:, b, :], KT)
            last.then_inc(S("ctxT_ps"), 1)
            ln_turn(1, [1, 2])
            pe.wait_ge(S("ld_attn"), 16 * 6)
            pe.wait_ge(S("ctxT"), 3)
            pe.matmul(bank(3, NC), Wk_s[:, :], ctxT[:, :, :].rearrange("p b k -> p (b k)"), start=True, stop=True).then_inc(S("k_ps"), 1)
            for b in range(B):
                pe.matmul(bank(4, C, b * C), ctxT[:, b, 0:KM], Wv_s[:, :], start=True, stop=True)
                last = pe.matmul(bank(5, C, b * C), ctxTail[:, b, :, :].rearrange("p j k -> p (j k)"), Wv_s[:, :], start=True, stop=True)
            last.then_inc(S("v_ps"), 1)
            for b in range(B):
                pe.wait_ge(S("ln1_XT"), b + 1)
                pe.matmul(bank(6 + b), Wq_s[:, :], XNT[:, b * T:(b + 1) * T], start=True, stop=True).then_inc(S("q_ps"), 1)

            def stack_rows(k, n, g, blocks, hi, lo):
                pe.matmul(bank(k, n), STACK[:, g, blocks[0]:blocks[0] + 4, :].rearrange("p c q -> p (c q)"), hi, start=True, stop=False)
                return pe.matmul(bank(k, n), STACK[:, g, blocks[1]:blocks[1] + 4, :].rearrange("p c q -> p (c q)"), lo, start=False, stop=True)

            def stack_queries(b, g, k):
                pe.wait_ge(S("q_lo"), b + 1)
                sl = slice(b * T, (b + 1) * T)
                stack_rows(k, T, g, (5, 6), QTh[:, sl], QTl[:, sl]).then_inc(S("q_stack"), 1)

            pe.wait_ge(S("stack"), 1)
            pe.wait_ge(S("k_lo"), 1)
            for g in range(NG):
                stack_rows(g, NC, g, (0, 2), KTh[:, :, :].rearrange("p b k -> p (b k)"),
                           KTl[:, :, :].rearrange("p b k -> p (b k)")).then_inc(S("k_stack_ps"), 1)
            pe.wait_ge(S("q"), B)
            for g in range(2):
                stack_queries(0, g, stack_bank[g])

            pe.wait_ge(S("ld_wo"), 32)

            def scores(n):
                i, g = divmod(n, NG)
                b = i // TB
                if i % TB == 0:
                    if b == 0:
                        pe.wait_ge(S("qs"), g + 1)
                        pe.wait_ge(S("k_stack"), NG)
                    if b == 0 and g % 2 == 0:
                        pe.wait_ge(S("kbd"), g // 2 + 1)
                    else:
                        pe.wait_ge(S("kbd_gpsimd"), (g + 1) // 2 if b == 0 else NG // 2 + g + 1)
                if n >= 2:
                    pe.wait_ge(S("clipped"), n - 1)
                for a in range(2):
                    last = pe.matmul(bank(2 * (n % 2) + a, 2 * NK), QS[:, g, i * R:(i + 1) * R],
                                     KBD[:, b, g, 2 * a:2 * a + 2, :].rearrange("p h k -> p (h k)"), start=True, stop=True)
                last.then_inc(S("scores"), 1)

            def turn_probs(n):
                pe.wait_ge(S("probs"), n + 1)
                if n >= 1:
                    pe.wait_ge(S("probsT"), n)
                for j in range(HG):
                    turn(bank(4, R, j * R), P0[:, n % 2, j * KM:(j + 1) * KM])
                turn(bank(5, R), P0[:, n % 2, HG * KM:]).then_inc(S("probs_turned"), 1)

            def repeated(cols):
                return cols.unsqueeze(1).to_broadcast([R, VR, VW])

            def pv(n):
                i, g = divmod(n, NG)
                b = i // TB
                pe.wait_ge(S("probsT"), n + 1)
                if g == 0 and i >= 1:
                    pe.wait_ge(S("on"), i)
                pe.matmul(bank(6, VR * VW, g * VR * VW), PT0[:, n % 2, HG * R:], repeated(VT[:, b, g, :]),
                          start=True, stop=False, skip_group_check=True)
                for j in range(HG):
                    last = pe.matmul(bank(6, VR * VW, g * VR * VW), PT0[:, n % 2, j * R:(j + 1) * R], repeated(VM[:, b, g, j, :]),
                                     start=False, stop=j == HG - 1, skip_group_check=True)
                last.then_inc(S("pv"), 1)

            def turn_heads(i):
                pe.wait_ge(S("on"), i + 1)
                if i >= 1:
                    pe.wait_ge(S("x1"), i)
                else:
                    pe.wait_ge(S("sim_sum"), 1)
                turn(bank(7, R), ON[:, :, :].rearrange("p h d -> p (h d)")).then_inc(S("oT_ps"), 1)

            def project(i):
                pe.wait_ge(S("oT"), i + 1)
                pe.matmul(bank(7, C, R), OT[:, :], Wo_s[:, :], start=True, stop=True).then_inc(S("attn"), 1)

            def turn_weights_a():
                pe.wait_ge(S("wg_f"), 1)
                pe.wait_ge(S("wter"), 11)
                pe.wait_ge(S("clipped"), NT * NG)
                for m in range(3):
                    for k in range(HC):
                        last = turn(bank(m, R, k * R), WGf[:, m, k, :])
                last.then_inc(S("wgT_ps"), 1)
                for j in range(5):
                    o = WL[j].shape[1]
                    last = turn(bview(3, R, j * R, o), WQb[j][:, 0:o], R, identb)
                last.then_inc(S("wterT_ps"), 1)

            def turn_weights_b():
                pe.wait_ge(S("wgT"), 3)
                for k in range(FC * 2):
                    turn(bview(0, R, k * R), WQb[5][:, k * R:(k + 1) * R], R, identb)
                for k in range(FC):
                    last = turn(bview(1, R, k * R), WQb[6][:, k * R:(k + 1) * R], R, identb)
                last.then_inc(S("wterT_ps"), 1)

            def bview(k, n, off, rows=R):
                return bank(k).bitcast(BF16)[0:rows, off:off + n]

            def column_turn(k):
                pe.wait_ge(S("amax"), k + 1)
                pe.transpose(bank(max_bank[k], R, 0, 1), amax[:, k:k + 1], ident[:, :]).then_inc(S("mxT"), 1)

            def spread(k):
                pe.wait_ge(S("mxr"), k + 1)
                pe.matmul(bank(max_bank[k], 1), ones[0:1, :], grow[0:1, k:k + 1], start=True, stop=True).then_inc(S("mxb"), 1)

            def spread_max(k):
                column_turn(k)
                spread(k)

            def context_step(t):
                if t in (3, 6):
                    column_turn(t // 3)
                if t in (4, 7):
                    spread(t // 3)
                if t == 2:
                    pe.wait_ge(S("qx0"), 1)
                    pe.wait_ge(S("x1"), NT)
                    pe.matmul(bank(7, NC), WQT[0][:, :], QC[:, :], start=True, stop=True).then_inc(S("bn0"), 1)
                if t == 5:
                    pe.wait_ge(S("qx1"), 1)
                    pe.matmul(bank(7, NC), WQT[1][:, :], QV[:, :], start=True, stop=True).then_inc(S("bn1"), 1)
                if t == 8:
                    pe.wait_ge(S("qx2"), 1)
                    for l in range(2):
                        pe.matmul(bank(7 - l, NC), WQT[3 + l][:, :], QI[:, :], start=True, stop=True).then_inc(S("bn_kv"), 1)
                if t == 9:
                    pe.wait_ge(S("ka"), 2)
                    for l in range(2):
                        for b in range(B):
                            turn(bank(6, R, (2 * l + b) * R), KA[l][:, b, 0:KM])
                            last = turn(bank(7, R, (2 * l + b) * R, KT), KA[l][:, b, KM:NK])
                    last.then_inc(S("kk_ps"), 1)

            def ffn_step(b, t):
                if t == 0:
                    if b:
                        pe.wait_ge(S("ln2_XT"), b)
                    else:
                        pe.wait_ge(S("probsT"), NT * NG)
                    for i in range(TB):
                        pe.wait_ge(S("ln2_xn"), b * TB + i + 1)
                        last = turn(bank(4, R, i * R), XN[:, b * TB + i, :])
                    last.then_inc(S("ln2_T"), 1)
                elif t <= HC:
                    k = t - 1
                    n = b * HC + k
                    if t == 1:
                        pe.wait_ge(S("ln2_XT"), b + 1)
                    if n == 0:
                        pe.wait_ge(S("wterT"), 3)
                    if n >= 2:
                        pe.wait_ge(S("hid"), n - 1)
                    for m in range(2):
                        last = pe.matmul(bank(2 * (n % 2) + m), WGT[:, m, k, :], XNT[:, b * T:(b + 1) * T], start=True, stop=True)
                    last.then_inc(S("gate"), 1)
                else:
                    if b:
                        pe.wait_ge(S("x2"), b)
                    pe.wait_ge(S("hid"), (b + 1) * HC)
                    for i in range(TB):
                        for k in range(HC):
                            last = pe.matmul(bank(5, C, i * R), HH[:, k, i * R:(i + 1) * R], WGT[:, 2, k, :], start=k == 0, stop=k == HC - 1)
                    last.then_inc(S("ffn"), 1)

            for n in range(NT * NG + 8):
                if n < NT * NG:
                    scores(n)
                if n == 1:
                    pe.wait_ge(S("vaug"), 1)
                    for g in range(2, NG):
                        stack_queries(0, g, stack_bank[g])
                    for g in range(NG):
                        pe.wait_ge(S("qs"), g + 1)
                        stack_queries(1, g, stack_bank[g])
                if 3 <= n < NT * NG + 3:
                    turn_probs(n - 3)
                if 4 <= n < NT * NG + 4:
                    pv(n - 4)
                if n == 3:
                    pe.wait_ge(S("qs"), B * NG)
                    column_turn(0)
                if n == 5:
                    spread(0)
                if n == 8:
                    pe.wait_ge(S("sc"), 1)
                    pe.wait_ge(S("wabs"), 7)
                    pe.wait_ge(S("sim2"), 1)
                    pe.matmul(bank(7, 7), ones[:, :], wsum[:, :], start=True, stop=True)
                    pe.matmul(bank(7, E, R), ones[:, :], SIM2[:, :], start=True, stop=True).then_inc(S("sums_ps"), 1)
                if n >= 9 and (n - 9) % NG == 0 and (n - 9) // NG < NT:
                    turn_heads((n - 9) // NG)
                if n >= 11 and (n - 11) % NG == 0:
                    project((n - 11) // NG)
                if n == NT * NG + 2:
                    turn_weights_a()
                if n == NT * NG + 4:
                    ffn_step(0, 0)
                if n == NT * NG + 5:
                    turn_weights_b()
                if n == NT * NG + 7:
                    ffn_step(0, 1)

            for c, step in enumerate(((0, 2), (0, 3), (1, 0), (1, 1), (0, 4), (1, 2), (1, 3), (1, 4))):
                ffn_step(*step)
                if step == (1, HC + 1):
                    ln_turn_batch(3, 0, 4)
                context_step(c + 2)

            pe.wait_ge(S("x2"), B)
            ln_turn_batch(3, 1, 5)
            spread_max(3)
            for b in range(B):
                pe.wait_ge(S("qx3"), b + 1)
                if b == 0:
                    pe.wait_ge(S("ln3_XT"), 2)
                pe.matmul(bank(4 + b), WQT[2][:, :], QX[:, b * T:(b + 1) * T], start=True, stop=True).then_inc(S("bn_txt"), 1)
            for l in range(2):
                for b in range(B):
                    pe.wait_ge(S("fused"), 2 * l + b + 1)
                    for i in range(TB):
                        last = pe.matmul(bank(2 * b + i // 2, NK, (i % 2) * NK), FT[:, (b * TB + i) * R:(b * TB + i + 1) * R], KA[l][:, b, :],
                                         start=True, stop=True)
                    last.then_inc(S("s1"), 1)
                pe.wait_ge(S("kk"), 2)
                for b in range(B):
                    pe.wait_ge(S("p1n"), 2 * l + b + 1)
                    for i in range(TB):
                        t = b * TB + i
                        turn(bank(4 + b, R, i * R), P1[:, t, 0:KM])
                        last = turn(bank(6 + b, R, i * R, KT), P1[:, t, KM:NK])
                    last.then_inc(S("p1_turned"), 1)
                for b in range(B):
                    pe.wait_ge(S("p1_main"), 2 * l + b + 1)
                    pe.wait_ge(S("p1_tail"), 2 * l + b + 1)
                    pe.matmul(bank(2 * b), KKm[l][:, b, :], PM1[:, b * T:(b + 1) * T], start=True, stop=False)
                    pe.matmul(bank(2 * b), KKt[l][:, b, :], PX1[:, b * T:(b + 1) * T], start=False, stop=True).then_inc(S("upd"), 1)
            spread_max(4)
            pe.wait_ge(S("qa"), 1)
            for k in range(FC):
                last = pe.matmul(bank(5, B, k * B), WQT[5][:, 2 * k + 1, :], QA[:, :], start=True, stop=True)
            last.then_inc(S("bn_avg"), 1)
            for n in range(B * FC):
                b, k = divmod(n, FC)
                pe.wait_ge(S("qx4"), b + 1)
                if n >= 4:
                    pe.wait_ge(S("h"), n - 3)
                pe.matmul(bank(n % 4), WQT[5][:, 2 * k, :], QX[:, b * T:(b + 1) * T], start=True, stop=True).then_inc(S("h_sum"), 1)
            spread_max(5)
            for i in range(NT):
                if i % TB == 0:
                    pe.wait_ge(S("qh"), FC * (i // TB + 1))
                for k in range(FC):
                    last = pe.matmul(bank(4 * (i // TB), C, (i % TB) * R), QH[:, k, i * R:(i + 1) * R], WQT[6][:, k, :], start=k == 0, stop=k == FC - 1)
                if i % TB == TB - 1:
                    last.then_inc(S("bn_f2"), 1)

            def gate_logits(b):
                pe.wait_ge(S("simn"), 1)
                pe.wait_ge(S("ln4_XT"), b + 1)
                for i in range(TB):
                    t = b * TB + i
                    last = pe.matmul(bank(7 - 3 * b, E, i * E), XNT[:, t * R:(t + 1) * R], SIMN[:, :], start=True, stop=True)
                last.then_inc(S("logits"), 1)

            def turn_gates(b):
                pe.wait_ge(S("rw_parts"), b + 1)
                for i in range(TB):
                    last = turn(bank(6 - b).bitcast(BF16)[0:96, i * R:(i + 1) * R], RWS[:, b * TB + i, :], R, identb)
                last.then_inc(S("rwT_ps"), 1)

            ln_turn_batch(4, 0, 2)
            gate_logits(0)
            def weights_row(m):
                b, e = m // E % 2, m % E
                if m >= 2:
                    pe.wait_ge(S("xe"), m - 1)
                pe.matmul(bank(6 + m % 2), SEL[:, e, :], RWT[:, b * T:(b + 1) * T], start=True, stop=True).then_inc(S("wrow"), 1)

            def product(k, hi, lo, m, first, end):
                xh, xl = XEh[:, m % NX, :], XEl[:, m % NX, :]
                pe.matmul(bank(k), hi, xh, start=first, stop=False)
                pe.matmul(bank(k), lo, xh, start=False, stop=False)
                return pe.matmul(bank(k), hi, xl, start=False, stop=end)

            def expert(m):
                ph, e = divmod(m, E)
                if ph == 0:
                    pe.wait_ge(S("w_lo"), e + 1)
                if ph == 2 and e % 4 == 0:
                    pe.wait_ge(S("o_lo"), e // 4 + 1)
                pe.wait_ge(*low_ready(m))
                first, end = e == 0, e == E - 1
                if ph < 2:
                    for q in range(3):
                        last = product(3 * ph + q, WEh[:, e, q, :], WEl[:, e, q, :], m, first, end)
                else:
                    last = product(ph - 2, OEh[:, e, :], OEl[:, e, :], m, first, end)
                last.then_inc(S("expert"), 1)

            def turn_out(b):
                pe.wait_ge(S("oc"), b + 1)
                for i in range(TB):
                    last = turn(bank(2 - 2 * b, R, i * R), OC[:, i * R:(i + 1) * R])
                last.then_inc(S("oc_turned"), 1)

            def causal_step(b, t):
                k0 = 3 * b
                if 2 <= t < TB + 2:
                    q = t - 2
                    n = b * TB + q
                    pe.wait_ge(S("pc"), n + 1)
                    if q:
                        pe.wait_ge(S("pcT"), n)
                    for k in range(q + 1):
                        last = turn(bank(k0 + 1, R, k * R), PC[:, n % 2, k * R:(k + 1) * R])
                    last.then_inc(S("pc_turned"), 1)
                if t < TB:
                    n = b * TB + t
                    if t == 0:
                        pe.wait_ge(S("qkv_out"), 3 * (b + 1))
                    if t > b:
                        pe.wait_ge(S("pc"), n - b)
                    pe.matmul(bank(score_bank(b, t), (t + 1) * R), qkT[:, 0, n * R:(n + 1) * R], qkT[:, 1, b * T:b * T + (t + 1) * R],
                              start=True, stop=True).then_inc(S("cscore"), 1)
                if 3 <= t < TB + 3:
                    q = t - 3
                    n = b * TB + q
                    pe.wait_ge(S("pcT"), n + 1)
                    pe.wait_ge(S("vv"), b + 1)
                    if q > b:
                        pe.wait_ge(S("ao"), n - b)
                    for k in range(q + 1):
                        last = pe.matmul(bank(value_bank(b, q), C), PCT[:, n % 2, k * R:(k + 1) * R], VV[:, b * TB + k, :], start=k == 0, stop=k == q)
                    last.then_inc(S("cpv"), 1)
                if t == 0:
                    for i in range(TB):
                        last = turn(bank(k0 + 2, R, i * R), VC[:, i * R:(i + 1) * R])
                    last.then_inc(S("v_turned"), 1)
                if t == TB + 4:
                    pe.wait_ge(S("ao"), (b + 1) * TB)
                    for i in range(TB):
                        last = turn(bank(k0 + 1, R, i * R), AO[:, b * TB + i, :])
                    last.then_inc(S("aoT_ps"), 1)

            turn_gates(0)
            pe.wait_ge(S("rwT"), 1)
            for m in range(3):
                weights_row(m)
            for m in range(4 * E):
                ph, e = divmod(m, E)
                if m == 3:
                    ln_turn_batch(4, 1, 3)
                if m == 5:
                    gate_logits(1)
                if m == 12:
                    turn_gates(1)
                if m == E - 3:
                    pe.wait_ge(S("rwT"), 2)
                if ph == 2 and e in causal_at[1]:
                    causal_step(1, causal_at[1].index(e))
                if m + 3 < 4 * E:
                    weights_row(m + 3)
                expert(m)
                if ph == 1 and e in causal_at[0]:
                    causal_step(0, causal_at[0].index(e))
                if ph == 3 and e == 1:
                    turn_out(0)
            turn_out(1)

        @block.vector
        def _(v):
            chain = [0]

            def link(ins):
                chain[0] += 1
                ins.then_inc(S("v_chain"), 1)
                v.wait_ge(S("v_chain"), chain[0])

            def ln_stats(stage, i):
                link(v.bn_stats(stats[:, i, :], X[:, i, :]))
                a = v.bn_aggr(mv[:, i, :], stats[:, i, :])
                if i % TB == TB - 1:
                    a.then_inc(S(f"ln{stage}_var"), 1)
                else:
                    link(a)

            def ln_stats_batch(stage, b):
                tiles = range(b * TB, (b + 1) * TB)
                for i in tiles:
                    last = v.bn_stats(stats[:, i, :], X[:, i, :])
                link(last)
                for i in tiles:
                    last = v.bn_aggr(mv[:, i, :], stats[:, i, :])
                last.then_inc(S(f"ln{stage}_var"), 1)

            def ln_norm(stage, i):
                v.wait_ge(S(f"ln{stage}_rstd"), i // TB + 1)
                v.tensor_scalar(XN[:, i, :], X[:, i, :], mv[:, i, 0:1], rstd[:, i:i + 1], ALU.subtract, ALU.mult)\
                    .then_inc(S(f"ln{stage}_xn"), 1)

            def ln_out(stage, b, k):
                v.wait_ge(S(f"ln{stage}_T"), b + 1)
                v.tensor_copy(XNT[:, b * T:(b + 1) * T], bank(k)).then_inc(S(f"ln{stage}_XT"), 1)

            link(v.memset(P0[:, :, :], 0.0))
            link(v.memset(VM[:, :, :, :, :], 0.0))
            for j in range(HG):
                link(v.memset(VM[:, :, :, j, j * (D + 1) + D:(j + 1) * (D + 1)], 1.0))
            link(v.memset(VT[:, :, :, :], 0.0))
            for j in range(HG):
                link(v.memset(VT[j * KP:(j + 1) * KP, :, :, j * (D + 1) + D:(j + 1) * (D + 1)], 1.0))
            link(v.memset(ctxTail[:, :, :, :], 0.0))
            for b in range(B):
                v.wait_ge(S("ld_x"), 16 * B)
                ln_stats_batch(1, b)
            v.wait_ge(S("ctxT_ps"), 1)
            cps = bank(0, NC, 0, CK).rearrange("p (b k) -> p b k", b=B)
            v.tensor_copy(ctxT[:, :, :], cps).then_inc(S("ctxT"), 1)
            for b in range(B):
                v.tensor_copy(ctxTail[:, b, :, 0:KT], cps[:, b, KM:NK].unsqueeze(1).to_broadcast([CK, HG, KT])).then_inc(S("ctxT"), 1)
            for b in range(B):
                for i in range(b * TB, (b + 1) * TB):
                    ln_norm(1, i)
            for b in range(B):
                ln_out(1, b, 1 + b)
            v.wait_ge(S("ld_attn"), 16 * 6)
            v.wait_ge(S("k_ps"), 1)
            v.tensor_scalar(KTs[:, :, :].rearrange("p b k -> p (b k)"), bank(3, NC), cols[:, 1:2], None, ALU.add).then_inc(S("keys"), 1)
            def query_projection(b):
                v.wait_ge(S("q_ps"), b + 1)
                v.tensor_scalar(QT[:, b * T:(b + 1) * T], bank(6 + b), cols[:, 0:1], SC0, ALU.add, ALU.mult).then_inc(S("q"), 1)

            def query_low(b):
                sl = slice(b * T, (b + 1) * T)
                v.wait_ge(S("q_hi"), b + 1)
                v.tensor_tensor(QTl[:, sl], QT[:, sl], QTh[:, sl].bitcast(F32), ALU.subtract).then_inc(S("q_lo"), 1)

            def spread_keys(g):
                v.wait_ge(S("k_stack"), g + 1)
                v.tensor_tensor(KBD[:, 0, g, :, :], KS[:, g, 0, :].unsqueeze(1).to_broadcast([R, HG, NK]).bitcast(F32),
                                headmask[:, :].unsqueeze(2).to_broadcast([R, HG, NK]), ALU.mult).then_inc(S("kbd"), 1)

            query_projection(0)
            v.wait_ge(S("k_hi"), 1)
            v.tensor_tensor(KTl[:, :, :], KTs[:, :, :], KTh[:, :, :].bitcast(F32), ALU.subtract).then_inc(S("k_lo"), 1)
            query_projection(1)
            query_low(0)
            v.wait_ge(S("consts"), 3)
            spread_keys(0)
            v.wait_ge(S("v_ps"), 1)
            for b in range(B):
                for j in range(HG):
                    v.tensor_tensor(VM[:, b, :, j, j * (D + 1):j * (D + 1) + D], bank(4, C, b * C).rearrange("p (g j d) -> p g j d", g=NG, j=HG)[:, :, j, :],
                                    rows_b[:, 0, :].rearrange("p (g j d) -> p g j d", g=NG, j=HG)[:, :, j, :], ALU.add)
                    q = slice(j * KP, (j + 1) * KP)
                    src = bank(5, C, b * C).rearrange("p (g j d) -> p g j d", g=NG, j=HG)
                    last = v.tensor_tensor(VT[q, b, :, j * (D + 1):j * (D + 1) + D], src[q, :, j, :],
                                           rows_b[:, 0, :].rearrange("p (g j d) -> p g j d", g=NG, j=HG)[q, :, j, :], ALU.add)
            last.then_inc(S("vaug"), 1)
            query_low(1)
            spread_keys(2)

            def mean_magnitudes():
                v.wait_ge(S("sums_ps"), 1)
                for j in range(7):
                    last = v.tensor_scalar(wsc[:, j:j + 1], bank(7, 1, j), 1.0 / (R * WL[j].shape[1]), 1e-5, ALU.mult, ALU.max)
                link(last)
                v.tensor_scalar(wth[:, 0, :], wsc[:, :], 0.5, None, ALU.mult)
                link(v.tensor_scalar(wth[:, 1, :], wsc[:, :], -0.5, None, ALU.mult))
                v.tensor_copy(SIM2[:, :], bank(7, E, R)).then_inc(S("sim_sum"), 1)

            def clip(n):
                v.wait_ge(S("scores"), n + 1)
                if n >= NS:
                    v.wait_ge(S("probs"), n - NS + 1)
                src = PS[:, 2 * (n % 2):2 * (n % 2) + 2, 0:2 * NK]
                v.tensor_scalar(SCL[:, n % NS, :, :].rearrange("p (a h) k -> p a (h k)", a=2), src, CLAMP, -CLAMP, ALU.min, ALU.max)\
                    .then_inc(S("clipped"), 1)

            def row_max(n):
                v.wait_ge(S("clipped"), n + 1)
                v.tensor_reduce(mx[:, n % NS, :], SCL[:, n % NS, :, :], AX.X, ALU.max).then_inc(S("rowmax"), 1)

            def normalise(i):
                v.wait_ge(S("pv"), NG * (i + 1))
                if i:
                    v.wait_ge(S("oT_ps"), i)
                o = bank(6, NG * VR * VW).rearrange("p (g w) -> p g w", g=NG)[:, :, 0:HG * (D + 1)].rearrange("p g (j d) -> p g j d", j=HG)
                rec = rec0[:, :].rearrange("p (g j) -> p g j", g=NG).unsqueeze(3)
                link(v.reciprocal(rec, o[:, :, :, D:D + 1]))
                v.tensor_tensor(ON[:, :, :].rearrange("p (g j) d -> p g j d", g=NG), o[:, :, :, 0:D], rec.to_broadcast([R, NG, HG, D]),
                                ALU.mult).then_inc(S("on"), 1)

            def take_heads(i):
                v.wait_ge(S("oT_ps"), i + 1)
                v.tensor_copy(OT[:, :], bank(7, R)).then_inc(S("oT"), 1)

            def add_residual(i):
                if i == 0:
                    v.wait_ge(S("xb"), 1)
                v.wait_ge(S("attn"), i + 1)
                v.tensor_tensor(X[:, i, :], bank(7, C, R), XB[:, i, :], ALU.add).then_inc(S("x1"), 1)
                v.wait_ge(S("x1"), i + 1)
                ln_stats(2, i)

            pieces = [(j, c, min(c + 2 * R, WL[j].shape[1])) for j in range(7) for c in range(0, WL[j].shape[1], 2 * R)]

            def ternary(k):
                j, c0, c1 = pieces[k]
                link(v.tensor_scalar(WLt[:, 0:c1 - c0], WL[j][:, c0:c1], wth[:, 1, j:j + 1], None, ALU.is_lt))
                v.scalar_tensor_tensor(WQb[j][:, c0:c1], WL[j][:, c0:c1], wth[:, 0, j:j + 1], WLt[:, 0:c1 - c0],
                                       ALU.is_gt, ALU.subtract).then_inc(S("wter"), 1)
                v.wait_ge(S("wter"), k + 1)

            cT = ctxT[:, :, :].rearrange("p b k -> p (b k)")

            def context_largest():
                link(v.memset(amax[:, :], 0.0))
                v.tensor_reduce(amax[0:CK, 0:1], cT, AX.X, ALU.max, apply_absolute_value=True).then_inc(S("amax"), 1)

            def largest(k):
                v.wait_ge(S("mxT"), k + 1)
                v.tensor_reduce(grow[0:1, k:k + 1], bank(max_bank[k], R, 0, 1), AX.X, ALU.max).then_inc(S("mxr"), 1)

            def step_size(k):
                v.wait_ge(S("mxb"), k + 1)
                link(v.tensor_scalar(isc[:, k:k + 1], bank(max_bank[k], 1), 1e-8, 1.0 / 127.0, ALU.max, ALU.mult))
                v.reciprocal(rinv[:, k:k + 1], isc[:, k:k + 1]).then_inc(S("sc"), 1)
                v.wait_ge(S("sc"), k + 1)

            def quantise(dst, src, tmp, k, done):
                link(v.tensor_scalar(tmp, src, rinv[0:src.shape[0], k:k + 1], MAGIC, ALU.mult, ALU.add))
                v.tensor_scalar(dst, tmp, MAGIC, 127.0, ALU.subtract, ALU.min).then_inc(done, 1)

            def context_step(t):
                if t in (3, 6):
                    largest(t // 3)
                if t == 1:
                    step_size(0)
                    quantise(QC[:, :], cT, rounded[0:CK, 0:NC], 0, S("qx0"))
                if t == 2:
                    link(v.tensor_tensor(osc[:, 0:1], isc[:, 0:1], wsc[:, 0:1], ALU.mult))
                    v.wait_ge(S("bn0"), 1)
                    link(v.tensor_scalar(VIS[:, :], bank(7, NC), osc[:, 0:1], cols[:, 2:3], ALU.mult, ALU.add))
                    v.tensor_reduce(amax[:, 1:2], VIS[:, :], AX.X, ALU.max, apply_absolute_value=True).then_inc(S("amax"), 1)
                if t == 4:
                    step_size(1)
                    quantise(QV[:, :], VIS[:, :], rounded[:, 0:NC], 1, S("qx1"))
                    link(v.tensor_tensor(osc[:, 1:2], isc[:, 1:2], wsc[:, 1:2], ALU.mult))
                if t == 5:
                    v.wait_ge(S("bn1"), 1)
                    link(v.tensor_scalar(IMG[:, :], bank(7, NC), osc[:, 1:2], cols[:, 3:4], ALU.mult, ALU.add))
                    v.tensor_reduce(amax[:, 2:3], IMG[:, :], AX.X, ALU.max, apply_absolute_value=True).then_inc(S("amax"), 1)
                    link(v.tensor_reduce(avg[:, :], IMG[:, :].rearrange("p (b k) -> p b k", b=B), AX.X, ALU.add))
                    link(v.tensor_scalar(avg[:, :], avg[:, :], 1.0 / NK, None, ALU.mult))
                if t == 7:
                    step_size(2)
                    quantise(QI[:, :], IMG[:, :], rounded[:, 0:NC], 2, S("qx2"))
                    for l in range(2):
                        link(v.tensor_tensor(osc[:, 3 + l:4 + l], isc[:, 2:3], wsc[:, 3 + l:4 + l], ALU.mult))
                if t == 8:
                    for l in range(2):
                        v.wait_ge(S("bn_kv"), l + 1)
                        v.tensor_scalar(KA[l][:, :, :].rearrange("p b k -> p (b k)"), bank(7 - l, NC), osc[:, 3 + l:4 + l],
                                        cols[:, 5 + l:6 + l], ALU.mult, ALU.add).then_inc(S("ka"), 1)

            def ffn_weights():
                v.wait_ge(S("ld_ffn"), 48)
                v.tensor_scalar(WGf[:, :, :, :].rearrange("p a k c -> p (a k c)"), WGi[:, :, :, :].rearrange("p a k c -> p (a k c)"),
                                1.0 / 127.0, None, ALU.mult).then_inc(S("wg_f"), 1)

            def ffn_step(b, t):
                if t <= HC:
                    k = t - 1
                    n = b * HC + k
                    v.wait_ge(S("silu"), n + 1)
                    if b:
                        v.wait_ge(S("ffn"), b)
                    v.tensor_tensor(HH[:, k, :], SG[:, n % 2, :], bank(2 * (n % 2) + 1), ALU.mult).then_inc(S("hid"), 1)
                else:
                    v.wait_ge(S("ffn"), b + 1)
                    xb = X[:, b * TB:(b + 1) * TB, :].rearrange("p i c -> p (i c)")
                    v.tensor_tensor(xb, xb, bank(5), ALU.add).then_inc(S("x2"), 1)
                    v.wait_ge(S("x2"), b + 1)
                    ln_stats_batch(3, b)

            v.wait_ge(S("ld_sim"), 32)
            v.wait_ge(S("ld_bl"), 16 * 9)
            v.tensor_tensor(SIM2[:, :], SIM[:, :], SIM[:, :], ALU.mult).then_inc(S("sim2"), 1)
            for n in range(NT * NG + 8):
                if n == NT * NG:
                    row_max(n - 1)
                if n >= 8 and (n - 8) % NG == 0 and (n - 8) // NG < NT:
                    normalise((n - 8) // NG)
                if n < NT * NG:
                    clip(n)
                if 1 <= n < NT * NG:
                    row_max(n - 1)
                if n >= 10 and (n - 10) % NG == 0 and (n - 10) // NG < NT:
                    take_heads((n - 10) // NG)
                if n >= 11 and (n - 11) % NG == 0:
                    add_residual((n - 11) // NG)
                if n == 1:
                    context_largest()
                if n == 4:
                    largest(0)
                if n == 6:
                    context_step(1)
                if n == 8:
                    mean_magnitudes()
                if n == NT * NG + 1:
                    ffn_weights()
                if n == NT * NG + 7:
                    ffn_step(0, 1)
                if n >= 9 and n % 4 in (1, 2) and 2 * (n // 4 - 2) + n % 4 - 1 < len(pieces):
                    ternary(2 * (n // 4 - 2) + n % 4 - 1)
                if n == NT * NG + 2:
                    for i in range(TB):
                        ln_norm(2, i)
            for i in range(TB, NT):
                ln_norm(2, i)

            for step in (2, 3):
                ffn_step(0, step)
                context_step(step)
            context_step(4)
            context_step(5)
            ffn_step(0, 4)
            context_step(6)
            ffn_step(1, 1)
            context_step(7)
            ffn_step(1, 2)
            ffn_step(1, 3)
            context_step(8)
            for i in range(TB):
                ln_norm(3, i)
            v.wait_ge(S("ln3_xn"), TB)
            v.tensor_reduce(xmx[:, 0:1], XN[:, 0:TB, :].rearrange("p i c -> p (i c)"), AX.X, ALU.max, apply_absolute_value=True)
            ffn_step(1, 4)

            v.wait_ge(S("gate_exp"), 1)
            link(v.tensor_scalar(sigg[:, :], sigg[:, :], 1.0, None, ALU.add))
            link(v.reciprocal(sigg[:, :], sigg[:, :]))

            for i in range(TB, NT):
                ln_norm(3, i)
            v.wait_ge(S("ln3_xn"), NT)
            link(v.tensor_reduce(xmx[:, 1:2], XN[:, TB:NT, :].rearrange("p i c -> p (i c)"), AX.X, ALU.max, apply_absolute_value=True))
            v.tensor_reduce(amax[:, 3:4], xmx[:, :], AX.X, ALU.max).then_inc(S("amax"), 1)
            largest(3)
            step_size(3)
            link(v.tensor_tensor(osc[:, 2:3], isc[:, 3:4], wsc[:, 2:3], ALU.mult))
            v.wait_ge(S("ln3_XT"), 2)
            for b in range(B):
                sl = slice(b * T, (b + 1) * T)
                quantise(QX[:, sl], XNT[:, sl], RND[:, sl], 3, S("qx3"))
            for b in range(B):
                v.wait_ge(S("bn_txt"), b + 1)
                v.tensor_scalar(FT[:, b * T:(b + 1) * T], bank(4 + b), osc[:, 2:3], cols[:, 4:5], ALU.mult, ALU.add).then_inc(S("fused"), 1)
            for l in range(2):
                for b in range(B):
                    tb = slice(b * TB, (b + 1) * TB)
                    v.wait_ge(S("s1"), 2 * l + b + 1)
                    link(v.tensor_reduce(mx1[:, tb], PS[:, 2 * b:2 * b + 2, 0:2 * NK].rearrange("p a (i k) -> p a i k", i=2), AX.X, ALU.max))
                    v.tensor_scalar(nm1[:, tb], mx1[:, tb], -SC1, None, ALU.mult).then_inc(S("nm1"), 1)
                for b in range(B):
                    tb = slice(b * TB, (b + 1) * TB)
                    v.wait_ge(S("p1"), 2 * l + b + 1)
                    link(v.reciprocal(rd1[:, tb], den1[:, tb]))
                    v.tensor_tensor(P1[:, tb, :], P1[:, tb, :], rd1[:, tb].unsqueeze(2).to_broadcast([R, TB, NK]), ALU.mult)\
                        .then_inc(S("p1n"), 1)
                for b in range(B):
                    v.wait_ge(S("p1_turned"), 2 * l + b + 1)
                    v.tensor_copy(PM1[:, b * T:(b + 1) * T], bank(4 + b)).then_inc(S("p1_main"), 1)
                for b in range(B):
                    v.wait_ge(S("upd"), 2 * l + b + 1)
                    ft = FT[:, b * T:(b + 1) * T]
                    v.scalar_tensor_tensor(ft, bank(2 * b), 0.1, ft, ALU.mult, ALU.add).then_inc(S("fused"), 1)
                    if l:
                        v.wait_ge(S("fused"), 2 * (l + 1) + b + 1)
                        v.tensor_reduce(avga[:, 1 + b:2 + b], ft, AX.X, ALU.max, apply_absolute_value=True)
            link(v.tensor_reduce(avga[:, 0:1], avg[:, :], AX.X, ALU.max, apply_absolute_value=True))
            v.tensor_reduce(amax[:, 4:5], avga[:, :], AX.X, ALU.max).then_inc(S("amax"), 1)
            largest(4)
            step_size(4)
            link(v.tensor_tensor(osc[:, 5:6], isc[:, 4:5], wsc[:, 5:6], ALU.mult))
            quantise(QA[:, :], avg[:, :], avgr[:, :], 4, S("qa"))
            for b in range(B):
                sl = slice(b * T, (b + 1) * T)
                quantise(QX[:, sl], FT[:, sl], RND[:, sl], 4, S("qx4"))
            v.wait_ge(S("bn_avg"), 1)
            for k in range(FC):
                last = v.tensor_scalar(f1b[:, k, :], bank(5, B, k * B), osc[:, 5:6], bfc[:, k:k + 1], ALU.mult, ALU.add)
            last.then_inc(S("f1b"), 1)
            for n in range(B * FC):
                b, k = divmod(n, FC)
                v.wait_ge(S("h"), n + 1)
                last = v.tensor_reduce(hmx[:, n:n + 1], HT[:, k, b * T:(b + 1) * T], AX.X, ALU.max)
            link(last)
            v.tensor_reduce(amax[:, 5:6], hmx[:, :], AX.X, ALU.max).then_inc(S("amax"), 1)
            largest(5)
            step_size(5)
            link(v.tensor_tensor(osc[:, 6:7], isc[:, 5:6], wsc[:, 6:7], ALU.mult))
            def take_hidden(b):
                for k in range(FC):
                    n = b * FC + k
                    ht = HT[:, k, b * T:(b + 1) * T]
                    if n % 3 == 0:
                        link(v.tensor_scalar(ht, ht, rinv[:, 5:6], MAGIC, ALU.mult, ALU.add))
                    else:
                        v.wait_ge(S("h_rnd"), n - n // 3)
                    v.tensor_scalar(QH[:, k, b * T:(b + 1) * T], ht, MAGIC, 127.0, ALU.subtract, ALU.min).then_inc(S("qh"), 1)

            def add_hidden(b):
                v.wait_ge(S("bn_f2"), b + 1)
                sl = slice(b * TB, (b + 1) * TB)
                link(v.scalar_tensor_tensor(X[:, sl, :].rearrange("p i c -> p (i c)"), bank(4 * b), osc[:, 6:7],
                                            XB[:, sl, :].rearrange("p i c -> p (i c)"), ALU.mult, ALU.add))
                ln_stats_batch(4, b)

            take_hidden(0)
            take_hidden(1)
            v.wait_ge(S("xb"), 2)

            def gates(b, part):
                tb = slice(b * TB, (b + 1) * TB)

                def wide(col):
                    return col[:, tb].unsqueeze(2).to_broadcast([R, TB, E])

                if part == 0:
                    add_hidden(b)
                if part == 1:
                    for i in range(b * TB, (b + 1) * TB):
                        ln_norm(4, i)
                if part == 2:
                    ln_out(4, b, 2 + b)
                if part == 3:
                    v.wait_ge(S("logits"), b + 1)
                    v.wait_ge(S("rn"), b + 1)
                    lg = bank(7 - 3 * b, TB * E).rearrange("p (i e) -> p i e", e=E)
                    link(v.tensor_tensor(g1[:, tb, :], lg, wide(rn), ALU.mult))
                    link(v.tensor_tensor(LG[:, tb, :], g1[:, tb, :], sigg[:, :].unsqueeze(1).to_broadcast([R, TB, E]), ALU.subtract))
                    link(v.tensor_reduce(r1[:, tb], LG[:, tb, :], AX.X, ALU.max))
                if part == 4:
                    v.tensor_scalar(r2[:, tb], r1[:, tb], 0.0, None, ALU.is_le)
                    link(v.tensor_scalar(r3[:, tb], r1[:, tb], 0.0, None, ALU.max))
                    v.scalar_tensor_tensor(gs[:, tb, :], LG[:, tb, :], 0.0, wide(r3), ALU.max, ALU.subtract).then_inc(S("gshift"), 1)
                if part in (4, 6):
                    src, dst = (LG, fb) if part == 4 else (g2, msk)
                    if part == 6:
                        link(v.tensor_reduce(r1[:, tb], g2[:, tb, :], AX.X, ALU.max))
                    link(v.tensor_tensor(g1[:, tb, :], src[:, tb, :], wide(r1), ALU.is_ge))
                    link(v.tensor_tensor(g1[:, tb, :], g1[:, tb, :], down16[:, :].unsqueeze(1).to_broadcast([R, TB, E]), ALU.mult))
                if part in (5, 7):
                    dst = fb if part == 5 else msk
                    link(v.tensor_reduce(rn[:, tb], g1[:, tb, :], AX.X, ALU.max))
                    link(v.tensor_tensor(dst[:, tb, :], g1[:, tb, :], wide(rn), ALU.is_ge))
                if part == 5:
                    link(v.scalar_tensor_tensor(g2[:, tb, :], fb[:, tb, :], NEG, LG[:, tb, :], ALU.mult, ALU.add))
                if part == 8:
                    link(v.tensor_tensor(fb[:, tb, :], fb[:, tb, :], msk[:, tb, :], ALU.add))
                    link(v.tensor_tensor(fb[:, tb, :], fb[:, tb, :], wide(r2), ALU.mult))
                    link(v.scalar_tensor_tensor(msk[:, tb, :], LG[:, tb, :], 0.0, fb[:, tb, :], ALU.is_gt, ALU.add))
                if part == 9:
                    v.wait_ge(S("gexp"), b + 1)
                    link(v.tensor_tensor(g3[:, tb, :], g3[:, tb, :], msk[:, tb, :], ALU.mult))
                    link(v.tensor_reduce(r2[:, tb], g3[:, tb, :], AX.X, ALU.add))
                    link(v.reciprocal(r1[:, tb], r2[:, tb]))
                    link(v.tensor_tensor(RW[:, tb, :], g3[:, tb, :], wide(r1), ALU.mult))
                if part == 10:
                    rws = [RWS[:, tb, 32 * k:32 * k + E] for k in range(3)]
                    link(v.tensor_copy(rws[0], RW[:, tb, :]))
                    link(v.tensor_tensor(g1[:, tb, :], RW[:, tb, :], rws[0], ALU.subtract))
                    link(v.tensor_copy(rws[1], g1[:, tb, :]))
                    v.tensor_tensor(rws[2], g1[:, tb, :], rws[1], ALU.subtract).then_inc(S("rw_parts"), 1)
                if part == 11:
                    v.wait_ge(S("rwT_ps"), b + 1)
                    v.tensor_copy(RWT[:, b * T:(b + 1) * T], bank(6 - b).bitcast(BF16)[0:96, 0:T]).then_inc(S("rwT"), 1)

            for part in range(12):
                gates(0, part)
            beside = [(0,), (1,), (), (2,), (), (3,), (4,), (5,), (6,), (7, 8), (9,), (10,), (11,), (), (), ()]

            def weigh(m):
                ph = m // E
                b = ph % 2
                src = XNT if ph < 2 else AOT
                v.wait_ge(S("wrow"), m + 1)
                if ph >= 2 and m % E == 0:
                    v.wait_ge(S("aoT"), b + 1)
                if m >= NX:
                    v.wait_ge(*low_ready(m - NX))
                v.tensor_tensor(XE[:, m % NX, :], src[:, b * T:(b + 1) * T], bank(6 + m % 2), ALU.mult).then_inc(S("xe"), 1)

            def low_part(m):
                if m >= 2 * E and m % 2:
                    return
                v.wait_ge(S("xhi"), m + 1)
                if m >= NX:
                    v.wait_ge(S("expert"), m - NX + 1)
                v.tensor_tensor(XEl[:, m % NX, :], XE[:, m % NX, :], XEh[:, m % NX, :].bitcast(F32), ALU.subtract).then_inc(S("xlo"), 1)

            def causal_vector(b, t):
                k0 = 3 * b
                if t < TB:
                    n = b * TB + t
                    k = score_bank(b, t)
                    v.wait_ge(S("cscore"), n + 1)
                    dg = bank(k, R, t * R)
                    link(v.tensor_tensor(dg, dg, causal[:, :], ALU.add))
                    link(v.tensor_reduce(cmx[:, n:n + 1], bank(k, (t + 1) * R), AX.X, ALU.max))
                    v.tensor_scalar(cnm[:, n:n + 1], cmx[:, n:n + 1], -SC1, None, ALU.mult).then_inc(S("cnm"), 1)
                if 4 <= t < TB + 4:
                    q = t - 4
                    n = b * TB + q
                    v.wait_ge(S("cpv"), n + 1)
                    link(v.reciprocal(crd[:, n:n + 1], cden[:, n:n + 1]))
                    v.tensor_scalar(AO[:, n, :], bank(value_bank(b, q), C), crd[:, n:n + 1], None, ALU.mult).then_inc(S("ao"), 1)
                if t == TB + 4:
                    v.wait_ge(S("aoT_ps"), b + 1)
                    v.tensor_copy(AOT[:, b * T:(b + 1) * T], bank(k0 + 1)).then_inc(S("aoT"), 1)

            def add_out(b):
                v.wait_ge(S("oc_turned"), b + 1)
                xb = X[:, b * TB:(b + 1) * TB, :].rearrange("p i c -> p (i c)")
                v.tensor_tensor(xb, xb, bank(2 - 2 * b), ALU.add).then_inc(S("out_ready"), 1)

            weigh(0)
            weigh(1)
            low_part(0)
            for m in range(4 * E):
                ph, e = divmod(m, E)
                if m + 2 < 4 * E:
                    weigh(m + 2)
                if m + 1 < 4 * E:
                    low_part(m + 1)
                for part in beside[m] if m < E else ():
                    gates(1, part)
                if ph in (1, 2) and e == 0:
                    v.wait_ge(S("expert"), m)
                    v.tensor_copy(qkT[:, 1, (ph - 1) * T:ph * T], bank(3 * (ph - 1) + 1)).then_inc(S("qkv_out"), 1)
                if ph in (1, 2) and e in causal_at[ph - 1]:
                    causal_vector(ph - 1, causal_at[ph - 1].index(e))
                if ph == 3 and e == 2:
                    add_out(0)
            add_out(1)


_INS = ['x', 'ctx_768', 'L0_xattn_Wq', 'L0_xattn_bq', 'L0_xattn_Wk', 'L0_xattn_bk', 'L0_xattn_Wv', 'L0_xattn_bv',
        'L0_xattn_Wo', 'L0_xattn_bo', 'L0_ffn_w_gate', 'L0_ffn_w_up', 'L0_ffn_w_down', 'L1_xattn_W_d2v',
        'L1_xattn_b_d2v', 'L1_xattn_W_img', 'L1_xattn_b_img', 'L1_xattn_W_txt', 'L1_xattn_b_txt', 'L1_xattn_W_att0',
        'L1_xattn_b_att0', 'L1_xattn_W_att1', 'L1_xattn_b_att1', 'L1_xattn_W_f1', 'L1_xattn_b_f1', 'L1_xattn_W_f2',
        'L1_xattn_b_f2', 'L1_ffn_sim_matrix', 'L1_ffn_gates', 'L1_ffn_q_proj', 'L1_ffn_k_proj', 'L1_ffn_v_proj',
        'L1_ffn_o_proj']


def kernel(**inputs):
    import numpy as _np
    import concourse.bacc as _bacc
    from concourse import mybir as _mybir
    from concourse.bass_utils import run_bass_kernel_spmd as _run

    nc = _bacc.Bacc("TRN2", target_bir_lowering=False, num_devices=1)
    arrays, args = {}, []
    for name in _INS:
        a = _np.ascontiguousarray(inputs[name])
        arrays[f"in_{name}"] = a
        args.append(nc.dram_tensor(f"in_{name}", a.shape, _mybir.dt.from_np(a.dtype), kind="ExternalInput").ap())
    shape = tuple(inputs['x'].shape)
    args.append(nc.dram_tensor("out_0", shape, _mybir.dt.float32, kind="ExternalOutput").ap())
    build(nc, *args)
    r = _run(nc, [arrays], core_ids=[0])
    return r.results[0]["out_0"]
```
